# Optimizing a Trainium2 kernel written in Bass

```python
import numpy as np
import jax
import jax.numpy as jnp

def _softmax(x, axis=-1):
    return jax.nn.softmax(x, axis=axis)

def _gelu(x):
    return jax.nn.gelu(x, approximate=True)

def _silu(x):
    return jax.nn.silu(x)

def _sigmoid(x):
    return jax.nn.sigmoid(x)

def _layernorm(x, axis=-1, eps=1e-05):
    m = jnp.mean(x, axis=axis, keepdims=True)
    v = jnp.var(x, axis=axis, keepdims=True)
    return (x - m) / jnp.sqrt(v + eps)

def _scatter_add(tgt, idx, src, axis=0):
    return tgt.at[idx].add(src)

def _segment_sum(src, seg, n):
    return jax.ops.segment_sum(src, seg, n)
kernel_name = 'mk_xattn_seq_d4_seqx_r8_bc9e06'

def setup_inputs(seed: int=0):
    np.random.seed(seed)
    _w = jnp.asarray

    def _rec_inputs():
        import jax
        import jax.numpy as jnp
        _rk = jax.random.key(seed)
        x = 7.22e-05 + 1 * jax.random.normal(jax.random.fold_in(_rk, 1), (32, 64, 256), jnp.float32)
        _lenS = 64 - jax.random.randint(jax.random.fold_in(_rk, 7), (32,), 0, max(1, 64 // 4) + 1, jnp.int32)
        _lenS2 = 64 - jax.random.randint(jax.random.fold_in(_rk, 8), (32,), 0, max(1, 64 // 4) + 1, jnp.int32)
        _ctx_2048P = jax.random.normal(jax.random.fold_in(_rk, 11), (32, 16, 256), jnp.float32)
        _ctx_2048c = jax.random.dirichlet(jax.random.fold_in(_rk, 511), 0.3 * jnp.ones((16,), jnp.float32), (32, 64))
        _ctx_2048t = jnp.einsum('bsk,bkd->bsd', _ctx_2048c, _ctx_2048P)
        _ctx_2048t = _ctx_2048t * jax.lax.rsqrt(jnp.mean(jnp.square(_ctx_2048t)) + 1e-12) * 0.953939
        ctx_2048 = 4.13588e-05 + 0.999923 * (_ctx_2048t + 0.3 * jax.random.normal(jax.random.fold_in(_rk, 611), (32, 64, 256), jnp.float32))
        _validS = jnp.arange(64)[None, :] < _lenS[:, None]
        _validS2 = jnp.arange(64)[None, :] < _lenS2[:, None]
        _causal = jnp.tril(jnp.ones((64, 64), dtype=bool))
        mask_1x1xSxS2_fc1 = jnp.where(jnp.broadcast_to(_validS2[0:1, None, None, :], (1, 1, 64, 64)), 1.0, 0.0).astype(jnp.float32)
        mask_Bx1xSxS2_ff1 = jnp.where(jnp.ones((32, 1, 64, 64), dtype=bool), 1.0, 0.0).astype(jnp.float32)
        return (x, ctx_2048, mask_1x1xSxS2_fc1, mask_Bx1xSxS2_ff1)
    x, ctx_2048, mask_1x1xSxS2_fc1, mask_Bx1xSxS2_ff1 = _rec_inputs()

    def _L0_xattn_setup():
        import jax, jax.numpy as jnp
        import numpy as np
        B, C, N = (8, 64, 256)
        key = jax.random.key(seed)
        ks = jax.random.split(key, 7)
        s = 1.0 / np.sqrt(C)
        return {'x': jax.random.normal(ks[0], (B, C, N), dtype=jnp.float32), 'y': jax.random.normal(ks[1], (B, C, N), dtype=jnp.float32), 'w_qk': jax.random.normal(ks[2], (C, C), dtype=jnp.float32) * s, 'w_v': jax.random.normal(ks[3], (C, C), dtype=jnp.float32) * s, 'b_v': jax.random.normal(ks[4], (C,), dtype=jnp.float32) * s, 'w_t': jax.random.normal(ks[5], (C, C), dtype=jnp.float32) * s, 'b_t': jax.random.normal(ks[6], (C,), dtype=jnp.float32) * s}
    _L0_xattn_all = _L0_xattn_setup()
    _L0_xattn_in = {k: v for k, v in _L0_xattn_all.items() if k in ('w_qk', 'w_v', 'b_v', 'w_t', 'b_t')}
    del _L0_xattn_all

    def _L1_xattn_setup():
        import jax, jax.numpy as jnp
        import numpy as np
        H = 256
        NH = 16
        HD = H // NH
        EPS = 1e-05

        def gelu(x):
            return 0.5 * x * (1.0 + jnp.tanh(0.7978845608028654 * x * (1.0 + 0.044715 * x * x)))

        def layernorm(x, scale, bias):
            m = jnp.mean(x, axis=-1, keepdims=True)
            v = jnp.mean(jnp.square(x - m), axis=-1, keepdims=True)
            return (x - m) * jax.lax.rsqrt(v + EPS) * scale + bias

        def split_heads(x):
            b, s, _ = x.shape
            return x.reshape(b, s, NH, HD).transpose(0, 2, 1, 3)

        def merge_heads(x):
            b, nh, s, hd = x.shape
            return x.transpose(0, 2, 1, 3).reshape(b, s, nh * hd)

        def attention(q, k, v, mask):
            scores = jnp.einsum('bhqd,bhkd->bhqk', q, k) / jnp.sqrt(jnp.float32(HD))
            scores = scores * mask - 10000.0 * (1.0 - mask)
            probs = jax.nn.softmax(scores, axis=-1)
            return jnp.einsum('bhqk,bhkd->bhqd', probs, v)
        key = jax.random.key(seed)
        ks = jax.random.split(key, 16)
        b, s, t = (2, 128, 128)
        w = lambda k, i, o: jax.random.normal(k, (i, o), jnp.float32) * 0.02
        inp = {'hidden_states': jax.random.normal(ks[0], (b, s, H), jnp.float32), 'encoder_states': jax.random.normal(ks[1], (b, t, H), jnp.float32), 'ltor_mask': jnp.tril(jnp.ones((1, 1, s, s), jnp.float32)), 'cross_mask': jnp.ones((b, 1, s, t), jnp.float32), 'ln1_s': jnp.ones((H,), jnp.float32), 'ln1_b': jnp.zeros((H,), jnp.float32), 'w_qkv': w(ks[2], H, 3 * H), 'b_qkv': jnp.zeros((3 * H,), jnp.float32), 'w_ao': w(ks[3], H, H), 'b_ao': jnp.zeros((H,), jnp.float32), 'ln2_s': jnp.ones((H,), jnp.float32), 'ln2_b': jnp.zeros((H,), jnp.float32), 'w_q': w(ks[4], H, H), 'b_q': jnp.zeros((H,), jnp.float32), 'w_kv': w(ks[5], H, 2 * H), 'b_kv': jnp.zeros((2 * H,), jnp.float32), 'w_co': w(ks[6], H, H), 'b_co': jnp.zeros((H,), jnp.float32), 'ln3_s': jnp.ones((H,), jnp.float32), 'ln3_b': jnp.zeros((H,), jnp.float32), 'w1': w(ks[7], H, 4 * H), 'b1': jnp.zeros((4 * H,), jnp.float32), 'w2': w(ks[8], 4 * H, H), 'b2': jnp.zeros((H,), jnp.float32)}
        return inp
    _L1_xattn_all = _L1_xattn_setup()
    _L1_xattn_in = {k: v for k, v in _L1_xattn_all.items() if k in ('ln1_s', 'ln1_b', 'w_qkv', 'b_qkv', 'w_ao', 'b_ao', 'ln2_s', 'ln2_b', 'w_q', 'b_q', 'w_kv', 'b_kv', 'w_co', 'b_co', 'ln3_s', 'ln3_b', 'w1', 'b1', 'w2', 'b2')}
    del _L1_xattn_all

    def _L2_xattn_setup():
        import jax, jax.numpy as jnp
        import numpy as np
        H = 256
        NH = 16
        HD = H // NH
        EPS = 1e-05

        def gelu(x):
            return 0.5 * x * (1.0 + jnp.tanh(0.7978845608028654 * x * (1.0 + 0.044715 * x * x)))

        def layernorm(x, scale, bias):
            m = jnp.mean(x, axis=-1, keepdims=True)
            v = jnp.mean(jnp.square(x - m), axis=-1, keepdims=True)
            return (x - m) * jax.lax.rsqrt(v + EPS) * scale + bias

        def split_heads(x):
            b, s, _ = x.shape
            return x.reshape(b, s, NH, HD).transpose(0, 2, 1, 3)

        def merge_heads(x):
            b, nh, s, hd = x.shape
            return x.transpose(0, 2, 1, 3).reshape(b, s, nh * hd)

        def attention(q, k, v, mask):
            scores = jnp.einsum('bhqd,bhkd->bhqk', q, k) / jnp.sqrt(jnp.float32(HD))
            scores = scores * mask - 10000.0 * (1.0 - mask)
            probs = jax.nn.softmax(scores, axis=-1)
            return jnp.einsum('bhqk,bhkd->bhqd', probs, v)
        key = jax.random.key(seed)
        ks = jax.random.split(key, 16)
        b, s, t = (2, 128, 128)
        w = lambda k, i, o: jax.random.normal(k, (i, o), jnp.float32) * 0.02
        inp = {'hidden_states': jax.random.normal(ks[0], (b, s, H), jnp.float32), 'encoder_states': jax.random.normal(ks[1], (b, t, H), jnp.float32), 'ltor_mask': jnp.tril(jnp.ones((1, 1, s, s), jnp.float32)), 'cross_mask': jnp.ones((b, 1, s, t), jnp.float32), 'ln1_s': jnp.ones((H,), jnp.float32), 'ln1_b': jnp.zeros((H,), jnp.float32), 'w_qkv': w(ks[2], H, 3 * H), 'b_qkv': jnp.zeros((3 * H,), jnp.float32), 'w_ao': w(ks[3], H, H), 'b_ao': jnp.zeros((H,), jnp.float32), 'ln2_s': jnp.ones((H,), jnp.float32), 'ln2_b': jnp.zeros((H,), jnp.float32), 'w_q': w(ks[4], H, H), 'b_q': jnp.zeros((H,), jnp.float32), 'w_kv': w(ks[5], H, 2 * H), 'b_kv': jnp.zeros((2 * H,), jnp.float32), 'w_co': w(ks[6], H, H), 'b_co': jnp.zeros((H,), jnp.float32), 'ln3_s': jnp.ones((H,), jnp.float32), 'ln3_b': jnp.zeros((H,), jnp.float32), 'w1': w(ks[7], H, 4 * H), 'b1': jnp.zeros((4 * H,), jnp.float32), 'w2': w(ks[8], 4 * H, H), 'b2': jnp.zeros((H,), jnp.float32)}
        return inp
    _L2_xattn_all = _L2_xattn_setup()
    _L2_xattn_in = {k: v for k, v in _L2_xattn_all.items() if k in ('ln1_s', 'ln1_b', 'w_qkv', 'b_qkv', 'w_ao', 'b_ao', 'ln2_s', 'ln2_b', 'w_q', 'b_q', 'w_kv', 'b_kv', 'w_co', 'b_co', 'ln3_s', 'ln3_b', 'w1', 'b1', 'w2', 'b2')}
    del _L2_xattn_all

    def _L3_xattn_setup():
        import jax, jax.numpy as jnp
        import numpy as np
        B, L, E, H = (4, 64, 256, 32)
        S = E // H
        EXTRA_MAA, EXTRA_DECAY = (32, 64)
        EPS = 1e-05

        def _ln(x, w, b):
            m = jnp.mean(x, axis=-1, keepdims=True)
            v = jnp.mean((x - m) ** 2, axis=-1, keepdims=True)
            return (x - m) * jax.lax.rsqrt(v + EPS) * w + b

        def _token_shift(xn, prev_row):
            first = (prev_row - xn[:, 0])[:, None]
            rest = xn[:, :-1] - xn[:, 1:]
            return jnp.concatenate([first, rest], axis=1)
        key = jax.random.key(seed)
        ks = jax.random.split(key, 24)
        rn = lambda k, shp, s=1.0: jax.random.normal(k, shp, dtype=jnp.float32) * s
        return dict(x=rn(ks[0], (B, L, E)), state=rn(ks[1], (B, 2 + S, E), 0.1), ln1_w=jnp.ones((E,), jnp.float32), ln1_b=jnp.zeros((E,), jnp.float32), ln2_w=jnp.ones((E,), jnp.float32), ln2_b=jnp.zeros((E,), jnp.float32), maa_x=rn(ks[2], (E,), 0.02), maa_w1=rn(ks[3], (E, 5 * EXTRA_MAA), 0.02), maa_w2=rn(ks[4], (5, EXTRA_MAA, E), 0.02), maa_stack=rn(ks[5], (5, E), 0.02), time_decay=rn(ks[6], (E,), 0.5), decay_w1=rn(ks[7], (E, EXTRA_DECAY), 0.02), decay_w2=rn(ks[8], (EXTRA_DECAY, E), 0.02), faaaa=rn(ks[9], (H, S), 0.1), Wr=rn(ks[10], (E, E), 0.02), Wk=rn(ks[11], (E, E), 0.02), Wv=rn(ks[12], (E, E), 0.02), Wg=rn(ks[13], (E, E), 0.02), Wo=rn(ks[14], (E, E), 0.02), gn_w=jnp.ones((E,), jnp.float32), gn_b=jnp.zeros((E,), jnp.float32), ffn_maa_k=rn(ks[15], (E,), 0.02), ffn_maa_r=rn(ks[16], (E,), 0.02), ffn_Wk=rn(ks[17], (E, E), 0.02), ffn_Wr=rn(ks[18], (E, E), 0.02), ffn_Wv=rn(ks[19], (E, E), 0.02), i=0)
    _L3_xattn_all = _L3_xattn_setup()
    _L3_xattn_in = {k: v for k, v in _L3_xattn_all.items() if k in ('ln1_w', 'ln1_b', 'ln2_w', 'ln2_b', 'maa_x', 'maa_w1', 'maa_w2', 'maa_stack', 'time_decay', 'decay_w1', 'decay_w2', 'faaaa', 'Wr', 'Wk', 'Wv', 'Wg', 'Wo', 'gn_w', 'gn_b', 'ffn_maa_k', 'ffn_maa_r', 'ffn_Wk', 'ffn_Wr', 'ffn_Wv')}
    del _L3_xattn_all
    return {'x': x, 'ctx_2048': ctx_2048, 'mask_1x1xSxS2_fc1': mask_1x1xSxS2_fc1, 'mask_Bx1xSxS2_ff1': mask_Bx1xSxS2_ff1, 'L0_xattn_w_qk': _L0_xattn_in['w_qk'], 'L0_xattn_w_v': _L0_xattn_in['w_v'], 'L0_xattn_b_v': _L0_xattn_in['b_v'], 'L0_xattn_w_t': _L0_xattn_in['w_t'], 'L0_xattn_b_t': _L0_xattn_in['b_t'], 'L1_xattn_ln1_s': _L1_xattn_in['ln1_s'], 'L1_xattn_ln1_b': _L1_xattn_in['ln1_b'], 'L1_xattn_w_qkv': _L1_xattn_in['w_qkv'], 'L1_xattn_b_qkv': _L1_xattn_in['b_qkv'], 'L1_xattn_w_ao': _L1_xattn_in['w_ao'], 'L1_xattn_b_ao': _L1_xattn_in['b_ao'], 'L1_xattn_ln2_s': _L1_xattn_in['ln2_s'], 'L1_xattn_ln2_b': _L1_xattn_in['ln2_b'], 'L1_xattn_w_q': _L1_xattn_in['w_q'], 'L1_xattn_b_q': _L1_xattn_in['b_q'], 'L1_xattn_w_kv': _L1_xattn_in['w_kv'], 'L1_xattn_b_kv': _L1_xattn_in['b_kv'], 'L1_xattn_w_co': _L1_xattn_in['w_co'], 'L1_xattn_b_co': _L1_xattn_in['b_co'], 'L1_xattn_ln3_s': _L1_xattn_in['ln3_s'], 'L1_xattn_ln3_b': _L1_xattn_in['ln3_b'], 'L1_xattn_w1': _L1_xattn_in['w1'], 'L1_xattn_b1': _L1_xattn_in['b1'], 'L1_xattn_w2': _L1_xattn_in['w2'], 'L1_xattn_b2': _L1_xattn_in['b2'], 'L2_xattn_ln1_s': _L2_xattn_in['ln1_s'], 'L2_xattn_ln1_b': _L2_xattn_in['ln1_b'], 'L2_xattn_w_qkv': _L2_xattn_in['w_qkv'], 'L2_xattn_b_qkv': _L2_xattn_in['b_qkv'], 'L2_xattn_w_ao': _L2_xattn_in['w_ao'], 'L2_xattn_b_ao': _L2_xattn_in['b_ao'], 'L2_xattn_ln2_s': _L2_xattn_in['ln2_s'], 'L2_xattn_ln2_b': _L2_xattn_in['ln2_b'], 'L2_xattn_w_q': _L2_xattn_in['w_q'], 'L2_xattn_b_q': _L2_xattn_in['b_q'], 'L2_xattn_w_kv': _L2_xattn_in['w_kv'], 'L2_xattn_b_kv': _L2_xattn_in['b_kv'], 'L2_xattn_w_co': _L2_xattn_in['w_co'], 'L2_xattn_b_co': _L2_xattn_in['b_co'], 'L2_xattn_ln3_s': _L2_xattn_in['ln3_s'], 'L2_xattn_ln3_b': _L2_xattn_in['ln3_b'], 'L2_xattn_w1': _L2_xattn_in['w1'], 'L2_xattn_b1': _L2_xattn_in['b1'], 'L2_xattn_w2': _L2_xattn_in['w2'], 'L2_xattn_b2': _L2_xattn_in['b2'], 'L3_xattn_ln1_w': _L3_xattn_in['ln1_w'], 'L3_xattn_ln1_b': _L3_xattn_in['ln1_b'], 'L3_xattn_ln2_w': _L3_xattn_in['ln2_w'], 'L3_xattn_ln2_b': _L3_xattn_in['ln2_b'], 'L3_xattn_maa_x': _L3_xattn_in['maa_x'], 'L3_xattn_maa_w1': _L3_xattn_in['maa_w1'], 'L3_xattn_maa_w2': _L3_xattn_in['maa_w2'], 'L3_xattn_maa_stack': _L3_xattn_in['maa_stack'], 'L3_xattn_time_decay': _L3_xattn_in['time_decay'], 'L3_xattn_decay_w1': _L3_xattn_in['decay_w1'], 'L3_xattn_decay_w2': _L3_xattn_in['decay_w2'], 'L3_xattn_faaaa': _L3_xattn_in['faaaa'], 'L3_xattn_Wr': _L3_xattn_in['Wr'], 'L3_xattn_Wk': _L3_xattn_in['Wk'], 'L3_xattn_Wv': _L3_xattn_in['Wv'], 'L3_xattn_Wg': _L3_xattn_in['Wg'], 'L3_xattn_Wo': _L3_xattn_in['Wo'], 'L3_xattn_gn_w': _L3_xattn_in['gn_w'], 'L3_xattn_gn_b': _L3_xattn_in['gn_b'], 'L3_xattn_ffn_maa_k': _L3_xattn_in['ffn_maa_k'], 'L3_xattn_ffn_maa_r': _L3_xattn_in['ffn_maa_r'], 'L3_xattn_ffn_Wk': _L3_xattn_in['ffn_Wk'], 'L3_xattn_ffn_Wr': _L3_xattn_in['ffn_Wr'], 'L3_xattn_ffn_Wv': _L3_xattn_in['ffn_Wv']}

def reference(x, ctx_2048, mask_1x1xSxS2_fc1, mask_Bx1xSxS2_ff1, L0_xattn_w_qk, L0_xattn_w_v, L0_xattn_b_v, L0_xattn_w_t, L0_xattn_b_t, L1_xattn_ln1_s, L1_xattn_ln1_b, L1_xattn_w_qkv, L1_xattn_b_qkv, L1_xattn_w_ao, L1_xattn_b_ao, L1_xattn_ln2_s, L1_xattn_ln2_b, L1_xattn_w_q, L1_xattn_b_q, L1_xattn_w_kv, L1_xattn_b_kv, L1_xattn_w_co, L1_xattn_b_co, L1_xattn_ln3_s, L1_xattn_ln3_b, L1_xattn_w1, L1_xattn_b1, L1_xattn_w2, L1_xattn_b2, L2_xattn_ln1_s, L2_xattn_ln1_b, L2_xattn_w_qkv, L2_xattn_b_qkv, L2_xattn_w_ao, L2_xattn_b_ao, L2_xattn_ln2_s, L2_xattn_ln2_b, L2_xattn_w_q, L2_xattn_b_q, L2_xattn_w_kv, L2_xattn_b_kv, L2_xattn_w_co, L2_xattn_b_co, L2_xattn_ln3_s, L2_xattn_ln3_b, L2_xattn_w1, L2_xattn_b1, L2_xattn_w2, L2_xattn_b2, L3_xattn_ln1_w, L3_xattn_ln1_b, L3_xattn_ln2_w, L3_xattn_ln2_b, L3_xattn_maa_x, L3_xattn_maa_w1, L3_xattn_maa_w2, L3_xattn_maa_stack, L3_xattn_time_decay, L3_xattn_decay_w1, L3_xattn_decay_w2, L3_xattn_faaaa, L3_xattn_Wr, L3_xattn_Wk, L3_xattn_Wv, L3_xattn_Wg, L3_xattn_Wo, L3_xattn_gn_w, L3_xattn_gn_b, L3_xattn_ffn_maa_k, L3_xattn_ffn_maa_r, L3_xattn_ffn_Wk, L3_xattn_ffn_Wr, L3_xattn_ffn_Wv):
    import jax
    import jax.numpy as jnp

    def _L0_xattn_ref(x, y, w_qk, w_v, b_v, w_t, b_t):
        import jax, jax.numpy as jnp
        import numpy as np
        B, C, N = (8, 64, 256)
        x_q = jnp.einsum('oc,bcn->bno', w_qk, y)
        x_k = jnp.einsum('oc,bcn->bon', w_qk, x)
        x_v = jnp.einsum('oc,bcn->bon', w_v, x) + b_v[None, :, None]
        energy = jnp.einsum('bnc,bcm->bnm', x_q, x_k)
        attention = jax.nn.softmax(energy, axis=-1)
        attention = attention / (1e-07 + attention.sum(axis=1, keepdims=True))
        x_r = jnp.einsum('bcn,bnm->bcm', x_v, attention)
        x_r = jax.nn.relu(jnp.einsum('oc,bcn->bon', w_t, x - x_r) + b_t[None, :, None])
        return x + x_r

    def _L1_xattn_ref(hidden_states, encoder_states, ltor_mask, cross_mask, ln1_s, ln1_b, w_qkv, b_qkv, w_ao, b_ao, ln2_s, ln2_b, w_q, b_q, w_kv, b_kv, w_co, b_co, ln3_s, ln3_b, w1, b1, w2, b2):
        import jax, jax.numpy as jnp
        import numpy as np
        H = 256
        NH = 16
        HD = H // NH
        EPS = 1e-05

        def gelu(x):
            return 0.5 * x * (1.0 + jnp.tanh(0.7978845608028654 * x * (1.0 + 0.044715 * x * x)))

        def layernorm(x, scale, bias):
            m = jnp.mean(x, axis=-1, keepdims=True)
            v = jnp.mean(jnp.square(x - m), axis=-1, keepdims=True)
            return (x - m) * jax.lax.rsqrt(v + EPS) * scale + bias

        def split_heads(x):
            b, s, _ = x.shape
            return x.reshape(b, s, NH, HD).transpose(0, 2, 1, 3)

        def merge_heads(x):
            b, nh, s, hd = x.shape
            return x.transpose(0, 2, 1, 3).reshape(b, s, nh * hd)

        def attention(q, k, v, mask):
            scores = jnp.einsum('bhqd,bhkd->bhqk', q, k) / jnp.sqrt(jnp.float32(HD))
            scores = scores * mask - 10000.0 * (1.0 - mask)
            probs = jax.nn.softmax(scores, axis=-1)
            return jnp.einsum('bhqk,bhkd->bhqd', probs, v)
        ln_out = layernorm(hidden_states, ln1_s, ln1_b)
        qkv = ln_out @ w_qkv + b_qkv
        q, k, v = jnp.split(qkv, 3, axis=-1)
        ctx = merge_heads(attention(split_heads(q), split_heads(k), split_heads(v), ltor_mask))
        attn_out = ctx @ w_ao + b_ao
        x = hidden_states + attn_out
        ln_out = layernorm(x, ln2_s, ln2_b)
        q = ln_out @ w_q + b_q
        kv = encoder_states @ w_kv + b_kv
        k, v = jnp.split(kv, 2, axis=-1)
        ctx = merge_heads(attention(split_heads(q), split_heads(k), split_heads(v), cross_mask))
        cross_out = ctx @ w_co + b_co
        x = x + cross_out
        ln_out = layernorm(x, ln3_s, ln3_b)
        mlp_out = gelu(ln_out @ w1 + b1) @ w2 + b2
        return x + mlp_out

    def _L2_xattn_ref(hidden_states, encoder_states, ltor_mask, cross_mask, ln1_s, ln1_b, w_qkv, b_qkv, w_ao, b_ao, ln2_s, ln2_b, w_q, b_q, w_kv, b_kv, w_co, b_co, ln3_s, ln3_b, w1, b1, w2, b2):
        import jax, jax.numpy as jnp
        import numpy as np
        H = 256
        NH = 16
        HD = H // NH
        EPS = 1e-05

        def gelu(x):
            return 0.5 * x * (1.0 + jnp.tanh(0.7978845608028654 * x * (1.0 + 0.044715 * x * x)))

        def layernorm(x, scale, bias):
            m = jnp.mean(x, axis=-1, keepdims=True)
            v = jnp.mean(jnp.square(x - m), axis=-1, keepdims=True)
            return (x - m) * jax.lax.rsqrt(v + EPS) * scale + bias

        def split_heads(x):
            b, s, _ = x.shape
            return x.reshape(b, s, NH, HD).transpose(0, 2, 1, 3)

        def merge_heads(x):
            b, nh, s, hd = x.shape
            return x.transpose(0, 2, 1, 3).reshape(b, s, nh * hd)

        def attention(q, k, v, mask):
            scores = jnp.einsum('bhqd,bhkd->bhqk', q, k) / jnp.sqrt(jnp.float32(HD))
            scores = scores * mask - 10000.0 * (1.0 - mask)
            probs = jax.nn.softmax(scores, axis=-1)
            return jnp.einsum('bhqk,bhkd->bhqd', probs, v)
        ln_out = layernorm(hidden_states, ln1_s, ln1_b)
        qkv = ln_out @ w_qkv + b_qkv
        q, k, v = jnp.split(qkv, 3, axis=-1)
        ctx = merge_heads(attention(split_heads(q), split_heads(k), split_heads(v), ltor_mask))
        attn_out = ctx @ w_ao + b_ao
        x = hidden_states + attn_out
        ln_out = layernorm(x, ln2_s, ln2_b)
        q = ln_out @ w_q + b_q
        kv = encoder_states @ w_kv + b_kv
        k, v = jnp.split(kv, 2, axis=-1)
        ctx = merge_heads(attention(split_heads(q), split_heads(k), split_heads(v), cross_mask))
        cross_out = ctx @ w_co + b_co
        x = x + cross_out
        ln_out = layernorm(x, ln3_s, ln3_b)
        mlp_out = gelu(ln_out @ w1 + b1) @ w2 + b2
        return x + mlp_out

    def _L3_xattn_ref(x, state, ln1_w, ln1_b, ln2_w, ln2_b, maa_x, maa_w1, maa_w2, maa_stack, time_decay, decay_w1, decay_w2, faaaa, Wr, Wk, Wv, Wg, Wo, gn_w, gn_b, ffn_maa_k, ffn_maa_r, ffn_Wk, ffn_Wr, ffn_Wv, i):
        import jax, jax.numpy as jnp
        import numpy as np
        B, L, E, H = (4, 64, 256, 32)
        S = E // H
        EXTRA_MAA, EXTRA_DECAY = (32, 64)
        EPS = 1e-05

        def _ln(x, w, b):
            m = jnp.mean(x, axis=-1, keepdims=True)
            v = jnp.mean((x - m) ** 2, axis=-1, keepdims=True)
            return (x - m) * jax.lax.rsqrt(v + EPS) * w + b

        def _token_shift(xn, prev_row):
            first = (prev_row - xn[:, 0])[:, None]
            rest = xn[:, :-1] - xn[:, 1:]
            return jnp.concatenate([first, rest], axis=1)
        b, l = (x.shape[0], x.shape[1])
        i0 = (2 + S) * i + 0
        i1 = (2 + S) * i + 1
        xn = _ln(x, ln1_w, ln1_b)
        sx = _token_shift(xn, state[:, i1])
        xxx = jnp.tanh((xn + sx * maa_x) @ maa_w1).reshape(b, l, 5, 1, EXTRA_MAA)
        xxx = jnp.matmul(xxx, maa_w2).reshape(b, l, 5, E)
        x5 = xn[:, :, None] + sx[:, :, None] * (maa_stack + xxx)
        w = jnp.exp(-jnp.exp(time_decay + jnp.tanh(x5[:, :, 1] @ decay_w1) @ decay_w2))
        w = w.reshape(b, l, H, S)
        r = (x5[:, :, 3] @ Wr.T).reshape(b, l, H, S)
        k = (x5[:, :, 0] @ Wk.T).reshape(b, l, H, S)
        v = (x5[:, :, 2] @ Wv.T).reshape(b, l, H, S)
        g = jax.nn.silu(x5[:, :, 4] @ Wg.T)
        s0 = state[:, (2 + S) * i + 2:(2 + S) * (i + 1)].reshape(b, H, S, S)
        u = faaaa[None, :, :, None]

        def step(s, rkvw):
            r_t, k_t, v_t, w_t = rkvw
            a = k_t[:, :, :, None] * v_t[:, :, None, :]
            out = jnp.einsum('bhk,bhkd->bhd', r_t, u * a + s)
            return (a + w_t[:, :, :, None] * s, out)
        xs = tuple((jnp.moveaxis(t, 1, 0) for t in (r, k, v, w)))
        _, outs = jax.lax.scan(step, s0, xs)
        att = jnp.moveaxis(outs, 0, 1).reshape(b, l, E)
        a4 = att.reshape(b, l, H, S)
        m = jnp.mean(a4, axis=-1, keepdims=True)
        var = jnp.mean((a4 - m) ** 2, axis=-1, keepdims=True)
        att = ((a4 - m) * jax.lax.rsqrt(var + EPS)).reshape(b, l, E) * gn_w + gn_b
        x = x + att * g @ Wo.T
        xn2 = _ln(x, ln2_w, ln2_b)
        sx2 = _token_shift(xn2, state[:, i0])
        xk = xn2 + sx2 * ffn_maa_k
        xr = xn2 + sx2 * ffn_maa_r
        rr = jax.nn.sigmoid(xr @ ffn_Wr.T)
        kk = jnp.square(jax.nn.relu(xk @ ffn_Wk.T))
        x = x + rr * (kk @ ffn_Wv.T)
        return x
    x = _L0_xattn_ref(x, ctx_2048, L0_xattn_w_qk, L0_xattn_w_v, L0_xattn_b_v, L0_xattn_w_t, L0_xattn_b_t)
    x = _L1_xattn_ref(x, ctx_2048, mask_1x1xSxS2_fc1, mask_Bx1xSxS2_ff1, L1_xattn_ln1_s, L1_xattn_ln1_b, L1_xattn_w_qkv, L1_xattn_b_qkv, L1_xattn_w_ao, L1_xattn_b_ao, L1_xattn_ln2_s, L1_xattn_ln2_b, L1_xattn_w_q, L1_xattn_b_q, L1_xattn_w_kv, L1_xattn_b_kv, L1_xattn_w_co, L1_xattn_b_co, L1_xattn_ln3_s, L1_xattn_ln3_b, L1_xattn_w1, L1_xattn_b1, L1_xattn_w2, L1_xattn_b2)
    x = _L2_xattn_ref(x, ctx_2048, mask_1x1xSxS2_fc1, mask_Bx1xSxS2_ff1, L2_xattn_ln1_s, L2_xattn_ln1_b, L2_xattn_w_qkv, L2_xattn_b_qkv, L2_xattn_w_ao, L2_xattn_b_ao, L2_xattn_ln2_s, L2_xattn_ln2_b, L2_xattn_w_q, L2_xattn_b_q, L2_xattn_w_kv, L2_xattn_b_kv, L2_xattn_w_co, L2_xattn_b_co, L2_xattn_ln3_s, L2_xattn_ln3_b, L2_xattn_w1, L2_xattn_b1, L2_xattn_w2, L2_xattn_b2)
    x = _L3_xattn_ref(x, ctx_2048, L3_xattn_ln1_w, L3_xattn_ln1_b, L3_xattn_ln2_w, L3_xattn_ln2_b, L3_xattn_maa_x, L3_xattn_maa_w1, L3_xattn_maa_w2, L3_xattn_maa_stack, L3_xattn_time_decay, L3_xattn_decay_w1, L3_xattn_decay_w2, L3_xattn_faaaa, L3_xattn_Wr, L3_xattn_Wk, L3_xattn_Wv, L3_xattn_Wg, L3_xattn_Wo, L3_xattn_gn_w, L3_xattn_gn_b, L3_xattn_ffn_maa_k, L3_xattn_ffn_maa_r, L3_xattn_ffn_Wk, L3_xattn_ffn_Wr, L3_xattn_ffn_Wv, 0)
    return x

_drawn_inputs = setup_inputs


def setup_inputs(seed=0):
    import zlib

    import numpy as np

    out = dict(_drawn_inputs(seed))
    spreads = {'L1_xattn_ln1_s': (1.0, 0.6),
     'L1_xattn_ln1_b': (0.0, 0.8),
     'L1_xattn_b_qkv': (0.0, 0.34),
     'L1_xattn_b_ao': (0.0, 0.1),
     'L1_xattn_ln2_s': (1.0, 0.6),
     'L1_xattn_ln2_b': (0.0, 2.0),
     'L1_xattn_b_q': (0.0, 2.0),
     'L1_xattn_b_kv': (0.0, 0.345),
     'L1_xattn_b_co': (0.0, 0.1),
     'L1_xattn_ln3_s': (1.0, 0.6),
     'L1_xattn_ln3_b': (0.0, 0.8),
     'L1_xattn_b1': (0.0, 0.302),
     'L1_xattn_b2': (0.0, 0.1),
     'L2_xattn_ln1_s': (1.0, 0.6),
     'L2_xattn_ln1_b': (0.0, 0.8),
     'L2_xattn_b_qkv': (0.0, 0.362),
     'L2_xattn_b_ao': (0.0, 0.1),
     'L2_xattn_ln2_s': (1.0, 0.6),
     'L2_xattn_ln2_b': (0.0, 2.0),
     'L2_xattn_b_q': (0.0, 2.0),
     'L2_xattn_b_kv': (0.0, 0.333),
     'L2_xattn_b_co': (0.0, 0.1),
     'L2_xattn_ln3_s': (1.0, 0.6),
     'L2_xattn_ln3_b': (0.0, 0.8),
     'L2_xattn_b1': (0.0, 0.304),
     'L2_xattn_b2': (0.0, 0.1),
     'L3_xattn_ln1_w': (1.0, 0.6),
     'L3_xattn_ln1_b': (0.0, 0.721),
     'L3_xattn_ln2_w': (1.0, 0.6),
     'L3_xattn_ln2_b': (0.0, 0.8),
     'L3_xattn_gn_w': (1.0, 0.6),
     'L3_xattn_gn_b': (0.0, 0.8)}
    factors = {'L1_xattn_w_qkv': 3.857,
     'L1_xattn_w_q': 200.0,
     'L2_xattn_w_qkv': 3.122,
     'L2_xattn_w_q': 200.0,
     'L3_xattn_maa_x': 8.0,
     'L3_xattn_maa_w1': 8.0,
     'L3_xattn_maa_w2': 8.0,
     'L3_xattn_maa_stack': 8.0,
     'L3_xattn_time_decay': 3.615,
     'L3_xattn_decay_w1': 8.0,
     'L3_xattn_decay_w2': 8.0,
     'L3_xattn_faaaa': 7.508,
     'L3_xattn_ffn_maa_k': 8.0,
     'L3_xattn_ffn_maa_r': 8.0,
     'L3_xattn_ffn_Wk': 3.68,
     'L3_xattn_ffn_Wr': 8.0,
     'L3_xattn_ffn_Wv': 3.411}
    for name, (base, spread) in spreads.items():
        noise = np.random.default_rng([zlib.crc32(name.encode()), seed]).standard_normal(out[name].shape)
        drawn = base * np.exp(spread * noise) if base else spread * noise
        out[name] = jnp.asarray(drawn.astype(out[name].dtype))
    for name, factor in factors.items():
        out[name] = (out[name] * factor).astype(out[name].dtype)
    return out
```

```python
from contextlib import ExitStack

import concourse.bass as bass
from concourse import mybir

F32 = mybir.dt.float32
ALU = mybir.AluOpType
ACT = mybir.ActivationFunctionType
AX = mybir.AxisListType.X

P = 128
B, S, D = 32, 64, 256
T = B * S
NP = 4
GT = NP * P
GB = GT // S
NG = T // GT
NC = D // P
NH, HD = 16, 16
NPAIR = NH // 2
VW = 2 * HD + 2
DFF = 1024
NJ = DFF // P
LAYERS = 2
TURNS = LAYERS * NG
EPS = 1e-5
GELU_C = 0.7978845608028654
RS = 8
NMAA, RMAA, RDEC = 5, 32, 64

WL = {}
_at = 0
for _n, _w in (("qk", 2 * D), ("v", D), ("ao", D), ("q2", D), ("k2", D), ("v2", D), ("co", D), ("w1", DFF)):
    WL[_n] = (_at, _at + _w)
    _at += _w
WL_COLS = _at
VL = {}
_at = 0
for _n, _w in (("ln1_s", 2), ("ln1_b", 2), ("ln2_s", 2), ("ln2_b", 2), ("ln3_s", 2), ("ln3_b", 2),
               ("bq", 2), ("bk", 2), ("bq2", 2), ("bk2", 2), ("b1", NJ)):
    VL[_n] = _at
    _at += _w
VL_COLS = _at
RL = {n: i * D for i, n in enumerate(("bv", "bao", "bv2", "bco", "b2"))}
RL_COLS = len(RL) * D
WC = {}
_at = 0
for _n, _w in (("maa1", NMAA * RMAA), ("dec1", RDEC), ("r", D), ("k", D), ("v", D), ("g", D), ("o", D),
               ("fk", D), ("fr", D), ("fv", D)):
    WC[_n] = (_at, _at + _w)
    _at += _w
WC_COLS = _at
VC = {n: 2 * i for i, n in enumerate(("ln1_w", "ln1_b", "ln2_w", "ln2_b", "maa_x", "st0", "st1", "st2", "st3", "st4",
                                      "decay", "u", "gn_w", "gn_b", "fmk", "fmr"))}
VC_COLS = 2 * len(VC)


def build(nc, io):
    ctx = ExitStack()
    with ctx:
        def sb(name, *shape):
            return ctx.enter_context(nc.sbuf_tensor(name, [P, *shape], F32))

        ps = ctx.enter_context(nc.psum_tensor("ps", [P, 8, 512], F32))
        x_mid = nc.dram_tensor("x_mid", [T, D], F32, kind="Internal").ap()
        sem = lambda n: ctx.enter_context(nc.semaphore(n))
        ld_b, ld_c, ld_v, ld_r = sem("ld_b"), sem("ld_c"), sem("ld_vectors"), sem("ld_rows")
        ld_w = {n: sem("ld_" + n) for n in ("k2", "v2", "qk", "v", "ao", "q2", "co", "w1", "w2")}
        weights = {
            "ident": sb("ident", P),
            "wc": sb("wc", NC, WC_COLS), "maa2a": sb("maa2a", D), "maa2b": sb("maa2b", D), "dec2": sb("dec2", D),
            "vc": sb("vc", VC_COLS), "sel": sb("sel", RS, P), "red": sb("red", RS, P),
            "head_ones": sb("head_ones", P), "head_mean": sb("head_mean", P),
        }
        with ExitStack() as layer_ctx:
            def sb(name, *shape):
                return layer_ctx.enter_context(nc.sbuf_tensor(name, [P, *shape], F32))
            weights |= {
                "wl": sb("wl", NC, WL_COLS), "w2": sb("w2", NJ, D), "vl": sb("vl", VL_COLS), "rl": sb("rl", RL_COLS),
                "self_mask": sb("self_mask", S), "parity": sb("parity", 2),
            }
            phase_a(nc, io, ps, weights, x_mid, ld_b, ld_c, dict(ld_w, vl=ld_v, rl=ld_r))
            phase_b(nc, io, ps, weights, x_mid, ld_b, ld_v, ld_r, ld_w)
        phase_c(nc, io, ps, weights, x_mid, ld_c)


def load_layer_pieces(w, io, layer):
    def cols(n):
        a, b = WL[n]
        return w["wl"][:, :, a:b], io["wl"][layer].rearrange("(c p) n -> p c n", p=P)[:, :, a:b]
    rows = (w["rl"][:, :], io["rl"][layer:layer + 1, :].broadcast_to([P, RL_COLS]))
    return ([("vl", w["vl"][:, :], io["vl"][layer]), ("rl", *rows)]
            + [(n, *cols(n)) for n in ("k2", "v2", "qk", "v", "ao", "q2", "co", "w1")]
            + [("w2", w["w2"][:, :, :], io["w2"][layer].rearrange("(c p) n -> p c n", p=P))])


N_B_CONST = 4
N_C_CONST = 9


def phase_a(nc, io, ps, w, x_mid, ld_b, ld_c, ld_piece):
    ctx = ExitStack()
    with ctx:
        def sb(name, *shape):
            return ctx.enter_context(nc.sbuf_tensor("a_" + name, [P, *shape], F32))

        def sem(name):
            return ctx.enter_context(nc.semaphore("a_" + name))

        x_in, y_in, x_keep, x_out = (sb(n, NP, D) for n in ("x_in", "y_in", "x_keep", "x_out"))
        w0, bv, bt = sb("w0", 3, P), sb("bv", P), sb("bt", 1)
        qk = sb("qk", 2, 2, D)
        att = sb("att", 2, 4, D)
        neg_max, row_sum, row_inv = sb("neg_max", NP, 4), sb("row_sum", NP, 4), sb("row_inv", NP, 4)
        xv_b, xv_n = sb("xv_b", 2, D), sb("xv_n", 2, D)
        col_inv, diff, gate = sb("col_inv", 2, D), sb("diff", 2, D), sb("gate", 2, D)

        ld_w, ld_xy, stored, out_free = sem("ld_w"), sem("ld_xy"), sem("stored"), sem("out_free")
        proj_ps, qk_ok, xv_ps, xvb_ok, xvn_ok = sem("proj_ps"), sem("qk_ok"), sem("xv_ps"), sem("xvb_ok"), sem("xvn_ok")
        en_ps, max_ok, exp_ok, inv_ok = sem("en_ps"), sem("max_ok"), sem("exp_ok"), sem("inv_ok")
        xr_ps, eps_ok, col_ok, xrn_ok, diff_ok = (sem("xr_ps"), sem("eps_ok"), sem("col_ok"), sem("xrn_ok"),
                                                  sem("diff_ok"))
        t_ps, gate_ok, keep_ok, out_ok = sem("t_ps"), sem("gate_ok"), sem("keep_ok"), sem("out_ok")

        x_rows = io["x"].rearrange("(g p q) d -> g q p d", p=NP, q=P)
        y_rows = io["ctx"].rearrange("(g p q) d -> g q p d", p=NP, q=P)
        o_rows = x_mid.rearrange("(g p q) d -> g q p d", p=NP, q=P)
        EN, PROJ, TPS, XV, XR = 0, 4, 5, 6, 7
        block = ctx.enter_context(nc.Block())

        @block.sync
        def _(sp):
            sp.dma_start(w0[:, :, :], io["w0"]).then_inc(ld_w, 16)
            sp.dma_start(x_in[:, :, :], x_rows[0]).then_inc(ld_xy, 16)
            sp.dma_start(y_in[:, :, :], y_rows[0]).then_inc(ld_xy, 16)
            sp.dma_start(bv[:, :], io["bv0"].broadcast_to([P, P])).then_inc(ld_w, 16)
            sp.dma_start(bt[:, :], io["bt0"]).then_inc(ld_w, 16)
            for n, dst, src in load_layer_pieces(w, io, 0):
                sp.dma_start(dst, src).then_inc(ld_piece[n], 16)
            sp.sem_inc(out_free, 1)
            with sp.Fori(0, NG - 1) as it:
                sp.wait_ge(xv_ps, NP * it + NP)
                sp.wait_ge(keep_ok, NP * it + NP)
                sp.dma_start(x_in[:, :, :], x_rows[bass.ds(it + 1, 1)].rearrange("g q p d -> (g q) p d")).then_inc(ld_xy, 16)
                sp.dma_start(y_in[:, :, :], y_rows[bass.ds(it + 1, 1)].rearrange("g q p d -> (g q) p d")).then_inc(ld_xy, 16)
                sp.wait_ge(out_ok, NP * it + NP)
                sp.dma_start(o_rows[bass.ds(it, 1)].rearrange("g q p d -> (g q) p d"), x_out[:, :, :]).then_inc(stored, 16)
                sp.wait_ge(stored, 16 * it + 16)
                sp.sem_inc(out_free, 1)
            sp.wait_ge(out_ok, NP * NG)
            sp.dma_start(o_rows[NG - 1], x_out[:, :, :]).then_inc(stored, 16)
            sp.wait_ge(stored, 16 * NG)

        @block.gpsimd
        def _(pool):
            pool.dma_start(w["ident"][:, :], io["ident"]).then_inc(ld_b, 16)
            pool.dma_start(w["self_mask"][0:S, :], io["self_mask"]).then_inc(ld_b, 16)
            pool.dma_start(w["self_mask"][S:P, :], io["self_mask"]).then_inc(ld_b, 16)
            pool.dma_start(w["parity"][:, :], io["parity"]).then_inc(ld_b, 16)
            pool.dma_start(w["wc"][:, :, :], io["wc"].rearrange("(c p) n -> p c n", p=P)).then_inc(ld_c, 16)
            pool.dma_start(w["maa2a"][:, :], io["maa2"][0:P, :]).then_inc(ld_c, 16)
            pool.dma_start(w["maa2b"][0:RMAA, :], io["maa2"][P:NMAA * RMAA, :]).then_inc(ld_c, 16)
            pool.dma_start(w["dec2"][0:RDEC, :], io["dec2"]).then_inc(ld_c, 16)
            pool.dma_start(w["vc"][:, :], io["vc"]).then_inc(ld_c, 16)
            pool.dma_start(w["sel"][:, :, :], io["sel"]).then_inc(ld_c, 16)
            pool.dma_start(w["red"][:, :, :], io["red"]).then_inc(ld_c, 16)
            pool.dma_start(w["head_ones"][:, :], io["head_ones"]).then_inc(ld_c, 16)
            pool.dma_start(w["head_mean"][:, :], io["head_mean"]).then_inc(ld_c, 16)
            with pool.Fori(0, NG) as it:
                pool.wait_ge(out_free, it + 1)
                for p in range(NP):
                    pool.wait_ge(gate_ok, NP * it + p + 1)
                    pool.tensor_tensor(x_out[:, p, :], x_keep[:, p, :], gate[:, p % 2, :], ALU.add).then_inc(out_ok, 1)

        @block.tensor
        def _(pe):
            pe.wait_ge(ld_w, 16 * 3)
            with pe.Fori(0, NG) as it:
                pe.wait_ge(ld_xy, 32 * it + 32)

                def project(p):
                    if p >= 1:
                        pe.wait_ge(qk_ok, NP * it + p)
                    pe.matmul(ps[:, PROJ, 0:D], w0[:, 0, :], y_in[:, p, :], start=True, stop=True)
                    pe.matmul(ps[:, PROJ, D:2 * D], w0[:, 0, :], x_in[:, p, :], start=True, stop=True).then_inc(proj_ps, 1)
                    if p >= 1:
                        pe.wait_ge(xvb_ok, NP * it + p)
                    for j in range(2):
                        mm = pe.matmul(ps[:, XV, j * P:(j + 1) * P], x_in[:, p, j * P:(j + 1) * P], w0[:, 1, :],
                                       start=True, stop=True)
                    mm.then_inc(xv_ps, 1)

                def energy(p):
                    pe.wait_ge(qk_ok, NP * it + p + 1)
                    if p >= 2:
                        pe.wait_ge(exp_ok, NP * it + p - 1)
                    for j in range(2):
                        for b in range(2):
                            h = slice(b * S, (b + 1) * S)
                            mm = pe.matmul(ps[:, EN + 2 * (p % 2) + b, j * D:(j + 1) * D],
                                           qk[h, p % 2, 0, j * P:(j + 1) * P], qk[h, p % 2, 1, :], start=True, stop=True)
                    mm.then_inc(en_ps, 1)

                def read_out(p):
                    pe.wait_ge(exp_ok, NP * it + p + 1)
                    pe.wait_ge(xvn_ok, NP * it + p + 1)
                    if p >= 1:
                        pe.wait_ge(xrn_ok, NP * it + p)
                    for b in range(2):
                        for j in range(2):
                            pe.matmul(ps[b * S:(b + 1) * S, XR, 0:D], xv_n[:, p % 2, (2 * b + j) * S:(2 * b + j + 1) * S],
                                      att[:, p % 2, 2 * b + j, :], start=(j == 0), stop=(j == 1))
                    for b in range(2):
                        for j in range(2):
                            mm = pe.matmul(ps[b * S:(b + 1) * S, XR, D:2 * D],
                                           row_inv[:, p, 2 * b + j:2 * b + j + 1].broadcast_to([P, S]),
                                           att[:, p % 2, 2 * b + j, :], start=(j == 0), stop=(j == 1))
                    mm.then_inc(xr_ps, 1)

                def mix_out(p):
                    pe.wait_ge(diff_ok, NP * it + p + 1)
                    if p >= 1:
                        pe.wait_ge(gate_ok, NP * it + p)
                    pe.matmul(ps[:, TPS, 0:D], w0[:, 2, :], diff[:, p % 2, :], start=True, stop=True).then_inc(t_ps, 1)

                project(0)
                project(1)
                energy(0)
                for p in range(NP):
                    if p + 2 < NP:
                        project(p + 2)
                    if p + 1 < NP:
                        energy(p + 1)
                    read_out(p)
                    if p >= 1:
                        mix_out(p - 1)
                mix_out(NP - 1)

        @block.scalar
        def _(act):
            act.wait_ge(ld_w, 16 * 3)
            with act.Fori(0, NG) as it:
                def copy_qk(p):
                    act.wait_ge(proj_ps, NP * it + p + 1)
                    if p >= 2:
                        act.wait_ge(en_ps, NP * it + p - 1)
                    act.activation(qk[:, p % 2, :, :].rearrange("q a d -> q (a d)"), ps[:, PROJ, :], ACT.Copy).then_inc(qk_ok, 1)

                def exps(p):
                    act.wait_ge(max_ok, NP * it + p + 1)
                    if p >= 2:
                        act.wait_ge(xr_ps, NP * it + p - 1)
                    for i in range(4):
                        a = act.activation(att[:, p % 2, i, :], ps[:, EN + 2 * (p % 2) + i // 2, (i % 2) * D:(i % 2 + 1) * D],
                                           ACT.Exp, bias=neg_max[:, p, i:i + 1], accum_out=row_sum[:, p, i:i + 1])
                    a.then_inc(exp_ok, 1)

                def relu(p):
                    act.wait_ge(t_ps, NP * it + p + 1)
                    if p >= 2:
                        act.wait_ge(out_ok, NP * it + p - 1)
                    act.activation(gate[:, p % 2, :], ps[:, TPS, 0:D], ACT.Relu, bias=bt[:, 0:1]).then_inc(gate_ok, 1)

                act.wait_ge(ld_xy, 32 * it + 32)
                act.wait_ge(out_free, it + 1)
                act.activation(x_keep[:, :, :], x_in[:, :, :], ACT.Copy).then_inc(keep_ok, NP)
                copy_qk(0)
                copy_qk(1)
                for p in range(NP):
                    exps(p)
                    if p + 2 < NP:
                        copy_qk(p + 2)
                    if p >= 2:
                        relu(p - 2)
                relu(NP - 2)
                relu(NP - 1)

        @block.vector
        def _(dve):
            dve.wait_ge(ld_w, 16 * 3)
            with dve.Fori(0, NG) as it:
                def row_max(p):
                    dve.wait_ge(en_ps, NP * it + p + 1)
                    dve.tensor_reduce(neg_max[:, p, :],
                                      ps[:, EN + 2 * (p % 2):EN + 2 * (p % 2) + 2, :].rearrange("q e (j m) -> q (e j) m", j=2),
                                      AX, ALU.max, negate=True).then_inc(max_ok, 1)

                def values(p):
                    dve.wait_ge(xv_ps, NP * it + p + 1)
                    dve.tensor_tensor(xv_b[:, p % 2, :].rearrange("q (j c) -> q j c", j=2),
                                      ps[:, XV, 0:D].rearrange("q (j c) -> q j c", j=2),
                                      bv[:, :].unsqueeze(1).broadcast_to([P, 2, P]), ALU.add).then_inc(xvb_ok, 1)

                def scale_values(p):
                    dve.wait_ge(exp_ok, NP * it + p + 1)
                    dve.reciprocal(row_inv[:, p, :], row_sum[:, p, :]).then_inc(inv_ok, 1)
                    dve.wait_ge(inv_ok, NP * it + p + 1)
                    dve.wait_ge(xvb_ok, NP * it + p + 1)
                    if p >= 2:
                        dve.wait_ge(xr_ps, NP * it + p - 1)
                    dve.tensor_tensor(xv_n[:, p % 2, :].rearrange("q (b j c) -> q b j c", b=2, j=2),
                                      xv_b[:, p % 2, :].rearrange("q (j b c) -> q b j c", b=2, j=2),
                                      row_inv[:, p, :].rearrange("q (b j) -> q b j", b=2).unsqueeze(3).broadcast_to([P, 2, 2, S]),
                                      ALU.mult).then_inc(xvn_ok, 1)

                def difference(p):
                    dve.wait_ge(xr_ps, NP * it + p + 1)
                    dve.tensor_scalar(col_inv[:, p % 2, :], ps[:, XR, D:2 * D], 1e-7, None, ALU.add).then_inc(eps_ok, 1)
                    dve.wait_ge(eps_ok, NP * it + p + 1)
                    dve.reciprocal(col_inv[:, p % 2, :], col_inv[:, p % 2, :]).then_inc(col_ok, 1)
                    dve.wait_ge(col_ok, NP * it + p + 1)
                    if p >= 2:
                        dve.wait_ge(t_ps, NP * it + p - 1)
                    dve.tensor_tensor(diff[:, p % 2, :], ps[:, XR, 0:D], col_inv[:, p % 2, :], ALU.mult).then_inc(xrn_ok, 1)
                    dve.wait_ge(xrn_ok, NP * it + p + 1)
                    dve.wait_ge(keep_ok, NP * it + p + 1)
                    dve.tensor_tensor(diff[:, p % 2, :], x_keep[:, p, :], diff[:, p % 2, :], ALU.subtract).then_inc(diff_ok, 1)

                values(0)
                for p in range(NP):
                    row_max(p)
                    scale_values(p)
                    if p + 1 < NP:
                        values(p + 1)
                    if p >= 1:
                        difference(p - 1)
                difference(NP - 1)


def phase_b(nc, io, ps, w, x_mid, ld_b, ld_v, ld_r, ld_w):
    ctx = ExitStack()
    with ctx:
        def sb(name, *shape):
            return ctx.enter_context(nc.sbuf_tensor("b_" + name, [P, *shape], F32))

        def sem(name):
            return ctx.enter_context(nc.semaphore("b_" + name))

        x_in, x_bias, x_cur, x_out = sb("x_in", NP, D), sb("x_bias", NP, D), sb("x_cur", NP, D), sb("x_out", NP, D)
        enc = sb("enc", NC, GT)
        raw_mask, cross_mul, cross_add = sb("raw_mask", NP, S), sb("cross_mul", NP, S), sb("cross_add", NP, S)
        self_mul, self_add = sb("self_mul", S), sb("self_add", S)
        bn, mv, var, rstd, xc = sb("bn", NP, 6), sb("mv", NP, 2), sb("var", NP), sb("rstd", NP), sb("xc", NP, D)
        minus_half, gate_mark = sb("minus_half", NP), sb("gate_mark", 1)
        hT = sb("hT", NC, GT)
        qT = sb("qT", NC, GT)
        kT = [sb(f"k{n}T", NC, 2, GT) for n in (1, 2)]
        vP = [sb(f"v{n}P", GB, NPAIR, VW) for n in (1, 2)]
        sc = sb("sc", 3, NH, S)
        neg_max = sb("neg_max", 3, NH)
        pT = sb("pT", NPAIR, P)
        inv_sum, c_tok = sb("inv_sum", NH), sb("c_tok", 2, D)
        cT = sb("cT", NC, GT)
        pre, sq, poly, th = sb("pre", 2, GT), sb("sq", 2, GT), sb("poly", 2, GT), sb("th", 2, GT)
        act_g = sb("act_g", NJ, GT)

        ld_x, ld_enc, ld_mask, stored, out_free = (sem(n) for n in ("ld_x", "ld_enc", "ld_mask", "stored", "out_free"))
        zero_ok, smask_ok, cmask_ok = sem("zero_ok"), sem("smask_ok"), sem("cmask_ok")
        k_ps, k_ok, v_ps, v_ok = ([sem(n + "1"), sem(n + "2")] for n in ("k_ps", "k_ok", "v_ps", "v_ok"))
        q_ps, q_ok = sem("q_ps"), sem("q_ok")
        bn_ok, mv_ok, var_ok, rstd_ok, xc_ok, ln_ps, hT_ok = (sem(n) for n in ("bn_ok", "mv_ok", "var_ok", "rstd_ok", "xc_ok", "ln_ps", "hT_ok"))
        sc_ps, mul_ok, add_ok, max_ok, sub_ok, exp_ok = (sem(n) for n in ("sc_ps", "mul_ok", "add_ok", "max_ok", "sub_ok", "exp_ok"))
        pT_ps, pT_ok, v_sum_ps, inv_ok, tok_ok, c_ps, c_ok = (sem(n) for n in ("pT_ps", "pT_ok", "v_sum_ps", "inv_ok", "tok_ok", "c_ps", "c_ok"))
        o_ps, bias_ok, res_ok = sem("o_ps"), sem("bias_ok"), sem("res_ok")
        h_ps, pre_ok, sq_ok, poly_ok, arg_ok, th_ok, g_ok = (sem(n) for n in ("h_ps", "pre_ok", "sq_ok", "poly_ok", "arg_ok", "th_ok", "g_ok"))
        m_ps, out_ok = sem("m_ps"), sem("out_ok")

        N_LN, N_ATT, N_BIAS = 3 * NP, 2 * NP, 3 * NP

        rows = x_mid.rearrange("(g p q) d -> g q p d", p=NP, q=P)
        enc_cols = io["ctxT"].rearrange("(c p) (g t) -> g p c t", p=P, g=NG)
        mask_rows = io["cross_mask"].rearrange("(g p q) k -> g q p k", p=NP, q=P)

        def weight(n, c, a=0, b=None):
            lo, hi = WL[n]
            return w["wl"][:, c, lo + a:hi if b is None else lo + b]

        def vec(n, i):
            return w["vl"][:, VL[n] + i:VL[n] + i + 1]

        def row(n):
            return w["rl"][:, RL[n]:RL[n] + D]

        SC, CT, LN1, Q_BANK, LN23, PT, V_BANK, K_BANK, CX, OUT, H_BANK, M_BANK = 0, 0, 0, 2, 4, 4, 4, 6, 6, 7, 6, 0
        block = ctx.enter_context(nc.Block())

        @block.sync
        def _(sp):
            def one(view, group):
                return view[bass.ds(group, 1)].rearrange("g p c t -> (g p) c t")

            def load_next(it, group):
                sp.wait_ge(v_ps[1], 2 * it + 2)
                sp.dma_start(enc[:, :, :], one(enc_cols, group)).then_inc(ld_enc, 16)
                sp.wait_ge(cmask_ok, 2 * it + 2)
                sp.dma_start(raw_mask[:, :, :], one(mask_rows, group)).then_inc(ld_mask, 16)
                sp.wait_ge(bias_ok, N_BIAS * it + NP)
                sp.wait_ge(xc_ok, N_LN * it + NP)
                sp.dma_start(x_in[:, :, :], one(rows, group)).then_inc(ld_x, 16)

            def store(it, group):
                sp.wait_ge(out_ok, NP * it + 2 * NP)
                sp.dma_start(one(rows, group), x_out[:, :, :]).then_inc(stored, 16)
                sp.wait_ge(stored, 16 * it + 16)
                sp.sem_inc(out_free, 1)

            sp.dma_start(x_in[:, :, :], rows[0]).then_inc(ld_x, 16)
            sp.dma_start(enc[:, :, :], enc_cols[0]).then_inc(ld_enc, 16)
            sp.dma_start(raw_mask[:, :, :], mask_rows[0]).then_inc(ld_mask, 16)
            sp.sem_inc(out_free, 1)
            with sp.Fori(0, NG - 1) as it:
                load_next(it, it + 1)
                store(it, it)
            last = NG - 1
            load_next(last, 0)
            pieces = {n: (dst, src) for n, dst, src in load_layer_pieces(w, io, 1)}
            for n, used, count in (("k2", k_ps[1], 2 * NG), ("v2", v_ps[1], 2 * NG), ("qk", k_ps[0], 2 * NG),
                                   ("v", v_ps[0], 2 * NG), ("ao", o_ps, N_ATT * NG - NP), ("q2", q_ps, 4 * NG),
                                   ("co", o_ps, N_ATT * NG), ("w1", h_ps, NJ * NG)):
                sp.wait_ge(used, count)
                sp.dma_start(*pieces[n]).then_inc(ld_w[n], 16)
            sp.wait_ge(bias_ok, N_BIAS * NG)
            sp.dma_start(*pieces["rl"]).then_inc(ld_r, 16)
            sp.wait_ge(sq_ok, NJ * NG)
            sp.dma_start(*pieces["vl"]).then_inc(ld_v, 16)
            sp.wait_ge(m_ps, NG)
            sp.dma_start(*pieces["w2"]).then_inc(ld_w["w2"], 16)
            store(last, last)
            with sp.Fori(NG, TURNS - 1) as it:
                load_next(it, it - (NG - 1))
                store(it, it - NG)
            store(TURNS - 1, NG - 1)

        @block.gpsimd
        def _(pool):
            pool.wait_ge(smask_ok, 2)
            pool.wait_ge(zero_ok, 7)
            with pool.Fori(0, LAYERS) as layer, pool.Fori(0, NG) as g:
                it = layer * NG + g

                def add_bias(ln, p):
                    if ln > 0:
                        pool.wait_ge(res_ok, N_ATT * it + (ln - 1) * NP + p + 1)
                    src = x_in if ln == 0 else x_cur
                    pool.tensor_tensor(x_bias[:, p, :], src[:, p, :], row(("bao", "bco", "b2")[ln]), ALU.add).then_inc(bias_ok, 1)

                def add_mask(a, p):
                    pool.wait_ge(mul_ok, N_ATT * it + a * NP + p + 1)
                    t = sc[:, p % 3, :, :]
                    m = self_add[:, :] if a == 0 else cross_add[:, p, :]
                    pool.tensor_tensor(t, t, m.unsqueeze(1).broadcast_to([P, NH, S]), ALU.add).then_inc(add_ok, 1)

                def inv_std(ln, tiles):
                    pool.wait_ge(var_ok, N_LN * it + ln * NP + tiles.stop)
                    pool.tensor_tensor(rstd[:, tiles], var[:, tiles], minus_half[:, tiles], ALU.pow).then_inc(rstd_ok, tiles.stop - tiles.start)

                pool.wait_ge(ld_r, 16 * layer + 16)
                pool.wait_ge(ld_x, 16 * it + 16)
                inv_std(0, slice(0, NP))
                pool.wait_ge(out_free, it + 1)
                for p in range(NP):
                    add_bias(0, p)
                for a in range(2):
                    for p in range(NP):
                        add_mask(a, p)
                    for p in range(NP):
                        inv_std(a + 1, slice(p, p + 1))
                        add_bias(a + 1, p)
                for j in range(NJ):
                    pool.wait_ge(poly_ok, NJ * it + j + 1)
                    pool.tensor_tensor(poly[:, j % 2, :], poly[:, j % 2, :], pre[:, j % 2, :], ALU.mult).then_inc(arg_ok, 1)

        @block.tensor
        def _(pe):
            pe.wait_ge(ld_b, 16 * N_B_CONST)
            pe.wait_ge(zero_ok, 7)
            with pe.Fori(0, LAYERS) as layer, pe.Fori(0, NG) as g:
                it = layer * NG + g

                def weights(n):
                    pe.wait_ge(ld_w[n], 16 * layer + 16)

                def project_T(name, rhs, bank, done, first=0):
                    for c in range(NC):
                        for k in range(NC):
                            mm = pe.matmul(ps[:, bank + c, :], weight(name, k, first + c * P, first + (c + 1) * P), rhs[:, k, :],
                                           start=(k == 0), stop=(k == NC - 1))
                        mm.then_inc(done, 1)

                def project_v(name, lhs, n):
                    for b in range(GB):
                        for par in range(2):
                            for k in range(NC):
                                mm = pe.matmul(ps[par * S:(par + 1) * S, V_BANK + b // 4, (b % 4) * P:(b % 4 + 1) * P],
                                               lhs[:, k, b * S:(b + 1) * S], weight(name, k, par * P, (par + 1) * P),
                                               start=(k == 0), stop=(k == NC - 1))
                        if b % 4 == 3:
                            mm.then_inc(v_ps[n], 1)

                def norm_T(ln, bank):
                    for p in range(NP):
                        pe.wait_ge(xc_ok, N_LN * it + ln * NP + p + 1)
                        for c in range(NC):
                            mm = pe.transpose(ps[:, bank + c, p * P:(p + 1) * P], xc[:, p, c * P:(c + 1) * P], w["ident"][:, :])
                    mm.then_inc(ln_ps, 1)

                def attention(a, out_weight):
                    base = N_ATT * it + a * NP

                    def scores(p):
                        if p >= 1:
                            pe.wait_ge(mul_ok, base + p)
                        for c in range(NC):
                            for b in range(2):
                                t = slice(p * P + b * S, p * P + (b + 1) * S)
                                for r in range(4):
                                    f = slice(32 * r, 32 * r + 32)
                                    mm = pe.matmul(ps[b * S:(b + 1) * S, SC + r, c * P:(c + 1) * P], qT[f, c, t], kT[a][f, c, :, t],
                                                   start=True, stop=True)
                        mm.then_inc(sc_ps, 1)

                    def probs_T(p):
                        pe.wait_ge(exp_ok, base + p + 1)
                        for i in range(NPAIR):
                            mm = pe.transpose(ps[:, PT + i // 4, (i % 4) * P:(i % 4 + 1) * P],
                                              sc[:, p % 3, 2 * i:2 * i + 2, :].rearrange("q h k -> q (h k)"), w["ident"][:, :])
                            if i % 4 == 3:
                                mm.then_inc(pT_ps, 1)

                    def times_v(p):
                        pe.wait_ge(pT_ok, 2 * (base + p) + 2)
                        if p >= 1:
                            pe.wait_ge(tok_ok, base + p)
                        for b in range(2):
                            for i in range(NPAIR):
                                mm = pe.matmul(ps[b * S:(b + 1) * S, CX, i * VW:(i + 1) * VW], pT[:, 2 * (i % 4) + i // 4, b * S:(b + 1) * S],
                                               vP[a][:, 2 * p + b, i, :], start=True, stop=True)
                        mm.then_inc(v_sum_ps, 1)

                    def result_T(p):
                        pe.wait_ge(tok_ok, base + p + 1)
                        if p == 0:
                            pe.wait_ge(mul_ok, base + NP)
                        for c in range(NC):
                            mm = pe.transpose(ps[:, CT, D + c * P:D + (c + 1) * P], c_tok[:, p % 2, c * P:(c + 1) * P], w["ident"][:, :])
                        mm.then_inc(c_ps, 1)

                    def out_project(p):
                        pe.wait_ge(c_ok, base + p + 1)
                        if p >= 1:
                            pe.wait_ge(res_ok, base + p)
                        for k in range(NC):
                            mm = pe.matmul(ps[:, OUT, 0:D], cT[:, k, p * P:(p + 1) * P], weight(out_weight, k),
                                           start=(k == 0), stop=(k == NC - 1))
                        mm.then_inc(o_ps, 1)

                    scores(0)
                    scores(1)
                    scores(2)
                    pe.wait_ge(v_ok[a], 2 * it + 2)
                    weights(out_weight)
                    probs_T(0)
                    times_v(0)
                    scores(3)
                    for p in range(1, NP):
                        probs_T(p)
                        result_T(p - 1)
                        times_v(p)
                        out_project(p - 1)
                    result_T(NP - 1)
                    out_project(NP - 1)

                pe.wait_ge(ld_enc, 16 * it + 16)
                weights("k2")
                project_T("k2", enc, K_BANK, k_ps[1])
                weights("v2")
                project_v("v2", enc, 1)
                norm_T(0, LN1)
                pe.wait_ge(hT_ok, 6 * it + 2)
                weights("qk")
                project_T("qk", hT, Q_BANK, q_ps)
                pe.wait_ge(k_ok[1], 2 * it + 2)
                project_T("qk", hT, K_BANK, k_ps[0], first=D)
                pe.wait_ge(v_ok[1], 2 * it + 2)
                weights("v")
                project_v("v", hT, 0)
                pe.wait_ge(q_ok, 4 * it + 2)
                pe.wait_ge(k_ok[0], 2 * it + 2)
                attention(0, "ao")
                norm_T(1, LN23)
                pe.wait_ge(hT_ok, 6 * it + 4)
                weights("q2")
                project_T("q2", hT, Q_BANK, q_ps)
                pe.wait_ge(q_ok, 4 * it + 4)
                attention(1, "co")
                norm_T(2, LN23)
                pe.wait_ge(hT_ok, 6 * it + 6)
                weights("w1")
                weights("w2")

                def hidden(j):
                    if j >= 2:
                        pe.wait_ge(sq_ok, NJ * it + j - 1)
                    for k in range(NC):
                        mm = pe.matmul(ps[:, H_BANK + j % 2, :], weight("w1", k, j * P, (j + 1) * P), hT[:, k, :],
                                       start=(k == 0), stop=(k == NC - 1))
                    mm.then_inc(h_ps, 1)

                def mlp_out(j):
                    pe.wait_ge(g_ok, NJ * it + j + 1)
                    for p in range(NP):
                        mm = pe.matmul(ps[:, M_BANK + p, 0:D], act_g[:, j, p * P:(p + 1) * P], w["w2"][:, j, :],
                                       start=(j == 0), stop=(j == NJ - 1))
                    if j == NJ - 1:
                        mm.then_inc(m_ps, 1)

                hidden(0)
                hidden(1)
                for j in range(NJ):
                    if j + 2 < NJ:
                        hidden(j + 2)
                    mlp_out(j)

        @block.scalar
        def _(act):
            with act.Fori(0, LAYERS) as layer, act.Fori(0, NG) as g:
                it = layer * NG + g

                def norm_out(ln, bank):
                    act.wait_ge(ln_ps, 3 * it + ln + 1)
                    for c in range(NC):
                        act.activation(hT[:, c, :], ps[:, bank + c, :], ACT.Identity, bias=vec(f"ln{ln + 1}_b", c),
                                       scale=vec(f"ln{ln + 1}_s", c)).then_inc(hT_ok, 1)

                def queries(a):
                    for c in range(NC):
                        act.wait_ge(q_ps, 4 * it + 2 * a + c + 1)
                        act.activation(qT[:, c, :], ps[:, Q_BANK + c, :], ACT.Identity, bias=vec(("bq", "bq2")[a], c)).then_inc(q_ok, 1)

                def exps(a, p):
                    act.wait_ge(sub_ok, N_ATT * it + a * NP + p + 1)
                    t = sc[:, p % 3, :, :]
                    act.activation(t, t, ACT.Exp).then_inc(exp_ok, 1)

                def copy_pT(a, p):
                    n = N_ATT * it + a * NP + p
                    for h in range(2):
                        act.wait_ge(pT_ps, 2 * n + h + 1)
                        act.activation(pT[:, 4 * h:4 * h + 4, :].rearrange("q i t -> q (i t)"), ps[:, PT + h, :], ACT.Copy).then_inc(pT_ok, 1)

                def copy_cT(a, p):
                    act.wait_ge(c_ps, N_ATT * it + a * NP + p + 1)
                    act.activation(cT[:, :, p * P:(p + 1) * P], ps[:, CT, D:2 * D].rearrange("f (c t) -> f c t", c=NC), ACT.Copy).then_inc(c_ok, 1)

                def attention(a):
                    exps(a, 0)
                    for p in range(NP):
                        if p + 1 < NP:
                            exps(a, p + 1)
                        copy_pT(a, p)
                        if p >= 1:
                            copy_cT(a, p - 1)
                    copy_cT(a, NP - 1)

                act.wait_ge(ld_v, 16 * layer + 16)
                norm_out(0, LN1)
                queries(0)
                attention(0)
                norm_out(1, LN23)
                queries(1)
                attention(1)
                norm_out(2, LN23)

                def pre_square(j):
                    act.wait_ge(h_ps, NJ * it + j + 1)
                    if j >= 2:
                        act.wait_ge(g_ok, NJ * it + j - 1)
                    act.activation(pre[:, j % 2, :], ps[:, H_BANK + j % 2, :], ACT.Identity, bias=vec("b1", j)).then_inc(pre_ok, 1)
                    act.activation(sq[:, j % 2, :], ps[:, H_BANK + j % 2, :], ACT.Square, bias=vec("b1", j)).then_inc(sq_ok, 1)

                def tanh(j):
                    act.wait_ge(arg_ok, NJ * it + j + 1)
                    act.activation(th[:, j % 2, :], poly[:, j % 2, :], ACT.Tanh, scale=GELU_C).then_inc(th_ok, 1)

                pre_square(0)
                for j in range(NJ):
                    if j + 1 < NJ:
                        pre_square(j + 1)
                    tanh(j)

        @block.vector
        def _(dve):
            for n in range(2):
                dve.memset(vP[n][:, :, :, :], 0.0).then_inc(zero_ok, 1)
            dve.wait_ge(zero_ok, 2)
            for n in range(2):
                for par in range(2):
                    dve.memset(vP[n][par * S:(par + 1) * S, :, :, 2 * HD + par:2 * HD + par + 1], 1.0).then_inc(zero_ok, 1)
            dve.memset(minus_half[:, :], -0.5).then_inc(zero_ok, 1)
            dve.memset(inv_sum[:, :], 0.0).then_inc(out_ok, NP)
            dve.wait_ge(ld_b, 16 * N_B_CONST)
            dve.tensor_scalar(self_mul[:, :], w["self_mask"][:, :], HD ** -0.5, None, ALU.mult).then_inc(smask_ok, 1)
            dve.tensor_scalar(self_add[:, :], w["self_mask"][:, :], 10000.0, -10000.0, ALU.mult, ALU.add).then_inc(smask_ok, 1)
            dve.wait_ge(smask_ok, 2)
            with dve.Fori(0, LAYERS) as layer, dve.Fori(0, NG) as g:
                it = layer * NG + g

                def stats(ln, src, tiles):
                    n = N_LN * it + ln * NP
                    for p in tiles:
                        dve.bn_stats(bn[:, p, :], src[:, p, :]).then_inc(bn_ok, 1)
                    dve.wait_ge(bn_ok, n + tiles[-1] + 1)
                    dve.memset(gate_mark[:, :], 0.0)
                    for p in tiles:
                        dve.bn_aggr(mv[:, p, :], bn[:, p, :]).then_inc(mv_ok, 1)
                    for p in tiles:
                        dve.wait_ge(mv_ok, n + p + 1)
                        dve.tensor_scalar(var[:, p:p + 1], mv[:, p, 1:2], EPS, None, ALU.add).then_inc(var_ok, 1)

                def norm(ln, src, tiles):
                    for p in tiles:
                        dve.wait_ge(rstd_ok, N_LN * it + ln * NP + p + 1)
                        dve.tensor_scalar(xc[:, p, :], src[:, p, :], mv[:, p, 0:1], rstd[:, p:p + 1], ALU.subtract, ALU.mult).then_inc(xc_ok, 1)

                def keys(n, bias):
                    for c in range(NC):
                        dve.wait_ge(k_ps[n], 2 * it + c + 1)
                        for par in range(2):
                            op = dve.tensor_scalar(kT[n][:, c, par, :], ps[:, K_BANK + c, :], vec(bias, c), w["parity"][:, par:par + 1],
                                                   ALU.add, ALU.mult)
                        op.then_inc(k_ok[n], 1)

                def values(n, bias):
                    for q in range(2):
                        dve.wait_ge(v_ps[n], 2 * it + q + 1)
                        for par in range(2):
                            h = slice(par * S, (par + 1) * S)
                            r = row(bias)[h, par * P:(par + 1) * P]
                            op = dve.tensor_tensor(vP[n][h, 4 * q:4 * q + 4, :, par * HD:(par + 1) * HD],
                                                   ps[h, V_BANK + q, :].rearrange("k (b i d) -> k b i d", b=4, d=HD),
                                                   r.rearrange("k (i d) -> k i d", d=HD).unsqueeze(1).broadcast_to([S, 4, NPAIR, HD]),
                                                   ALU.add)
                        op.then_inc(v_ok[n], 1)

                def attention(a):
                    base = N_ATT * it + a * NP

                    def mask(p):
                        dve.wait_ge(sc_ps, base + p + 1)
                        m = self_mul[:, :] if a == 0 else cross_mul[:, p, :]
                        dve.tensor_tensor(sc[:, p % 3, :, :].rearrange("q (r h) k -> q r h k", r=4),
                                          ps[:, SC:SC + 4, 0:D].rearrange("q r (h k) -> q r h k", k=S),
                                          m.unsqueeze(1).unsqueeze(1).broadcast_to([P, 4, 4, S]), ALU.mult).then_inc(mul_ok, 1)

                    def subtract_max(p):
                        dve.wait_ge(add_ok, base + p + 1)
                        t = sc[:, p % 3, :, :]
                        dve.tensor_reduce(neg_max[:, p % 3, :], t, AX, ALU.max, negate=True).then_inc(max_ok, 1)
                        dve.wait_ge(max_ok, base + p + 1)
                        dve.tensor_tensor(t, t, neg_max[:, p % 3, :].unsqueeze(2).broadcast_to([P, NH, S]), ALU.add).then_inc(sub_ok, 1)

                    def normalize(p):
                        dve.wait_ge(v_sum_ps, base + p + 1)
                        pairs = ps[:, CX, 0:NPAIR * VW].rearrange("q (i v) -> q i v", v=VW)
                        dve.reciprocal(inv_sum[:, :].rearrange("q (i h) -> q i h", h=2), pairs[:, :, 2 * HD:VW]).then_inc(inv_ok, 1)
                        dve.wait_ge(inv_ok, base + p + 1)
                        if p >= 2:
                            dve.wait_ge(c_ps, base + p - 1)
                        dve.tensor_tensor(c_tok[:, p % 2, :].rearrange("q (i h d) -> q i h d", h=2, d=HD),
                                          pairs[:, :, 0:2 * HD].rearrange("q i (h d) -> q i h d", h=2),
                                          inv_sum[:, :].rearrange("q (i h) -> q i h", h=2).unsqueeze(3).broadcast_to([P, NPAIR, 2, HD]),
                                          ALU.mult).then_inc(tok_ok, 1)

                    def residual(p):
                        dve.wait_ge(o_ps, base + p + 1)
                        dve.wait_ge(bias_ok, N_BIAS * it + a * NP + p + 1)
                        dve.tensor_tensor(x_cur[:, p, :], ps[:, OUT, 0:D], x_bias[:, p, :], ALU.add).then_inc(res_ok, 1)
                        dve.wait_ge(res_ok, base + p + 1)
                        stats(a + 1, x_cur, [p])

                    for i in range(NP + 3):
                        if i >= 3:
                            normalize(i - 3)
                        if i < NP:
                            mask(i)
                        if 1 <= i <= NP:
                            subtract_max(i - 1)
                        if i >= 3:
                            residual(i - 3)
                        if i >= 4:
                            norm(a + 1, x_cur, [i - 4])
                    norm(a + 1, x_cur, [NP - 1])

                dve.wait_ge(ld_x, 16 * it + 16)
                stats(0, x_in, range(NP))
                norm(0, x_in, range(NP))
                dve.wait_ge(ld_v, 16 * layer + 16)
                dve.wait_ge(ld_r, 16 * layer + 16)
                keys(1, "bk2")
                values(1, "bv2")
                keys(0, "bk")
                values(0, "bv")
                dve.wait_ge(ld_mask, 16 * it + 16)
                dve.tensor_scalar(cross_mul[:, :, :], raw_mask[:, :, :], HD ** -0.5, None, ALU.mult).then_inc(cmask_ok, 1)
                dve.tensor_scalar(cross_add[:, :, :], raw_mask[:, :, :], 10000.0, -10000.0, ALU.mult, ALU.add).then_inc(cmask_ok, 1)
                dve.wait_ge(cmask_ok, 2 * it + 2)
                attention(0)
                attention(1)

                def cubic(j):
                    dve.wait_ge(sq_ok, NJ * it + j + 1)
                    dve.tensor_scalar(poly[:, j % 2, :], sq[:, j % 2, :], 0.044715, 1.0, ALU.mult, ALU.add).then_inc(poly_ok, 1)

                def gelu(j):
                    dve.wait_ge(th_ok, NJ * it + j + 1)
                    dve.scalar_tensor_tensor(act_g[:, j, :], th[:, j % 2, :], 1.0, pre[:, j % 2, :], ALU.add, ALU.mult).then_inc(g_ok, 1)

                cubic(0)
                for j in range(NJ):
                    if j + 1 < NJ:
                        cubic(j + 1)
                    gelu(j)
                dve.wait_ge(m_ps, it + 1)
                dve.wait_ge(out_free, it + 1)
                for p in range(NP):
                    dve.wait_ge(bias_ok, N_BIAS * it + 2 * NP + p + 1)
                    dve.scalar_tensor_tensor(x_out[:, p, :], ps[:, M_BANK + p, 0:D], 0.5, x_bias[:, p, :], ALU.mult, ALU.add).then_inc(out_ok, 1)


def phase_c(nc, io, ps, w, x_mid, ld_c):
    ctx = ExitStack()
    with ctx:
        def sb(name, *shape):
            return ctx.enter_context(nc.sbuf_tensor("c_" + name, [P, *shape], F32))

        def sem(name):
            return ctx.enter_context(nc.semaphore("c_" + name))

        NS = NC * RS
        ORDER = (1, 0, 2, 3, 4)
        OUTS = 11
        PROJ_DONE = (1, 5, 7, 9, 11)

        x_in, x_cur, x_out = sb("x_in", NP, D), sb("x_cur", NP, D), sb("x_out", NP, D)
        s0, prev = sb("s0", NS, GB), sb("prev", 2, NC, GB)
        bn, mv, var, rstd, xc = sb("bn", NP, 6), sb("mv", NP, 2), sb("var", NP), sb("rstd", NP), sb("xc", NP, D)
        gate_mark = sb("gate_mark", 1)
        minus_half, eps = sb("minus_half", NP), sb("eps", 1)
        xn = [sb(f"xn{n}", NC, GB, S + 1) for n in (1, 2)]
        sx, xx = sb("sx", NC, GT), sb("xx", NC, GT)
        maa = sb("maa", 2, GT)
        x5 = sb("x5", 2, NC, GT)
        dec, dexp = sb("dec", GT), sb("dexp", NC, GT)
        decay = sb("decay", NC, GB, S)
        kF, vF, rF = sb("kF", NC, GT), sb("vF", NC, GT), sb("rF", NC, GT)
        th, gg = sb("th", NC, GT), sb("gg", NC, GT)
        kv = sb("kv", NS, GB, S)
        st, rs = sb("st", 3, GT), sb("rs", 2, GT)
        ruk, att, sqr, nrm = sb("ruk", NC, GT), sb("att", NC, GT), sb("sqr", NC, GT), sb("nrm", NC, GT)
        gn_var, gn_rstd = sb("gn_var", NC, GT), sb("gn_rstd", NC, GT)
        oT = sb("oT", NC, GT)
        relu, kk, rr, ff = sb("relu", NC, GT), sb("kk", NC, GT), sb("rr", NP, D), sb("ff", 2, D)

        ld_x, ld_s, stored, out_free = sem("ld_x"), sem("ld_s"), sem("stored"), sem("out_free")
        const_ok = sem("const_ok")
        bn_ok, mv_ok, var_ok, rstd_ok, xc_ok, ln_ps, xn_ok = (sem(n) for n in ("bn_ok", "mv_ok", "var_ok", "rstd_ok", "xc_ok", "ln_ps", "xn_ok"))
        state_ok, sx_ok, xx_ok, maa_ps, maa_ok = (sem(n) for n in ("state_ok", "sx_ok", "xx_ok", "maa_ps", "maa_ok"))
        mix_ps, mix_ok, x5_ok, proj_ps = (sem(n) for n in ("mix_ps", "mix_ok", "x5_ok", "proj_ps"))
        dec_ok, dexp_ok, decay_ok, k_ok, v_ok, r_ok, th_ok, gg_ok = (sem(n) for n in ("dec_ok", "dexp_ok", "decay_ok", "k_ok", "v_ok", "r_ok", "th_ok", "gg_ok"))
        ruk_ok, ruk_ps, vb_ps, kv_ok, st_ok, rs_ok, red_ps, bonus_ok, att_ok = (sem(n) for n in ("ruk_ok", "ruk_ps", "vb_ps", "kv_ok", "st_ok", "rs_ok", "red_ps", "bonus_ok", "att_ok"))
        mean_ps, dm_ok, sqr_ok, var_ps, gvar_ok, grstd_ok, nrm_ok, gn_ok, o_ok = (sem(n) for n in ("mean_ps", "dm_ok", "sqr_ok", "var_ps", "gvar_ok", "grstd_ok", "nrm_ok", "gn_ok", "o_ok"))
        o_ps, res_ok, ff_in_ok, kk_ps, relu_ok, kk_ok, rr_ps, rr_ok, ff_ps, ff_ok, out_ok = (sem(n) for n in ("o_ps", "res_ok", "ff_in_ok", "kk_ps", "relu_ok", "kk_ok", "rr_ps", "rr_ok", "ff_ps", "ff_ok", "out_ok"))

        rows = x_mid.rearrange("(g p q) d -> g q p d", p=NP, q=P)
        out_rows = io["out"].rearrange("(g p q) d -> g q p d", p=NP, q=P)

        def weight(n, c, a=0, b=None):
            lo, hi = WC[n]
            return w["wc"][:, c, lo + a:hi if b is None else lo + b]

        def vec(n, c):
            return w["vc"][:, VC[n] + c:VC[n] + c + 1]

        def seqs(ap):
            return ap.rearrange("f (b t) -> f b t", b=GB)

        LN, MAA, MIX, PROJ, VB, RED, MEAN, VAR, OUT, KK, RR, FF = 0, 2, 4, 0, 4, 6, 1, 4, 6, 2, 4, 6
        RUK = (3, 0)
        block = ctx.enter_context(nc.Block())

        @block.sync
        def _(sp):
            def store(it):
                sp.wait_ge(out_ok, NP * it + NP)
                sp.dma_start(out_rows[bass.ds(it, 1)].rearrange("g q p d -> (g q) p d"), x_out[:, :, :]).then_inc(stored, 16)
                sp.wait_ge(stored, 16 * it + 16)
                sp.sem_inc(out_free, 1)

            def flat(ap):
                return ap.rearrange("q a b -> q (a b)") if len(ap.shape) == 3 else ap.rearrange("q a b c -> q (a b c)")

            sp.dma_start(x_in[:, :, :], rows[0]).then_inc(ld_x, 16)
            sp.dma_start(flat(s0[:, :, :]), io["s0"][0]).then_inc(ld_s, 16)
            sp.dma_start(flat(prev[:, :, :, :]), io["prev"][0]).then_inc(ld_s, 16)
            sp.sem_inc(out_free, 1)
            with sp.Fori(0, NG - 1) as it:
                sp.wait_ge(state_ok, 3 * it + 3)
                sp.dma_start(flat(s0[:, :, :]), io["s0"][bass.ds(it + 1, 1)].rearrange("g q n -> (g q) n")).then_inc(ld_s, 16)
                sp.dma_start(flat(prev[:, :, :, :]), io["prev"][bass.ds(it + 1, 1)].rearrange("g q n -> (g q) n")).then_inc(ld_s, 16)
                sp.wait_ge(res_ok, NP * it + NP)
                sp.dma_start(x_in[:, :, :], rows[bass.ds(it + 1, 1)].rearrange("g q p d -> (g q) p d")).then_inc(ld_x, 16)
                store(it)
            store(NG - 1)

        @block.gpsimd
        def _(pool):
            pool.wait_ge(const_ok, 3)
            with pool.Fori(0, NG) as it:
                def inv_std(ln, tiles):
                    pool.wait_ge(var_ok, 2 * NP * it + ln * NP + tiles.stop)
                    pool.tensor_tensor(rstd[:, tiles], var[:, tiles], minus_half[:, tiles], ALU.pow).then_inc(rstd_ok, tiles.stop - tiles.start)

                inv_std(0, slice(0, NP))
                for n in range(NMAA):
                    for c in range(NC):
                        pool.wait_ge(mix_ok, NMAA * NC * it + n * NC + c + 1)
                        t = seqs(x5[:, n % 2, c, :])
                        pool.tensor_tensor(t, t, xn[0][:, c, :, 1:S + 1], ALU.add).then_inc(x5_ok, 1)
                for n in range(NS):
                    pool.wait_ge(st_ok, NS * it + n + 1)
                    if n >= 2:
                        pool.wait_ge(red_ps, NS * it + n - 1)
                    pool.tensor_tensor(rs[:, n % 2, :], st[:, n % 3, :], rF[:, n // RS, :], ALU.mult).then_inc(rs_ok, 1)
                for p in range(NP):
                    inv_std(1, slice(p, p + 1))

        @block.tensor
        def _(pe):
            pe.wait_ge(ld_c, 16 * N_C_CONST)
            with pe.Fori(0, NG) as it:
                def norm_T(ln):
                    for p in range(NP):
                        pe.wait_ge(xc_ok, 2 * NP * it + ln * NP + p + 1)
                        for c in range(NC):
                            mm = pe.transpose(ps[:, LN + c, p * P:(p + 1) * P], xc[:, p, c * P:(c + 1) * P], w["ident"][:, :])
                    mm.then_inc(ln_ps, 1)

                def mix(n):
                    i = ORDER[n]
                    src, first = (w["maa2a"], RMAA * i) if i < 4 else (w["maa2b"], 0)
                    f = slice(first, first + RMAA)
                    for c in range(NC):
                        m = n * NC + c
                        if m >= 4:
                            pe.wait_ge(mix_ok, NMAA * NC * it + m - 3)
                        pe.matmul(ps[:, MIX + m % 4, :], src[f, c * P:(c + 1) * P], maa[f, i // 4, :], start=True, stop=True).then_inc(mix_ps, 1)

                def bank_free(m):
                    old = m - 4
                    if old < 0:
                        return
                    if old == 0:
                        pe.wait_ge(dec_ok, it + 1)
                    elif old <= 2:
                        pe.wait_ge(dexp_ok, NC * it + old)
                    else:
                        pe.wait_ge((k_ok, v_ok, r_ok)[(old - 3) // 2], NC * it + (old - 3) % 2 + 1)

                def project(n, name, m0):
                    pe.wait_ge(x5_ok, NMAA * NC * it + n * NC + NC)
                    for c in range(NC):
                        bank_free(m0 + c)
                        for k in range(NC):
                            mm = pe.matmul(ps[:, PROJ + (m0 + c) % 4, :], weight(name, k, c * P, (c + 1) * P), x5[:, n % 2, k, :],
                                           start=(k == 0), stop=(k == NC - 1))
                        mm.then_inc(proj_ps, 1)

                norm_T(0)
                pe.wait_ge(xx_ok, NC * it + NC)
                for i, (rows_, bank) in enumerate(((P, MAA), (RMAA, MAA + 1))):
                    for k in range(NC):
                        mm = pe.matmul(ps[0:rows_, bank, :], weight("maa1", k, i * P, i * P + rows_), xx[:, k, :],
                                       start=(k == 0), stop=(k == NC - 1))
                    mm.then_inc(maa_ps, 1)
                pe.wait_ge(maa_ok, 2 * it + 2)
                mix(0)
                mix(1)
                pe.wait_ge(x5_ok, NMAA * NC * it + NC)
                for k in range(NC):
                    mm = pe.matmul(ps[0:RDEC, PROJ, :], weight("dec1", k), x5[:, 0, k, :], start=(k == 0), stop=(k == NC - 1))
                mm.then_inc(proj_ps, 1)
                mix(2)
                pe.wait_ge(dec_ok, it + 1)
                for c in range(NC):
                    pe.matmul(ps[:, PROJ + 1 + c, :], w["dec2"][0:RDEC, c * P:(c + 1) * P], dec[0:RDEC, :], start=True, stop=True).then_inc(proj_ps, 1)
                project(1, "k", 3)
                mix(3)
                project(2, "v", 5)
                mix(4)
                project(3, "r", 7)
                project(4, "g", 9)

                def spread_v(n):
                    c, d = divmod(n, RS)
                    if n >= 2:
                        pe.wait_ge(kv_ok, NS * it + n - 1)
                    pe.matmul(ps[:, VB + n % 2, :], w["sel"][:, d, :], vF[:, c, :], start=True, stop=True).then_inc(vb_ps, 1)

                def sum_k(n):
                    c, d = divmod(n, RS)
                    pe.wait_ge(rs_ok, NS * it + n + 1)
                    pe.matmul(ps[:, RED + c, :], w["red"][:, d, :], rs[:, n % 2, :], start=(d == 0), stop=(d == RS - 1)).then_inc(red_ps, 1)

                pe.wait_ge(v_ok, NC * it + NC)
                pe.wait_ge(mix_ok, NMAA * NC * it + NMAA * NC)
                spread_v(0)
                spread_v(1)
                for c in range(NC):
                    pe.wait_ge(ruk_ok, NC * it + c + 1)
                    pe.matmul(ps[:, RUK[c], :], w["head_ones"][:, :], ruk[:, c, :], start=True, stop=True).then_inc(ruk_ps, 1)
                for n in range(NS):
                    if n + 2 < NS:
                        spread_v(n + 2)
                    sum_k(n)
                pe.wait_ge(gg_ok, NC * it + NC)
                for c in range(NC):
                    pe.wait_ge(att_ok, NC * it + c + 1)
                    pe.matmul(ps[:, MEAN + c, :], w["head_mean"][:, :], att[:, c, :], start=True, stop=True).then_inc(mean_ps, 1)
                for c in range(NC):
                    pe.wait_ge(sqr_ok, NC * it + c + 1)
                    pe.matmul(ps[:, VAR + c, :], w["head_mean"][:, :], sqr[:, c, :], start=True, stop=True).then_inc(var_ps, 1)
                pe.wait_ge(o_ok, NC * it + NC)
                for p in range(NP):
                    if p >= 2:
                        pe.wait_ge(res_ok, NP * it + p - 1)
                    for k in range(NC):
                        mm = pe.matmul(ps[:, OUT + p % 2, 0:D], oT[:, k, p * P:(p + 1) * P], weight("o", k), start=(k == 0), stop=(k == NC - 1))
                    mm.then_inc(o_ps, 1)
                norm_T(1)
                pe.wait_ge(ff_in_ok, 2 * NC * it + 2 * NC)
                for c in range(NC):
                    for k in range(NC):
                        mm = pe.matmul(ps[:, KK + c, :], weight("fk", k, c * P, (c + 1) * P), x5[:, 0, k, :], start=(k == 0), stop=(k == NC - 1))
                    mm.then_inc(kk_ps, 1)
                for p in range(NP):
                    if p >= 2:
                        pe.wait_ge(rr_ok, NP * it + p - 1)
                    for k in range(NC):
                        mm = pe.matmul(ps[:, RR + p % 2, 0:D], x5[:, 1, k, p * P:(p + 1) * P], weight("fr", k), start=(k == 0), stop=(k == NC - 1))
                    mm.then_inc(rr_ps, 1)
                pe.wait_ge(kk_ok, NC * it + NC)
                for p in range(NP):
                    if p >= 2:
                        pe.wait_ge(ff_ok, NP * it + p - 1)
                    for k in range(NC):
                        mm = pe.matmul(ps[:, FF + p % 2, 0:D], kk[:, k, p * P:(p + 1) * P], weight("fv", k), start=(k == 0), stop=(k == NC - 1))
                    mm.then_inc(ff_ps, 1)

        @block.scalar
        def _(act):
            act.wait_ge(ld_c, 16 * N_C_CONST)
            act.wait_ge(const_ok, 3)
            with act.Fori(0, NG) as it:
                def norm_out(ln, scale, bias):
                    act.wait_ge(ln_ps, 2 * it + ln + 1)
                    for c in range(NC):
                        act.activation(xn[ln][:, c, :, 1:S + 1], seqs(ps[:, LN + c, :]), ACT.Identity, bias=vec(bias, c), scale=vec(scale, c)).then_inc(xn_ok, 1)

                norm_out(0, "ln1_w", "ln1_b")
                act.wait_ge(ld_s, 32 * it + 32)
                act.activation(xn[0][:, :, :, 0], prev[:, 1, :, :], ACT.Copy).then_inc(state_ok, 1)
                act.activation(xn[1][:, :, :, 0], prev[:, 0, :, :], ACT.Copy).then_inc(state_ok, 1)
                act.activation(kv[:, :, :, 0], s0[:, :, :], ACT.Copy).then_inc(state_ok, 1)
                for i, rows_ in enumerate((P, RMAA)):
                    act.wait_ge(maa_ps, 2 * it + i + 1)
                    act.activation(maa[0:rows_, i, :], ps[0:rows_, MAA + i, :], ACT.Tanh).then_inc(maa_ok, 1)
                act.wait_ge(proj_ps, OUTS * it + 1)
                act.activation(dec[0:RDEC, :], ps[0:RDEC, PROJ, :], ACT.Tanh).then_inc(dec_ok, 1)
                for c in range(NC):
                    act.wait_ge(proj_ps, OUTS * it + 2 + c)
                    act.activation(dexp[:, c, :], ps[:, PROJ + 1 + c, :], ACT.Exp, bias=vec("decay", c)).then_inc(dexp_ok, 1)
                for c in range(NC):
                    act.wait_ge(dexp_ok, NC * it + c + 1)
                    act.activation(decay[:, c, :, 1:S], seqs(dexp[:, c, :])[:, :, 0:S - 1], ACT.Exp, scale=-1.0).then_inc(decay_ok, 1)
                for dst, ok, m in ((kF, k_ok, 3), (vF, v_ok, 5), (rF, r_ok, 7)):
                    for c in range(NC):
                        act.wait_ge(proj_ps, OUTS * it + m + c + 1)
                        act.activation(dst[:, c, :], ps[:, PROJ + (m + c) % 4, :], ACT.Copy).then_inc(ok, 1)
                for c in range(NC):
                    act.wait_ge(proj_ps, OUTS * it + 9 + c + 1)
                    act.activation(th[:, c, :], ps[:, PROJ + (9 + c) % 4, :], ACT.Tanh, scale=0.5).then_inc(th_ok, 1)
                for c in range(NC):
                    act.wait_ge(dm_ok, NC * it + c + 1)
                    act.activation(sqr[:, c, :], att[:, c, :], ACT.Square).then_inc(sqr_ok, 1)
                for c in range(NC):
                    act.wait_ge(var_ps, NC * it + c + 1)
                    act.activation(gn_var[:, c, :], ps[:, VAR + c, :], ACT.Ln, bias=eps[:, 0:1]).then_inc(gvar_ok, 1)
                for c in range(NC):
                    act.wait_ge(gvar_ok, NC * it + c + 1)
                    act.activation(gn_rstd[:, c, :], gn_var[:, c, :], ACT.Exp, scale=-0.5).then_inc(grstd_ok, 1)
                for c in range(NC):
                    act.wait_ge(nrm_ok, NC * it + c + 1)
                    act.activation(nrm[:, c, :], nrm[:, c, :], ACT.Identity, bias=vec("gn_b", c), scale=vec("gn_w", c)).then_inc(gn_ok, 1)
                norm_out(1, "ln2_w", "ln2_b")
                for c in range(NC):
                    act.wait_ge(kk_ps, NC * it + c + 1)
                    act.activation(relu[:, c, :], ps[:, KK + c, :], ACT.Relu).then_inc(relu_ok, 1)
                for c in range(NC):
                    act.wait_ge(relu_ok, NC * it + c + 1)
                    act.activation(kk[:, c, :], relu[:, c, :], ACT.Square).then_inc(kk_ok, 1)
                for p in range(NP):
                    act.wait_ge(rr_ps, NP * it + p + 1)
                    act.activation(rr[:, p, :], ps[:, RR + p % 2, 0:D], ACT.Tanh, scale=0.5).then_inc(rr_ok, 1)

        @block.vector
        def _(dve):
            dve.memset(minus_half[:, :], -0.5).then_inc(const_ok, 1)
            dve.memset(eps[:, :], EPS).then_inc(const_ok, 1)
            dve.memset(decay[:, :, :, 0], 0.0).then_inc(const_ok, 1)
            dve.wait_ge(const_ok, 3)
            dve.wait_ge(ld_c, 16 * N_C_CONST)
            with dve.Fori(0, NG) as it:
                def stats(ln, src, tiles):
                    n = 2 * NP * it + ln * NP
                    for p in tiles:
                        dve.bn_stats(bn[:, p, :], src[:, p, :]).then_inc(bn_ok, 1)
                    dve.wait_ge(bn_ok, n + tiles[-1] + 1)
                    dve.memset(gate_mark[:, :], 0.0)
                    for p in tiles:
                        dve.bn_aggr(mv[:, p, :], bn[:, p, :]).then_inc(mv_ok, 1)
                    for p in tiles:
                        dve.wait_ge(mv_ok, n + p + 1)
                        dve.tensor_scalar(var[:, p:p + 1], mv[:, p, 1:2], EPS, None, ALU.add).then_inc(var_ok, 1)

                def norm(ln, src, tiles):
                    for p in tiles:
                        dve.wait_ge(rstd_ok, 2 * NP * it + ln * NP + p + 1)
                        dve.tensor_scalar(xc[:, p, :], src[:, p, :], mv[:, p, 0:1], rstd[:, p:p + 1], ALU.subtract, ALU.mult).then_inc(xc_ok, 1)

                def shift(ln):
                    dve.wait_ge(xn_ok, 2 * NC * it + (ln + 1) * NC)
                    if ln == 0:
                        dve.wait_ge(state_ok, 3 * it + 2)
                    for c in range(NC):
                        dve.tensor_tensor(seqs(sx[:, c, :]), xn[ln][:, c, :, 0:S], xn[ln][:, c, :, 1:S + 1], ALU.subtract).then_inc(sx_ok, 1)

                dve.wait_ge(ld_x, 16 * it + 16)
                stats(0, x_in, range(NP))
                norm(0, x_in, range(NP))
                shift(0)
                for c in range(NC):
                    dve.wait_ge(sx_ok, 2 * NC * it + c + 1)
                    dve.scalar_tensor_tensor(seqs(xx[:, c, :]), seqs(sx[:, c, :]), vec("maa_x", c), xn[0][:, c, :, 1:S + 1], ALU.mult, ALU.add).then_inc(xx_ok, 1)
                for n in range(NMAA):
                    if n >= 2:
                        dve.wait_ge(proj_ps, OUTS * it + PROJ_DONE[n - 2])
                    for c in range(NC):
                        m = n * NC + c
                        dve.wait_ge(mix_ps, NMAA * NC * it + m + 1)
                        dve.scalar_tensor_tensor(x5[:, n % 2, c, :], ps[:, MIX + m % 4, :], vec(f"st{ORDER[n]}", c), sx[:, c, :], ALU.add, ALU.mult).then_inc(mix_ok, 1)
                for c in range(NC):
                    dve.wait_ge(r_ok, NC * it + c + 1)
                    dve.wait_ge(k_ok, NC * it + c + 1)
                    dve.scalar_tensor_tensor(ruk[:, c, :], rF[:, c, :], vec("u", c), kF[:, c, :], ALU.mult, ALU.mult).then_inc(ruk_ok, 1)

                def key_value(n):
                    dve.wait_ge(vb_ps, NS * it + n + 1)
                    dve.tensor_tensor(kv[:, n, :, 1:S], seqs(ps[:, VB + n % 2, :])[:, :, 0:S - 1], seqs(kF[:, n // RS, :])[:, :, 0:S - 1], ALU.mult).then_inc(kv_ok, 1)

                def scan(n):
                    dve.wait_ge(kv_ok, NS * it + n + 1)
                    if n >= 3:
                        dve.wait_ge(rs_ok, NS * it + n - 2)
                    dve.tensor_tensor_scan(st[:, n % 3, :], decay[:, n // RS, :, :].rearrange("f b t -> f (b t)"),
                                           kv[:, n, :, :].rearrange("f b t -> f (b t)"), 0.0, ALU.mult, ALU.add).then_inc(st_ok, 1)

                dve.wait_ge(state_ok, 3 * it + 3)
                dve.wait_ge(decay_ok, NC * it + NC)
                key_value(0)
                for n in range(NS):
                    if n + 1 < NS:
                        key_value(n + 1)
                    scan(n)
                for c in range(NC):
                    dve.wait_ge(th_ok, NC * it + c + 1)
                    dve.scalar_tensor_tensor(gg[:, c, :], th[:, c, :], 1.0, ps[:, PROJ + (9 + c) % 4, :], ALU.add, ALU.mult).then_inc(gg_ok, 1)
                for c in range(NC):
                    dve.wait_ge(ruk_ps, NC * it + c + 1)
                    dve.tensor_tensor(ruk[:, c, :], ps[:, RUK[c], :], vF[:, c, :], ALU.mult).then_inc(bonus_ok, 1)
                for c in range(NC):
                    dve.wait_ge(bonus_ok, NC * it + c + 1)
                    dve.wait_ge(red_ps, NS * it + (c + 1) * RS)
                    dve.tensor_tensor(att[:, c, :], ps[:, RED + c, :], ruk[:, c, :], ALU.add).then_inc(att_ok, 1)
                for c in range(NC):
                    dve.wait_ge(mean_ps, NC * it + c + 1)
                    dve.tensor_tensor(att[:, c, :], att[:, c, :], ps[:, MEAN + c, :], ALU.subtract).then_inc(dm_ok, 1)
                for c in range(NC):
                    dve.wait_ge(grstd_ok, NC * it + c + 1)
                    dve.tensor_tensor(nrm[:, c, :], att[:, c, :], gn_rstd[:, c, :], ALU.mult).then_inc(nrm_ok, 1)
                for c in range(NC):
                    dve.wait_ge(gn_ok, NC * it + c + 1)
                    dve.scalar_tensor_tensor(oT[:, c, :], gg[:, c, :], 0.5, nrm[:, c, :], ALU.mult, ALU.mult).then_inc(o_ok, 1)

                def residual(p):
                    dve.wait_ge(o_ps, NP * it + p + 1)
                    dve.tensor_tensor(x_cur[:, p, :], ps[:, OUT + p % 2, 0:D], x_in[:, p, :], ALU.add).then_inc(res_ok, 1)
                    dve.wait_ge(res_ok, NP * it + p + 1)
                    stats(1, x_cur, [p])

                for p in range(NP):
                    residual(p)
                    if p >= 1:
                        norm(1, x_cur, [p - 1])
                norm(1, x_cur, [NP - 1])
                shift(1)
                for i, mixer in enumerate(("fmk", "fmr")):
                    for c in range(NC):
                        dve.wait_ge(sx_ok, 2 * NC * it + NC + c + 1)
                        dve.scalar_tensor_tensor(seqs(x5[:, i, c, :]), seqs(sx[:, c, :]), vec(mixer, c), xn[1][:, c, :, 1:S + 1], ALU.mult, ALU.add).then_inc(ff_in_ok, 1)
                dve.wait_ge(out_free, it + 1)
                for p in range(NP):
                    dve.wait_ge(ff_ps, NP * it + p + 1)
                    dve.wait_ge(rr_ok, NP * it + p + 1)
                    dve.scalar_tensor_tensor(ff[:, p % 2, :], rr[:, p, :], 1.0, ps[:, FF + p % 2, 0:D], ALU.add, ALU.mult).then_inc(ff_ok, 1)
                    dve.wait_ge(ff_ok, NP * it + p + 1)
                    dve.scalar_tensor_tensor(x_out[:, p, :], ff[:, p % 2, :], 0.5, x_cur[:, p, :], ALU.mult, ALU.add).then_inc(out_ok, 1)


def kernel(**inputs):
    import numpy as np
    import concourse.bacc as bacc
    from concourse import mybir as mb
    from concourse.bass_utils import run_bass_kernel_spmd

    a = {k: np.asarray(v) for k, v in inputs.items()}
    f4 = np.float32
    eye2 = [(0, S), (S, P)]

    def block_diag(m):
        out = np.zeros((P, P), f4)
        for lo, hi in eye2:
            out[lo:hi, lo:hi] = m
        return out

    def chunks(v):
        return v.reshape(-1, P).T

    lay = {}
    lay["x"] = a["x"].reshape(T, D)
    lay["ctx"] = a["ctx_2048"].reshape(T, D)
    lay["ctxT"] = lay["ctx"].T
    lay["w0"] = np.stack([block_diag(a["L0_xattn_" + n].T) for n in ("w_qk", "w_v", "w_t")], 1)
    lay["bv0"] = np.concatenate([a["L0_xattn_b_v"]] * 2)[None, :]
    lay["bt0"] = np.concatenate([a["L0_xattn_b_t"]] * 2)[:, None]
    lay["self_mask"] = a["mask_1x1xSxS2_fc1"].reshape(S, S)
    lay["cross_mask"] = a["mask_Bx1xSxS2_ff1"].reshape(T, S)
    wl, w2, vl, rl = [], [], [], []
    for n in ("L1_xattn_", "L2_xattn_"):
        g = lambda k: a[n + k]
        def by_parity(m):
            v = m.reshape(m.shape[:-1] + (NPAIR, 2, HD))
            return np.moveaxis(v, -2, -3).reshape(m.shape)
        wl.append(np.concatenate([g("w_qkv")[:, 0:2 * D], by_parity(g("w_qkv")[:, 2 * D:]), g("w_ao"), g("w_q"),
                                  g("w_kv")[:, 0:D], by_parity(g("w_kv")[:, D:]), g("w_co"), g("w1")], 1))
        w2.append(g("w2"))
        vl.append(np.concatenate([chunks(v) for v in (g("ln1_s"), g("ln1_b"), g("ln2_s"), g("ln2_b"), g("ln3_s"), g("ln3_b"),
                                                      g("b_qkv")[0:D], g("b_qkv")[D:2 * D], g("b_q"), g("b_kv")[0:D], g("b1"))], 1))
        rl.append(np.concatenate([by_parity(g("b_qkv")[2 * D:]), g("b_ao"), by_parity(g("b_kv")[D:]), g("b_co"), g("b2")]))
    lay["wl"], lay["w2"], lay["vl"], lay["rl"] = np.stack(wl), np.stack(w2), np.stack(vl), np.stack(rl)
    c = lambda k: a["L3_xattn_" + k]
    lay["wc"] = np.concatenate([c("maa_w1"), c("decay_w1")] + [c(k).T for k in ("Wr", "Wk", "Wv", "Wg", "Wo", "ffn_Wk", "ffn_Wr", "ffn_Wv")], 1)
    lay["maa2"] = c("maa_w2").reshape(NMAA * RMAA, D)
    lay["dec2"] = c("decay_w2")
    lay["vc"] = np.concatenate([chunks(v) for v in [c("ln1_w"), c("ln1_b"), c("ln2_w"), c("ln2_b"), c("maa_x")]
                                + [c("maa_stack")[i] for i in range(NMAA)]
                                + [c("time_decay"), c("faaaa").reshape(D), c("gn_w"), c("gn_b"), c("ffn_maa_k"), c("ffn_maa_r")]], 1)
    ctx3 = a["ctx_2048"]
    s0 = ctx3[:, 2:2 + RS, :].reshape(NG, GB, NC, P, RS)
    lay["s0"] = s0.transpose(0, 3, 2, 4, 1).reshape(NG, P, NC * RS * GB)
    lay["prev"] = ctx3[:, 0:2, :].reshape(NG, GB, 2, NC, P).transpose(0, 4, 2, 3, 1).reshape(NG, P, 2 * NC * GB)
    i, j = np.arange(P)[:, None], np.arange(P)[None, :]
    lay["ident"] = (i == j)
    lay["parity"] = np.stack([(np.arange(P) // HD) % 2 == 0, (np.arange(P) // HD) % 2 == 1], 1)
    same = (i // RS) == (j // RS)
    lay["sel"] = np.stack([same & (i % RS == d) for d in range(RS)], 1)
    lay["red"] = np.stack([same & (j % RS == d) for d in range(RS)], 1)
    lay["head_ones"] = same
    lay["head_mean"] = same * f4(1 / RS)

    nc = bacc.Bacc("TRN2", target_bir_lowering=False, num_devices=1)
    arrays, io = {}, {}
    for name, v in lay.items():
        arrays["in_" + name] = np.ascontiguousarray(v, dtype=f4)
        io[name] = nc.dram_tensor("in_" + name, v.shape, mb.dt.float32, kind="ExternalInput").ap()
    io["out"] = nc.dram_tensor("out_x", (T, D), mb.dt.float32, kind="ExternalOutput").ap()
    build(nc, io)
    r = run_bass_kernel_spmd(nc, [arrays], core_ids=[0])
    return np.asarray(r.results[0]["out_x"]).reshape(B, S, D)
```

```python
from contextlib import ExitStack

import numpy as np

import concourse.bass as bass
from concourse import mybir

F32 = mybir.dt.float32
ALU = mybir.AluOpType
ACT = mybir.ActivationFunctionType
AX = mybir.AxisListType.X

P = 128
B, S, D = 32, 64, 256
T = B * S
NP = 4
GT = NP * P
GB = GT // S
NG = T // GT
NC = D // P
NH, HD = 16, 16
NPAIR = NH // 2
PF = 2 * HD
NR = P // PF
NPP = NPAIR // 2
VW = PF + 1
DFF = 1024
NJ = DFF // P
LAYERS = 2
TURNS = LAYERS * NG
EPS = 1e-5
GELU_C = 0.7978845608028654
RS = 8
NMAA, RMAA, RDEC = 5, 32, 64

SETS = {"first": 3, "middle": 3, "last": 4}


def packed(**sets):
    cols, spans, at = {}, {}, 0
    for s, parts in sets.items():
        start = at
        for n, width in parts:
            cols[n] = (at, at + width)
            at += width
        spans[s] = (start, at)
    return cols, spans, at


WL, WL_SETS, WL_COLS = packed(first=(("qk", 2 * D), ("v", D)), middle=(("ao", D), ("k2", D), ("v2", D), ("q2", D)),
                              last=(("co", D), ("w1", DFF)))
VL, VL_SETS, VL_COLS = packed(first=(("ln1_s", 2), ("ln1_b", 2), ("bq", 4), ("bk", 2)),
                              middle=(("ln2_s", 2), ("ln2_b", 2), ("bq2", 4), ("bk2", 2)),
                              last=(("ln3_s", 2), ("ln3_b", 2), ("b1", NJ)))
RL, RL_SETS, RL_COLS = packed(first=(("bv", D),), middle=(("bao", D), ("bv2", D), ("bco", D)), last=(("b2", D),))
WC = {}
_at = 0
for _n, _w in (("maa1", NMAA * RMAA), ("dec1", RDEC), ("r", D), ("k", D), ("v", D), ("g", D), ("o", D),
               ("fk", D), ("fr", D), ("fv", D)):
    WC[_n] = (_at, _at + _w)
    _at += _w
WC_COLS = _at
VC = {n: 2 * i for i, n in enumerate(("ln1_w", "ln1_b", "ln2_w", "ln2_b", "maa_x", "st0", "st1", "st2", "st3", "st4",
                                      "decay", "u", "gn_w", "gn_b", "fmk", "fmr"))}
VC_COLS = 2 * len(VC)


def build(nc, io):
    ctx = ExitStack()
    with ctx:
        def sb(name, *shape):
            return ctx.enter_context(nc.sbuf_tensor(name, [P, *shape], F32))

        ps = ctx.enter_context(nc.psum_tensor("ps", [P, 8, 512], F32))
        x_mid = nc.dram_tensor("x_mid", [T, D], F32, kind="Internal").ap()
        sem = lambda n: ctx.enter_context(nc.semaphore(n))
        ld_b, ld_c, zero_ok = sem("ld_b"), sem("ld_c"), sem("zero_ok")
        ld_set = {s: sem("ld_" + s) for s in SETS}
        sizes_b = {"self_q": (NC, GB, 2, S), "self_k": (NC, GB, NR, S), "self_v": (GB, NPP, 2 * VW)}
        sizes_c = {"wc": (NC, WC_COLS), "maa2a": (D,), "maa2b": (D,), "dec2": (D,), "vc": (VC_COLS,), "sel": (RS, P),
                   "red": (RS, P), "head_ones": (P,), "head_mean": (P,)}
        size = lambda shape: int(np.prod(shape))
        area = sb("area", max(sum(map(size, sizes_b.values())), sum(map(size, sizes_c.values()))))
        weights = {"ident": sb("ident", P)}
        for sizes in (sizes_b, sizes_c):
            at = 0
            for n, shape in sizes.items():
                dims = " ".join("abcd"[:len(shape)])
                weights[n] = area[:, at:at + size(shape)].rearrange(f"p ({dims}) -> p {dims}", **dict(zip("abcd", shape)))
                at += size(shape)
        with ExitStack() as layer_ctx:
            def sb(name, *shape):
                return layer_ctx.enter_context(nc.sbuf_tensor(name, [P, *shape], F32))
            weights |= {
                "wl": sb("wl", NC, WL_COLS), "w2": sb("w2", NJ, D), "vl": sb("vl", VL_COLS), "rl": sb("rl", RL_COLS),
                "self_mask": sb("self_mask", S), "parity": sb("parity", 2),
            }
            weights |= {"cross" + n[4:]: sb("cross" + n[4:], *shape) for n, shape in sizes_b.items()}
            phase_a(nc, io, ps, weights, x_mid, ld_b, ld_set, zero_ok)
            phase_b(nc, io, ps, weights, x_mid, ld_b, ld_c, ld_set, zero_ok)
        phase_c(nc, io, ps, weights, x_mid, ld_c)


def load_set(w, io, layer, s):
    wl, vl, rl = (slice(*spans[s]) for spans in (WL_SETS, VL_SETS, RL_SETS))
    loads = [(w["vl"][:, vl], io["vl"][layer][:, vl]),
             (w["rl"][:, rl], io["rl"][layer:layer + 1, rl].broadcast_to([P, rl.stop - rl.start])),
             (w["wl"][:, :, wl], io["wl"][layer].rearrange("(c p) n -> p c n", p=P)[:, :, wl])]
    if s == "last":
        loads.append((w["w2"][:, :, :], io["w2"][layer].rearrange("(c p) n -> p c n", p=P)))
    return loads


def load_c_weights(w, io):
    return [(w["vc"], io["vc"]), (w["wc"], io["wc"].rearrange("(c p) n -> p c n", p=P)),
            (w["maa2a"], io["maa2"][0:P, :]), (w["maa2b"][0:RMAA, :], io["maa2"][P:NMAA * RMAA, :]),
            (w["dec2"][0:RDEC, :], io["dec2"]), (w["sel"], io["sel"]), (w["red"], io["red"]),
            (w["head_ones"], io["head_ones"]), (w["head_mean"], io["head_mean"])]


N_B_CONST = 4
N_ZERO = 8
N_C_CONST = 9


def phase_a(nc, io, ps, w, x_mid, ld_b, ld_set, zero_ok):
    ctx = ExitStack()
    with ctx:
        def sb(name, *shape):
            return ctx.enter_context(nc.sbuf_tensor("a_" + name, [P, *shape], F32))

        def sem(name):
            return ctx.enter_context(nc.semaphore("a_" + name))

        TILES = NG * NP
        LEAD = 3
        OUT_CREDIT = 2

        x_in, y_in, x_keep, x_out = (sb(n, NP, D) for n in ("x_in", "y_in", "x_keep", "x_out"))
        w0, bv, bt = sb("w0", 3, P), sb("bv", P), sb("bt", 1)
        qk = sb("qk", 2, 2, D)
        att = sb("att", 2, 4, D)
        neg_max, row_sum, row_inv = sb("neg_max", NP, 4), sb("row_sum", NP, 4), sb("row_inv", NP, 4)
        xv_b, xv_n = sb("xv_b", 2, D), sb("xv_n", 2, D)
        col_inv, diff, gate = sb("col_inv", 2, D), sb("diff", 2, D), sb("gate", 2, D)

        ld_w, stored, out_free = sem("ld_w"), sem("stored"), sem("out_free")
        ld_xy = [sem(f"ld_xy{p}") for p in range(NP)]
        proj_ps, qk_ok, xv_ps, xvb_ok, xvn_ok = sem("proj_ps"), sem("qk_ok"), sem("xv_ps"), sem("xvb_ok"), sem("xvn_ok")
        en_ps, max_ok, exp_ok, inv_ok = sem("en_ps"), sem("max_ok"), sem("exp_ok"), sem("inv_ok")
        xr_ps, eps_ok, col_ok, xrn_ok, diff_ok = (sem("xr_ps"), sem("eps_ok"), sem("col_ok"), sem("xrn_ok"),
                                                  sem("diff_ok"))
        t_ps, gate_ok, keep_ok, out_ok = sem("t_ps"), sem("gate_ok"), sem("keep_ok"), sem("out_ok")

        x_rows = io["x"].rearrange("(t q) d -> t q d", q=P)
        y_rows = io["ctx"].rearrange("(t q) d -> t q d", q=P)
        o_rows = x_mid.rearrange("(t q) d -> t q d", q=P)
        EN, PROJ, TPS, XV, XR = 0, 4, 5, 6, 7

        def after(engine, semaphore, count):
            if not (isinstance(count, int) and count <= 0):
                engine.wait_ge(semaphore, count)

        def run(engine, stages):
            def step(t, p, fixed):
                for ahead, stage in stages:
                    if not fixed or 0 <= t + ahead < TILES:
                        stage(t + ahead, (p + ahead) % NP)
            for t in range(-LEAD, 0):
                step(t, t % NP, True)
            with engine.Fori(0, NG - 1) as it:
                for p in range(NP):
                    step(NP * it + p, p, False)
            for t in range(TILES - NP, TILES):
                step(t, t % NP, True)

        block = ctx.enter_context(nc.Block())

        @block.sync
        def _(sp):
            def load(t, p):
                x, y = ((x_rows[t], y_rows[t]) if isinstance(t, int) else
                        (rows[bass.ds(t, 1)].rearrange("t q d -> (t q) d") for rows in (x_rows, y_rows)))
                sp.dma_start(x_in[:, p, :], x).then_inc(ld_xy[p], 16)
                sp.dma_start(y_in[:, p, :], y).then_inc(ld_xy[p], 16)

            def reload(t, p):
                sp.wait_ge(xv_ps, t - NP + 1)
                sp.wait_ge(keep_ok, t - NP + 1)
                load(t, p)

            def store(t, p):
                after(sp, stored, 16 * t)
                sp.sem_inc(out_free, 1)
                sp.wait_ge(out_ok, OUT_CREDIT + t + 1)
                dst = o_rows[t] if isinstance(t, int) else o_rows[bass.ds(t, 1)].rearrange("t q d -> (t q) d")
                sp.dma_start(dst, x_out[:, p, :]).then_inc(stored, 16)

            sp.sem_inc(out_free, NP - 1)
            sp.dma_start(w0[:, :, :], io["w0"]).then_inc(ld_w, 16)
            for t in range(NP):
                load(t, t)
                if t == 0:
                    sp.dma_start(bv[:, :], io["bv0"].broadcast_to([P, P])).then_inc(ld_w, 16)
                    sp.dma_start(bt[:, :], io["bt0"]).then_inc(ld_w, 16)
            for s in SETS:
                for dst, src in load_set(w, io, 0, s):
                    sp.dma_start(dst, src).then_inc(ld_set[s], 16)
            with sp.Fori(0, NG - 1) as it:
                for p in range(NP):
                    reload(NP * it + NP + p, p)
                    store(NP * it + p, p)
            for t in range(TILES - NP, TILES):
                store(t, t % NP)
            sp.wait_ge(stored, 16 * TILES)

        @block.gpsimd
        def _(pool):
            pool.dma_start(w["ident"][:, :], io["ident"]).then_inc(ld_b, 16)
            pool.dma_start(w["self_mask"][0:S, :], io["self_mask"]).then_inc(ld_b, 16)
            pool.dma_start(w["self_mask"][S:P, :], io["self_mask"]).then_inc(ld_b, 16)
            pool.dma_start(w["parity"][:, :], io["parity"]).then_inc(ld_b, 16)
            pool.memset(x_out[:, :, 0:1], 0.0).then_inc(out_ok, OUT_CREDIT)
            for a in ("self", "cross"):
                pool.memset(w[a + "_k"][:, :, :, :, :], 0.0).then_inc(zero_ok, 1)
                pool.memset(w[a + "_v"][:, :, :, :], 0.0).then_inc(zero_ok, 1)
            pool.wait_ge(zero_ok, 4)
            for a in ("self", "cross"):
                for odd in range(2):
                    pool.memset(w[a + "_v"][odd * S:(odd + 1) * S, :, :, odd * VW + PF:odd * VW + VW], 1.0).then_inc(zero_ok, 1)
            pool.wait_ge(zero_ok, N_ZERO)

            def add(t, p):
                pool.wait_ge(gate_ok, t + 1)
                pool.wait_ge(out_free, t + 1)
                pool.tensor_tensor(x_out[:, p, :], x_keep[:, p, :], gate[:, p % 2, :], ALU.add).then_inc(out_ok, 1)

            run(pool, ((0, add),))

        @block.tensor
        def _(pe):
            pe.wait_ge(ld_w, 16 * 3)

            def project(t, p):
                pe.wait_ge(ld_xy[p], 32 // NP * (t - p) + 32)
                after(pe, qk_ok, t)
                pe.matmul(ps[:, PROJ, 0:D], w0[:, 0, :], y_in[:, p, :], start=True, stop=True)
                pe.matmul(ps[:, PROJ, D:2 * D], w0[:, 0, :], x_in[:, p, :], start=True, stop=True).then_inc(proj_ps, 1)
                after(pe, xvb_ok, t)
                for j in range(2):
                    mm = pe.matmul(ps[:, XV, j * P:(j + 1) * P], x_in[:, p, j * P:(j + 1) * P], w0[:, 1, :],
                                   start=True, stop=True)
                mm.then_inc(xv_ps, 1)

            def energy(t, p):
                pe.wait_ge(qk_ok, t + 1)
                after(pe, exp_ok, t - 1)
                for j in range(2):
                    for b in range(2):
                        h = slice(b * S, (b + 1) * S)
                        mm = pe.matmul(ps[:, EN + 2 * (p % 2) + b, j * D:(j + 1) * D],
                                       qk[h, p % 2, 0, j * P:(j + 1) * P], qk[h, p % 2, 1, :], start=True, stop=True)
                mm.then_inc(en_ps, 1)

            def read_out(t, p):
                pe.wait_ge(exp_ok, t + 1)
                pe.wait_ge(xvn_ok, t + 1)
                after(pe, xrn_ok, t)
                for b in range(2):
                    for j in range(2):
                        pe.matmul(ps[b * S:(b + 1) * S, XR, 0:D], xv_n[:, p % 2, (2 * b + j) * S:(2 * b + j + 1) * S],
                                  att[:, p % 2, 2 * b + j, :], start=(j == 0), stop=(j == 1))
                for b in range(2):
                    for j in range(2):
                        mm = pe.matmul(ps[b * S:(b + 1) * S, XR, D:2 * D],
                                       row_inv[:, p, 2 * b + j:2 * b + j + 1].broadcast_to([P, S]),
                                       att[:, p % 2, 2 * b + j, :], start=(j == 0), stop=(j == 1))
                mm.then_inc(xr_ps, 1)

            def mix_out(t, p):
                pe.wait_ge(diff_ok, t + 1)
                after(pe, gate_ok, t)
                pe.matmul(ps[:, TPS, 0:D], w0[:, 2, :], diff[:, p % 2, :], start=True, stop=True).then_inc(t_ps, 1)

            run(pe, ((3, project), (2, energy), (1, read_out), (0, mix_out)))

        @block.scalar
        def _(act):
            act.wait_ge(ld_w, 16 * 3)

            def copy_qk(t, p):
                act.wait_ge(proj_ps, t + 1)
                after(act, en_ps, t - 1)
                act.activation(qk[:, p % 2, :, :].rearrange("q a d -> q (a d)"), ps[:, PROJ, :], ACT.Copy).then_inc(qk_ok, 1)

            def keep(t, p):
                after(act, out_ok, OUT_CREDIT + t - NP + 1)
                act.activation(x_keep[:, p, :], x_in[:, p, :], ACT.Copy).then_inc(keep_ok, 1)

            def exps(t, p):
                act.wait_ge(max_ok, t + 1)
                after(act, xr_ps, t - 1)
                for i in range(4):
                    a = act.activation(att[:, p % 2, i, :], ps[:, EN + 2 * (p % 2) + i // 2, (i % 2) * D:(i % 2 + 1) * D],
                                       ACT.Exp, bias=neg_max[:, p, i:i + 1], accum_out=row_sum[:, p, i:i + 1])
                a.then_inc(exp_ok, 1)

            def relu(t, p):
                act.wait_ge(t_ps, t + 1)
                act.wait_ge(out_ok, OUT_CREDIT + t - 1)
                act.activation(gate[:, p % 2, :], ps[:, TPS, 0:D], ACT.Relu, bias=bt[:, 0:1]).then_inc(gate_ok, 1)

            run(act, ((3, copy_qk), (2, exps), (0, relu), (3, keep)))

        @block.vector
        def _(dve):
            dve.wait_ge(ld_w, 16 * 3)

            def row_max(t, p):
                dve.wait_ge(en_ps, t + 1)
                dve.tensor_reduce(neg_max[:, p, :],
                                  ps[:, EN + 2 * (p % 2):EN + 2 * (p % 2) + 2, :].rearrange("q e (j m) -> q (e j) m", j=2),
                                  AX, ALU.max, negate=True).then_inc(max_ok, 1)

            def values(t, p):
                dve.wait_ge(xv_ps, t + 1)
                after(dve, xvn_ok, t - 1)
                dve.tensor_tensor(xv_b[:, p % 2, :].rearrange("q (j c) -> q j c", j=2),
                                  ps[:, XV, 0:D].rearrange("q (j c) -> q j c", j=2),
                                  bv[:, :].unsqueeze(1).broadcast_to([P, 2, P]), ALU.add).then_inc(xvb_ok, 1)

            def scale_values(t, p):
                dve.wait_ge(exp_ok, t + 1)
                dve.reciprocal(row_inv[:, p, :], row_sum[:, p, :]).then_inc(inv_ok, 1)
                dve.wait_ge(inv_ok, t + 1)
                dve.wait_ge(xvb_ok, t + 1)
                after(dve, xr_ps, t - 1)
                dve.tensor_tensor(xv_n[:, p % 2, :].rearrange("q (b j c) -> q b j c", b=2, j=2),
                                  xv_b[:, p % 2, :].rearrange("q (j b c) -> q b j c", b=2, j=2),
                                  row_inv[:, p, :].rearrange("q (b j) -> q b j", b=2).unsqueeze(3).broadcast_to([P, 2, 2, S]),
                                  ALU.mult).then_inc(xvn_ok, 1)

            def difference(t, p):
                dve.wait_ge(xr_ps, t + 1)
                dve.tensor_scalar(col_inv[:, p % 2, :], ps[:, XR, D:2 * D], 1e-7, None, ALU.add).then_inc(eps_ok, 1)
                dve.wait_ge(eps_ok, t + 1)
                dve.reciprocal(col_inv[:, p % 2, :], col_inv[:, p % 2, :]).then_inc(col_ok, 1)
                dve.wait_ge(col_ok, t + 1)
                after(dve, t_ps, t - 1)
                dve.tensor_tensor(diff[:, p % 2, :], ps[:, XR, 0:D], col_inv[:, p % 2, :], ALU.mult).then_inc(xrn_ok, 1)
                dve.wait_ge(xrn_ok, t + 1)
                dve.wait_ge(keep_ok, t + 1)
                dve.tensor_tensor(diff[:, p % 2, :], x_keep[:, p, :], diff[:, p % 2, :], ALU.subtract).then_inc(diff_ok, 1)

            run(dve, ((3, values), (2, row_max), (1, difference), (2, scale_values)))


def phase_b(nc, io, ps, w, x_mid, ld_b, ld_c, ld_set, zero_ok):
    ctx = ExitStack()
    with ctx:
        def sb(name, *shape):
            return ctx.enter_context(nc.sbuf_tensor("b_" + name, [P, *shape], F32))

        def sem(name):
            return ctx.enter_context(nc.semaphore("b_" + name))

        def sems(n, name):
            return [sem(f"{name}{i + 1}") for i in range(n)]

        x_in, x_cur, x_mlp, x_out = sb("x_in", NP, D), sb("x_cur", NP, D), sb("x_mlp", NP, D), sb("x_out", NP, D)
        enc = sb("enc", NC, GT)
        raw_mask, cross_mul, cross_add = sb("raw_mask", GB, S), sb("cross_mul", GB, S), sb("cross_add", GB, S)
        self_mul, self_add = sb("self_mul", S), sb("self_add", S)
        bn, mv, var, rstd, xc = sb("bn", NP, 6), sb("mv", NP, 2), sb("var", NP), sb("rstd", NP), sb("xc", NP, D)
        minus_half, gate_mark = sb("minus_half", NP), sb("gate_mark", 1)
        hT = sb("hT", NC, GT)
        qM, kB, vP = ([w[a + n] for a in ("self", "cross")] for n in ("_q", "_k", "_v"))
        sc = sb("sc", 2, 2, NPAIR, S)
        neg_max = sb("neg_max", 2, 2 * NPAIR)
        pT = sb("pT", 2, NPP, P)
        inv_sum, c_tok = sb("inv_sum", 2, NPAIR), sb("c_tok", 2, P)
        cT = sb("cT", 2, GT)
        pre, poly = sb("pre", 4, GT), sb("poly", 4, GT)
        act_g = sb("act_g", NJ, GT)

        ld_x, ld_enc, ld_mask, stored, out_free = (sem(n) for n in ("ld_x", "ld_enc", "ld_mask", "stored", "out_free"))
        ready = {n: sem("ready_" + n) for n in SETS}
        const_ok, smask_ok, cmask_ok = sem("const_ok"), sem("smask_ok"), sem("cmask_ok")
        q_ps, q_ok, k_ps, k_ok, v_ps, v_ok = (sems(2, n) for n in ("q_ps", "q_ok", "k_ps", "k_ok", "v_ps", "v_ok"))
        bn_ok, mv_ok, var_ok, rstd_ok, xc_ok = (sems(2, n) for n in ("bn_ok", "mv_ok", "var_ok", "rstd_ok", "xc_ok"))
        ln_ps, h_ok, bias_ok = sems(3, "ln_ps"), sems(3, "h_ok"), sems(3, "bias_ok")
        sc_ps, mul_ok, add_ok, max_ok, sub_ok, exp_ok = (sem(n) for n in ("sc_ps", "mul_ok", "add_ok", "max_ok", "sub_ok", "exp_ok"))
        pT_ps, pT_ok, v_sum_ps, inv_ok, tok_ok, c_ps, c_ok = (sem(n) for n in ("pT_ps", "pT_ok", "v_sum_ps", "inv_ok", "tok_ok", "c_ps", "c_ok"))
        o_ps, res_ok = sem("o_ps"), sem("res_ok")
        hid_ps, pre_ok, sq_ok, poly_ok, arg_ok, th_ok, g_ok = (sem(n) for n in ("hid_ps", "pre_ok", "sq_ok", "poly_ok", "arg_ok", "th_ok", "g_ok"))
        m_ps, out_ok = sem("m_ps"), sem("out_ok")

        rows = x_mid.rearrange("(g p q) d -> g q p d", p=NP, q=P)
        enc_cols = io["ctxT"].rearrange("(c p) (g t) -> g p c t", p=P, g=NG)
        mask_rows = io["cross_mask"].rearrange("(g b q) k -> g q b k", b=GB, q=S)

        def weight(n, c, a=0, b=None):
            lo, hi = WL[n]
            return w["wl"][:, c, lo + a:hi if b is None else lo + b]

        def vec(n, i, f=slice(0, P)):
            return w["vl"][f, VL[n][0] + i:VL[n][0] + i + 1]

        def row(n):
            return w["rl"][:, slice(*RL[n])]

        def tile(a, n, p):
            return (2 * n + a) * NP + p

        def after(engine, semaphore, count):
            if not (isinstance(count, int) and count == 0):
                engine.wait_ge(semaphore, count)

        SC, PT, CX, YB = 0, 2, 4, 6
        CT, OUT = CX, CX + 1
        V2_BANK = (YB, SC + 1)
        block = ctx.enter_context(nc.Block())

        @block.sync
        def _(sp):
            def one(view, group):
                return view[bass.ds(group, 1)].rearrange("g p c t -> (g p) c t")

            def load_enc(n, src):
                sp.wait_ge(v_ps[1], 2 * n)
                sp.dma_start(enc[:, :, :], src).then_inc(ld_enc, 16)

            def load_mask(n, src):
                sp.wait_ge(cmask_ok, 2 * n)
                for par in range(2):
                    sp.dma_start(raw_mask[par * S:(par + 1) * S, :, :], src).then_inc(ld_mask, 16)

            def load_x(n, src):
                sp.wait_ge(res_ok, tile(0, n, 0) - NP)
                sp.dma_start(x_in[:, :, :], src).then_inc(ld_x, 16)

            def store(n, dst):
                sp.wait_ge(out_ok, NP * n + 2 * NP)
                sp.dma_start(dst, x_out[:, :, :]).then_inc(stored, 16)
                sp.wait_ge(stored, 16 * n + 16)
                sp.sem_inc(out_free, 1)

            def reload(s):
                for dst, src in load_set(w, io, 1, s):
                    sp.dma_start(dst, src).then_inc(ld_set[s], 16)

            def mark_ready(s, layer):
                sp.wait_ge(ld_set[s], 16 * SETS[s] * (layer + 1))
                sp.sem_inc(ready[s], NG)

            sp.dma_start(x_in[:, :, :], rows[0]).then_inc(ld_x, 16)
            sp.dma_start(enc[:, :, :], enc_cols[0]).then_inc(ld_enc, 16)
            for par in range(2):
                sp.dma_start(raw_mask[par * S:(par + 1) * S, :, :], mask_rows[0]).then_inc(ld_mask, 16)
            sp.sem_inc(out_free, 1)
            for s in SETS:
                mark_ready(s, 0)
            load_x(1, rows[1])
            with sp.Fori(0, NG - 2) as it:
                load_enc(it + 1, one(enc_cols, it + 1))
                load_mask(it + 1, one(mask_rows, it + 1))
                load_x(it + 2, one(rows, it + 2))
                store(it, one(rows, it))
            n = NG - 2
            load_enc(n + 1, enc_cols[n + 1])
            load_mask(n + 1, mask_rows[n + 1])
            for done, count in ((q_ok, 4), (k_ok, 2), (v_ok, 2)):
                sp.wait_ge(done[0], count * NG)
            reload("first")
            load_x(n + 2, rows[0])
            store(n, rows[n])
            mark_ready("first", 1)
            n = NG - 1
            load_enc(n + 1, enc_cols[0])
            load_mask(n + 1, mask_rows[0])
            for done, count in ((q_ok, 4), (k_ok, 2), (v_ok, 2)):
                sp.wait_ge(done[1], count * NG)
            sp.wait_ge(bias_ok[1], NP * NG)
            reload("middle")
            mark_ready("middle", 1)
            load_x(n + 2, rows[1])
            store(n, rows[n])
            reload("last")
            mark_ready("last", 1)
            with sp.Fori(NG, TURNS - 2) as it:
                load_enc(it + 1, one(enc_cols, it - (NG - 1)))
                load_mask(it + 1, one(mask_rows, it - (NG - 1)))
                load_x(it + 2, one(rows, it - (NG - 2)))
                store(it, one(rows, it - NG))
            n = TURNS - 2
            load_enc(n + 1, enc_cols[NG - 1])
            load_mask(n + 1, mask_rows[NG - 1])
            store(n, rows[NG - 2])
            sp.wait_ge(v_sum_ps, tile(1, TURNS - 1, 0))
            for dst, src in load_c_weights(w, io):
                sp.dma_start(dst, src).then_inc(ld_c, 16)
            store(TURNS - 1, rows[NG - 1])

        @block.gpsimd
        def _(pool):
            pool.wait_ge(smask_ok, 2)
            pool.wait_ge(const_ok, 1)

            def add_bias(ln, n, p):
                if ln < 2:
                    pool.wait_ge(xc_ok[ln], NP * n + p + 1 if ln == 0 else tile(0, n, p) + 1)
                    x = (x_in, x_cur)[ln]
                    pool.tensor_tensor(x[:, p, :], x[:, p, :], row(("bao", "bco")[ln]), ALU.add).then_inc(bias_ok[ln], 1)
                else:
                    pool.wait_ge(res_ok, tile(1, n, p) + 1)
                    pool.wait_ge(out_ok, NP * n + NP)
                    pool.tensor_tensor(x_mlp[:, p, :], x_cur[:, p, :], row("b2"), ALU.add).then_inc(bias_ok[ln], 1)

            def add_mask(a, n, p):
                pool.wait_ge(mul_ok, tile(a, n, p) + 1)
                t = sc[:, p % 2, :, :, :]
                if a == 0:
                    m = self_add[:, :].unsqueeze(1).broadcast_to([P, 2 * NPAIR, S])
                    t = t.rearrange("q b i k -> q (b i) k")
                else:
                    m = cross_add[:, 2 * p:2 * p + 2, :].unsqueeze(2).broadcast_to([P, 2, NPAIR, S])
                pool.tensor_tensor(t, t, m, ALU.add).then_inc(add_ok, 1)

            def inv_std(a, n, p):
                pool.wait_ge(var_ok[1], tile(a, n, p) + 1)
                pool.tensor_tensor(rstd[:, p:p + 1], var[:, p:p + 1], minus_half[:, p:p + 1], ALU.pow).then_inc(rstd_ok[1], 1)

            def inv_std_first(n):
                pool.wait_ge(var_ok[0], NP * n + NP)
                pool.tensor_tensor(rstd[:, :], var[:, :], minus_half[:, :], ALU.pow).then_inc(rstd_ok[0], NP)

            def cube(n, j):
                pool.wait_ge(poly_ok, NJ * n + j + 1)
                pool.tensor_tensor(poly[:, j % 4, :], poly[:, j % 4, :], pre[:, j % 4, :], ALU.mult).then_inc(arg_ok, 1)

            def cross(n, nxt):
                add_mask(1, n, 0)
                add_mask(1, n, 1)
                pool.wait_ge(ready["last"], n + 1)
                if nxt is not None:
                    pool.wait_ge(ready["middle"], nxt + 1)
                for p in range(NP):
                    if p >= 1:
                        inv_std(1, n, p - 1)
                    if p + 2 < NP:
                        add_mask(1, n, p + 2)
                    if p >= 1:
                        add_bias(2, n, p - 1)
                    if nxt is not None:
                        if p >= 2:
                            add_mask(0, nxt, p - 2)
                        add_bias(0, nxt, p)
                if nxt is None:
                    inv_std(1, n, NP - 1)
                    add_bias(2, n, NP - 1)
                    for j in range(NJ):
                        cube(n, j)

            def self_attention(n, last):
                if last is None:
                    add_mask(0, n, 0)
                    add_mask(0, n, 1)
                    pool.wait_ge(ready["middle"], n + 1)
                    for p in range(NP):
                        add_bias(0, n, p)
                cubes = ((), (0, 1), (2, 3, 4), (5, 6)) if last is not None else ((),) * NP
                for p in range(NP):
                    if p >= 1:
                        inv_std(0, n, p - 1)
                    elif last is not None:
                        inv_std(1, last, NP - 1)
                    if p + 2 < NP:
                        add_mask(0, n, p + 2)
                    if p == 0 and last is not None:
                        add_bias(2, last, NP - 1)
                    for j in cubes[p][:1]:
                        cube(last, j)
                    if p >= 1:
                        add_bias(1, n, p - 1)
                    for j in cubes[p][1:]:
                        cube(last, j)
                if last is not None:
                    cube(last, NJ - 1)
                inv_std(0, n, NP - 1)
                add_bias(1, n, NP - 1)

            inv_std_first(0)
            self_attention(0, None)
            with pool.Fori(0, TURNS - 1) as it:
                inv_std_first(it + 1)
                cross(it, it + 1)
                self_attention(it + 1, it)
            cross(TURNS - 1, None)

        @block.tensor
        def _(pe):
            pe.wait_ge(ld_b, 16 * N_B_CONST)
            pe.wait_ge(zero_ok, N_ZERO)

            def project_T(name, rhs, c, done, first=0, bank=YB):
                for k in range(NC):
                    mm = pe.matmul(ps[:, bank + c, :], weight(name, k, first + c * P, first + (c + 1) * P), rhs[:, k, :],
                                   start=(k == 0), stop=(k == NC - 1))
                mm.then_inc(done, 1)

            def project_v(name, lhs, half, done, bank):
                for b in range(GB // 2):
                    t = (half * GB // 2 + b) * S
                    for odd in range(2):
                        for k in range(NC):
                            mm = pe.matmul(ps[odd * S:(odd + 1) * S, bank, b * P:(b + 1) * P], lhs[:, k, t:t + S],
                                           weight(name, k, odd * P, (odd + 1) * P), start=(k == 0), stop=(k == NC - 1))
                mm.then_inc(done, 1)

            NORM_BANK = (YB, CX, YB)

            def norm_T(ln, n):
                for p in range(NP):
                    pe.wait_ge(xc_ok[min(ln, 1)], (NP * n if ln == 0 else tile(ln - 1, n, 0)) + p + 1)
                    for c in range(NC):
                        mm = pe.transpose(ps[:, NORM_BANK[ln] + c, p * P:(p + 1) * P], xc[:, p, c * P:(c + 1) * P], w["ident"][:, :])
                mm.then_inc(ln_ps[ln], 1)

            def first_norm_T(n):
                if not isinstance(n, int):
                    pe.wait_ge(out_ok, NP * n)
                after(pe, k_ok[1], 2 * n)
                after(pe, v_ok[1], 2 * n)
                norm_T(0, n)

            def queries_1(n, c):
                if c == 0:
                    pe.wait_ge(h_ok[0], 2 * n + 2)
                    pe.wait_ge(ready["first"], n + 1)
                project_T("qk", hT, c, q_ps[0])

            def keys_1(n, c):
                pe.wait_ge(q_ok[0], 4 * n + 2 * c + 2)
                project_T("qk", hT, c, k_ps[0], first=D)

            def values_1(n, half):
                pe.wait_ge(k_ok[0], 2 * n + half + 1)
                project_v("v", hT, half, v_ps[0], YB + half)

            def keys_2(n, c):
                if c == 0:
                    pe.wait_ge(ld_enc, 16 * n + 16)
                    pe.wait_ge(ready["middle"], n + 1)
                pe.wait_ge(v_ok[0], 2 * n + c + 1)
                project_T("k2", enc, c, k_ps[1])

            def values_2(n, half):
                if half == 0:
                    pe.wait_ge(k_ok[1], 2 * n + 1)
                else:
                    pe.wait_ge(mul_ok, tile(1, n, 0))
                project_v("v2", enc, half, v_ps[1], V2_BANK[half])

            def queries_2(n, c):
                pe.wait_ge(h_ok[1], 2 * n + 2)
                project_T("q2", hT, c, q_ps[1], bank=PT)

            def scores(a, n, p):
                if p == 0:
                    pe.wait_ge(q_ok[a], 4 * n + 4)
                    pe.wait_ge(k_ok[a], 2 * n + 2)
                    if a == 1:
                        pe.wait_ge(v_ok[1], 2 * n + 2)
                after(pe, mul_ok, tile(a, n, p))
                for b in range(2):
                    for c in range(NC):
                        mm = pe.matmul(ps[:, SC + b, c * D:(c + 1) * D], qM[a][:, c, 2 * p + b, :, :].rearrange("f h q -> f (h q)"),
                                       kB[a][:, c, 2 * p + b, :, :].rearrange("f r k -> f (r k)"), start=True, stop=True)
                mm.then_inc(sc_ps, 1)

            def probs_T(a, n, p):
                pe.wait_ge(exp_ok, tile(a, n, p) + 1)
                for b in range(2):
                    for i in range(NPP):
                        mm = pe.transpose(ps[:, PT + b, i * P:(i + 1) * P],
                                          sc[:, p % 2, b, 2 * i:2 * i + 2, :].rearrange("q i k -> q (i k)"), w["ident"][:, :])
                    mm.then_inc(pT_ps, 1)

            def times_v(a, n, p):
                if p == 0:
                    pe.wait_ge(v_ok[a], 2 * n + 2)
                pe.wait_ge(pT_ok, 2 * tile(a, n, p) + 2)
                after(pe, c_ok, tile(a, n, p))
                after(pe, res_ok, tile(a, n, p))
                for b in range(2):
                    for i in range(NPP):
                        mm = pe.matmul(ps[:, CX + b, i * 2 * VW:(i + 1) * 2 * VW], pT[:, b, i, :], vP[a][:, 2 * p + b, i, :],
                                       start=True, stop=True)
                mm.then_inc(v_sum_ps, 1)

            def result_T(a, n, p):
                pe.wait_ge(tok_ok, tile(a, n, p) + 1)
                for b in range(2):
                    mm = pe.transpose(ps[:, CT, b * P:(b + 1) * P], c_tok[:, b, :], w["ident"][:, :])
                mm.then_inc(c_ps, 1)

            def out_project(a, n, p):
                if p == 0:
                    pe.wait_ge(ready[("middle", "last")[a]], n + 1)
                pe.wait_ge(c_ok, tile(a, n, p) + 1)
                for par in range(2):
                    mm = pe.matmul(ps[:, OUT, 0:D], cT[:, par, p * P:(p + 1) * P], weight(("ao", "co")[a], par),
                                   start=(par == 0), stop=(par == 1))
                mm.then_inc(o_ps, 1)

            def third_norm_T(n, nxt):
                if nxt is not None:
                    pe.wait_ge(v_ok[1], 2 * nxt + 1)
                    pe.wait_ge(k_ok[1], 2 * nxt + 2)
                else:
                    pe.wait_ge(out_ok, NP * n + NP)
                norm_T(2, n)

            def hidden(n, j):
                if j < 2:
                    pe.wait_ge(h_ok[2], 2 * n + 2)
                else:
                    pe.wait_ge(sq_ok, NJ * n + j - 1)
                for k in range(NC):
                    mm = pe.matmul(ps[:, YB + j % 2, :], weight("w1", k, j * P, (j + 1) * P), hT[:, k, :],
                                   start=(k == 0), stop=(k == NC - 1))
                mm.then_inc(hid_ps, 1)

            def mlp_out(n, p):
                if p == 0:
                    pe.wait_ge(sq_ok, NJ * n + NJ - 1)
                elif p >= 2:
                    pe.wait_ge(out_ok, NP * n + NP + p - 1)
                for j in range(NJ):
                    if p == 0:
                        pe.wait_ge(g_ok, NJ * n + j + 1)
                    mm = pe.matmul(ps[:, YB + p % 2, 0:D], act_g[:, j, p * P:(p + 1) * P], w["w2"][:, j, :],
                                   start=(j == 0), stop=(j == NJ - 1))
                mm.then_inc(m_ps, 1)

            def cross(n, nxt):
                beside = nxt is not None
                if beside:
                    first_norm_T(nxt)
                scores(1, n, 0)
                if beside:
                    queries_1(nxt, 0)
                scores(1, n, 1)
                if beside:
                    queries_1(nxt, 1)
                    keys_1(nxt, 0)
                    keys_1(nxt, 1)
                for p in range(NP):
                    probs_T(1, n, p)
                    if p >= 1:
                        out_project(1, n, p - 1)
                    if p + 2 < NP:
                        scores(1, n, p + 2)
                    elif beside:
                        scores(0, nxt, p + 2 - NP)
                    times_v(1, n, p)
                    if beside:
                        (values_1, values_1, keys_2, keys_2)[p](nxt, p % 2)
                    result_T(1, n, p)
                if not beside:
                    out_project(1, n, NP - 1)
                    third_norm_T(n, None)
                    hidden(n, 0)
                    hidden(n, 1)
                    for j in range(2, NJ):
                        hidden(n, j)
                    for p in range(NP):
                        mlp_out(n, p)

            def self_attention(n, last):
                beside = last is not None
                if not beside:
                    scores(0, n, 0)
                    scores(0, n, 1)
                for p in range(NP):
                    probs_T(0, n, p)
                    if p >= 1:
                        out_project(0, n, p - 1)
                    elif beside:
                        out_project(1, last, NP - 1)
                    if beside and p == 1:
                        third_norm_T(last, n)
                    if p + 2 < NP:
                        scores(0, n, p + 2)
                    times_v(0, n, p)
                    if beside:
                        for j in ((), (0, 1, 2), (3, 4, 5, 6), (7,))[p]:
                            hidden(last, j)
                    if p % 3 == 0:
                        values_2(n, p // 3)
                    result_T(0, n, p)
                out_project(0, n, NP - 1)
                if beside:
                    mlp_out(last, 0)
                    mlp_out(last, 1)
                pe.wait_ge(res_ok, tile(0, n, NP))
                norm_T(1, n)
                if beside:
                    mlp_out(last, 2)
                    mlp_out(last, 3)
                queries_2(n, 0)
                queries_2(n, 1)

            first_norm_T(0)
            for c in range(2):
                queries_1(0, c)
            for c in range(2):
                keys_1(0, c)
            for half in range(2):
                values_1(0, half)
            for c in range(2):
                keys_2(0, c)
            self_attention(0, None)
            with pe.Fori(0, TURNS - 1) as it:
                cross(it, it + 1)
                self_attention(it + 1, it)
            cross(TURNS - 1, None)

        @block.scalar
        def _(act):
            act.wait_ge(ld_b, 16 * N_B_CONST)
            act.wait_ge(zero_ok, N_ZERO)

            def norm_out(ln, n):
                act.wait_ge(ready[("first", "middle", "last")[ln]], n + 1)
                act.wait_ge(ln_ps[ln], n + 1)
                for c in range(NC):
                    act.activation(hT[:, c, :], ps[:, (YB, CX, YB)[ln] + c, :], ACT.Identity, bias=vec(f"ln{ln + 1}_b", c),
                                   scale=vec(f"ln{ln + 1}_s", c)).then_inc(h_ok[ln], 1)

            def queries(a, n, c):
                act.wait_ge(q_ps[a], 2 * n + c + 1)
                for par in range(2):
                    act.activation(qM[a][:, c, :, par, :], ps[:, (YB, PT)[a] + c, :].rearrange("f (b q) -> f b q", q=S), ACT.Identity,
                                   bias=vec(("bq", "bq2")[a], 2 * c + par), scale=w["parity"][:, par:par + 1]).then_inc(q_ok[a], 1)

            def keys(a, n, c):
                act.wait_ge(k_ps[a], 2 * n + c + 1)
                for r in range(NR):
                    f = slice(r * PF, (r + 1) * PF)
                    op = act.activation(kB[a][f, c, :, r, :], ps[f, YB + c, :].rearrange("f (b k) -> f b k", k=S), ACT.Identity,
                                        bias=vec(("bk", "bk2")[a], c, f))
                op.then_inc(k_ok[a], 1)

            def exps(a, n, p):
                act.wait_ge(sub_ok, tile(a, n, p) + 1)
                t = sc[:, p % 2, :, :, :].rearrange("q b i k -> q (b i k)")
                act.activation(t, t, ACT.Exp).then_inc(exp_ok, 1)

            def copy_pT(a, n, p):
                for b in range(2):
                    act.wait_ge(pT_ps, 2 * tile(a, n, p) + b + 1)
                    act.activation(pT[:, b, :, :].rearrange("k i q -> k (i q)"), ps[:, PT + b, :], ACT.Copy).then_inc(pT_ok, 1)

            def copy_cT(a, n, p):
                act.wait_ge(c_ps, tile(a, n, p) + 1)
                act.activation(cT[:, :, p * P:(p + 1) * P].rearrange("f h (b q) -> f b h q", b=2),
                               ps[:, CT, 0:D].rearrange("f (b h q) -> f b h q", b=2, h=2), ACT.Copy).then_inc(c_ok, 1)

            def pre_square(n, j):
                act.wait_ge(hid_ps, NJ * n + j + 1)
                if j >= 4:
                    act.wait_ge(g_ok, NJ * n + j - 3)
                act.activation(pre[:, j % 4, :], ps[:, YB + j % 2, :], ACT.Identity, bias=vec("b1", j)).then_inc(pre_ok, 1)
                act.activation(poly[:, j % 4, :], ps[:, YB + j % 2, :], ACT.Square, bias=vec("b1", j)).then_inc(sq_ok, 1)

            def tanh(n, j):
                act.wait_ge(arg_ok, NJ * n + j + 1)
                t = poly[:, j % 4, :]
                act.activation(t, t, ACT.Tanh, scale=GELU_C).then_inc(th_ok, 1)

            def cross(n, nxt):
                beside = nxt is not None
                if beside:
                    norm_out(0, nxt)
                    queries(0, nxt, 0)
                    queries(0, nxt, 1)
                exps(1, n, 0)
                if beside:
                    keys(0, nxt, 0)
                for p in range(NP):
                    if p >= 1:
                        copy_cT(1, n, p - 1)
                    copy_pT(1, n, p)
                    if beside and p == 0:
                        keys(0, nxt, 1)
                    if p + 1 < NP:
                        exps(1, n, p + 1)
                    elif beside:
                        exps(0, nxt, 0)
                        keys(1, nxt, 0)
                if not beside:
                    copy_cT(1, n, NP - 1)
                    norm_out(2, n)
                    pre_square(n, 0)
                    for j in range(NJ):
                        if j + 1 < NJ:
                            pre_square(n, j + 1)
                        tanh(n, j)

            def self_attention(n, last):
                beside = last is not None
                if not beside:
                    exps(0, n, 0)
                for p in range(NP):
                    if p >= 1:
                        copy_cT(0, n, p - 1)
                    elif beside:
                        copy_cT(1, last, NP - 1)
                    copy_pT(0, n, p)
                    if p + 1 < NP:
                        exps(0, n, p + 1)
                    if beside:
                        if p == 0:
                            keys(1, n, 1)
                        elif p == 1:
                            norm_out(2, last)
                            pre_square(last, 0)
                            pre_square(last, 1)
                            tanh(last, 0)
                        elif p == 2:
                            pre_square(last, 2)
                            tanh(last, 1)
                            pre_square(last, 3)
                            tanh(last, 2)
                            pre_square(last, 4)
                        elif p == 3:
                            pre_square(last, 5)
                            tanh(last, 3)
                            tanh(last, 4)
                            pre_square(last, 6)
                            tanh(last, 5)
                copy_cT(0, n, NP - 1)
                if beside:
                    pre_square(last, 7)
                    tanh(last, 6)
                    tanh(last, 7)
                norm_out(1, n)
                queries(1, n, 0)
                queries(1, n, 1)

            norm_out(0, 0)
            act.wait_ge(ready["middle"], 1)
            queries(0, 0, 0)
            queries(0, 0, 1)
            for a in range(2):
                for c in range(2):
                    keys(a, 0, c)
            self_attention(0, None)
            with act.Fori(0, TURNS - 1) as it:
                cross(it, it + 1)
                self_attention(it + 1, it)
            cross(TURNS - 1, None)

        @block.vector
        def _(dve):
            dve.memset(minus_half[:, :], -0.5).then_inc(const_ok, 1)
            dve.memset(inv_sum[:, :, :], 0.0).then_inc(out_ok, NP)
            dve.wait_ge(zero_ok, N_ZERO)
            dve.wait_ge(ld_b, 16 * N_B_CONST)
            dve.tensor_scalar(self_mul[:, :], w["self_mask"][:, :], HD ** -0.5, None, ALU.mult).then_inc(smask_ok, 1)
            dve.tensor_scalar(self_add[:, :], w["self_mask"][:, :], 10000.0, -10000.0, ALU.mult, ALU.add).then_inc(smask_ok, 1)
            dve.wait_ge(smask_ok, 2)

            def stats(s, count, src, tiles):
                for p in tiles:
                    dve.bn_stats(bn[:, p, :], src[:, p, :]).then_inc(bn_ok[s], 1)
                dve.wait_ge(bn_ok[s], count + tiles[-1] + 1)
                dve.memset(gate_mark[:, :], 0.0)
                for p in tiles:
                    dve.bn_aggr(mv[:, p, :], bn[:, p, :]).then_inc(mv_ok[s], 1)
                for p in tiles:
                    dve.wait_ge(mv_ok[s], count + p + 1)
                    dve.tensor_scalar(var[:, p:p + 1], mv[:, p, 1:2], EPS, None, ALU.add).then_inc(var_ok[s], 1)

            def norm(s, count, src, p):
                dve.wait_ge(rstd_ok[s], count + p + 1)
                dve.tensor_scalar(xc[:, p, :], src[:, p, :], mv[:, p, 0:1], rstd[:, p:p + 1], ALU.subtract, ALU.mult).then_inc(xc_ok[s], 1)

            def first_norm(n):
                dve.wait_ge(ld_x, 16 * n + 16)
                stats(0, NP * n, x_in, range(NP))
                if not isinstance(n, int):
                    dve.wait_ge(ln_ps[1], n)
                for p in range(NP):
                    norm(0, NP * n, x_in, p)

            def values(a, n, half):
                dve.wait_ge(v_ps[a], 2 * n + half + 1)
                for odd in range(2):
                    h = slice(odd * S, (odd + 1) * S)
                    r = row(("bv", "bv2")[a])[h, odd * P:(odd + 1) * P]
                    op = dve.tensor_tensor(vP[a][h, 4 * half:4 * half + 4, :, odd * VW:odd * VW + PF],
                                           ps[h, (YB + half, V2_BANK[half])[a], :].rearrange("k (b i e) -> k b i e", b=4, e=PF),
                                           r.rearrange("k (i e) -> k i e", e=PF).unsqueeze(1).broadcast_to([S, 4, NPP, PF]), ALU.add)
                op.then_inc(v_ok[a], 1)

            def cross_masks(n):
                dve.wait_ge(ld_mask, 32 * n + 32)
                dve.tensor_scalar(cross_mul[:, :, :], raw_mask[:, :, :], HD ** -0.5, None, ALU.mult).then_inc(cmask_ok, 1)
                dve.tensor_scalar(cross_add[:, :, :], raw_mask[:, :, :], 10000.0, -10000.0, ALU.mult, ALU.add).then_inc(cmask_ok, 1)
                dve.wait_ge(cmask_ok, 2 * n + 2)

            def mask(a, n, p):
                dve.wait_ge(sc_ps, tile(a, n, p) + 1)
                if a == 0:
                    dve.tensor_tensor(sc[:, p % 2, :, :, :].rearrange("q b i k -> q (b i) k"),
                                      ps[:, SC:SC + 2, :].rearrange("q b (i k) -> q (b i) k", k=S),
                                      self_mul[:, :].unsqueeze(1).broadcast_to([P, 2 * NPAIR, S]), ALU.mult).then_inc(mul_ok, 1)
                else:
                    dve.tensor_tensor(sc[:, p % 2, :, :, :], ps[:, SC:SC + 2, :].rearrange("q b (i k) -> q b i k", k=S),
                                      cross_mul[:, 2 * p:2 * p + 2, :].unsqueeze(2).broadcast_to([P, 2, NPAIR, S]),
                                      ALU.mult).then_inc(mul_ok, 1)

            def subtract_max(a, n, p):
                dve.wait_ge(add_ok, tile(a, n, p) + 1)
                t = sc[:, p % 2, :, :, :].rearrange("q b i k -> q (b i) k")
                dve.tensor_reduce(neg_max[:, p % 2, :], t, AX, ALU.max, negate=True).then_inc(max_ok, 1)
                dve.wait_ge(max_ok, tile(a, n, p) + 1)
                dve.tensor_tensor(t, t, neg_max[:, p % 2, :].unsqueeze(2).broadcast_to([P, 2 * NPAIR, S]), ALU.add).then_inc(sub_ok, 1)

            def normalize(a, n, p):
                dve.wait_ge(v_sum_ps, tile(a, n, p) + 1)
                pairs = ps[:, CX:CX + 2, 0:NPAIR * VW].rearrange("q b (i v) -> q b i v", v=VW)
                dve.reciprocal(inv_sum[:, :, :], pairs[:, :, :, PF:VW].rearrange("q b i v -> q b (i v)")).then_inc(inv_ok, 1)
                dve.wait_ge(inv_ok, tile(a, n, p) + 1)
                for par in range(2):
                    h = slice(par * S, (par + 1) * S)
                    op = dve.tensor_tensor(c_tok[h, :, :].rearrange("q b (i d) -> q b i d", d=HD),
                                           pairs[h, :, :, par * HD:(par + 1) * HD],
                                           inv_sum[h, :, :].unsqueeze(3).broadcast_to([S, 2, NPAIR, HD]), ALU.mult)
                op.then_inc(tok_ok, 1)

            def residual(a, n, p):
                dve.wait_ge(o_ps, tile(a, n, p) + 1)
                dve.wait_ge(bias_ok[a], NP * n + p + 1)
                if a == 0 and not isinstance(n, int):
                    dve.wait_ge(bias_ok[2], NP * (n - 1) + p + 1)
                dve.tensor_tensor(x_cur[:, p, :], ps[:, OUT, 0:D], (x_in, x_cur)[a][:, p, :], ALU.add).then_inc(res_ok, 1)
                dve.wait_ge(res_ok, tile(a, n, p) + 1)
                stats(1, tile(a, n, 0), x_cur, [p])

            def behind(a, n, p):
                norm(1, tile(a, n, 0), x_cur, p)

            def cubic(n, j):
                dve.wait_ge(sq_ok, NJ * n + j + 1)
                t = poly[:, j % 4, :]
                dve.tensor_scalar(t, t, 0.044715, 1.0, ALU.mult, ALU.add).then_inc(poly_ok, 1)

            def gelu(n, j):
                dve.wait_ge(th_ok, NJ * n + j + 1)
                dve.scalar_tensor_tensor(act_g[:, j, :], poly[:, j % 4, :], 1.0, pre[:, j % 4, :], ALU.add, ALU.mult).then_inc(g_ok, 1)

            def result(n, p):
                if p == 0:
                    dve.wait_ge(out_free, n + 1)
                dve.wait_ge(m_ps, NP * n + p + 1)
                dve.wait_ge(bias_ok[2], NP * n + p + 1)
                dve.scalar_tensor_tensor(x_out[:, p, :], ps[:, YB + p % 2, 0:D], 0.5, x_mlp[:, p, :], ALU.mult, ALU.add).then_inc(out_ok, 1)

            def cross(n, nxt):
                beside = nxt is not None
                if beside:
                    first_norm(nxt)
                mask(1, n, 0)
                mask(1, n, 1)
                subtract_max(1, n, 0)
                subtract_max(1, n, 1)
                if beside:
                    dve.wait_ge(ready["first"], nxt + 1)
                for p in range(NP):
                    if p >= 1:
                        residual(1, n, p - 1)
                    if p + 2 < NP:
                        mask(1, n, p + 2)
                    elif beside:
                        mask(0, nxt, p + 2 - NP)
                    if beside and 1 <= p <= 2:
                        values(0, nxt, p - 1)
                    if p >= 1:
                        behind(1, n, p - 1)
                    normalize(1, n, p)
                    if p + 2 < NP:
                        subtract_max(1, n, p + 2)
                    elif beside:
                        subtract_max(0, nxt, p + 2 - NP)
                if not beside:
                    residual(1, n, NP - 1)
                    behind(1, n, NP - 1)
                    cubic(n, 0)
                    for j in range(NJ):
                        if j + 1 < NJ:
                            cubic(n, j + 1)
                        gelu(n, j)
                    for p in range(NP):
                        result(n, p)

            def self_attention(n, last):
                beside = last is not None
                if not beside:
                    mask(0, n, 0)
                    mask(0, n, 1)
                    subtract_max(0, n, 0)
                    subtract_max(0, n, 1)
                for p in range(NP):
                    if p >= 1:
                        residual(0, n, p - 1)
                    elif beside:
                        residual(1, last, NP - 1)
                    if p + 2 < NP:
                        mask(0, n, p + 2)
                    if beside and p == 2:
                        gelu(last, 0)
                        cubic(last, 2)
                    if beside and p == 3:
                        gelu(last, 3)
                        cubic(last, 5)
                    if p >= 1:
                        behind(0, n, p - 1)
                    elif beside:
                        behind(1, last, NP - 1)
                    normalize(0, n, p)
                    if p == 0:
                        cross_masks(n)
                        dve.wait_ge(ready["middle"], n + 1)
                        values(1, n, 0)
                    if p + 2 < NP:
                        subtract_max(0, n, p + 2)
                    if beside:
                        if p == 1:
                            cubic(last, 0)
                            cubic(last, 1)
                        elif p == 2:
                            cubic(last, 3)
                            gelu(last, 1)
                            gelu(last, 2)
                            cubic(last, 4)
                        elif p == 3:
                            gelu(last, 4)
                            cubic(last, 6)
                            gelu(last, 5)
                if beside:
                    cubic(last, 7)
                    gelu(last, 6)
                residual(0, n, NP - 1)
                if beside:
                    gelu(last, 7)
                behind(0, n, NP - 1)
                values(1, n, 1)
                if beside:
                    for p in range(NP):
                        result(last, p)

            dve.wait_ge(ready["first"], 1)
            first_norm(0)
            values(0, 0, 0)
            values(0, 0, 1)
            self_attention(0, None)
            with dve.Fori(0, TURNS - 1) as it:
                cross(it, it + 1)
                self_attention(it + 1, it)
            cross(TURNS - 1, None)


def phase_c(nc, io, ps, w, x_mid, ld_c):
    ctx = ExitStack()
    with ctx:
        def sb(name, *shape):
            return ctx.enter_context(nc.sbuf_tensor("c_" + name, [P, *shape], F32))

        def sem(name):
            return ctx.enter_context(nc.semaphore("c_" + name))

        NS = NC * RS
        ORDER = (1, 0, 2, 3, 4)
        OUTS = 11
        PROJ_DONE = (1, 5, 7, 9, 11)

        x_in, x_cur, x_out = sb("x_in", NP, D), sb("x_cur", NP, D), sb("x_out", NP, D)
        s0, prev = sb("s0", NS, GB), sb("prev", 2, NC, GB)
        bn, mv, var, rstd, xc = sb("bn", NP, 6), sb("mv", NP, 2), sb("var", NP), sb("rstd", NP), sb("xc", NP, D)
        gate_mark = sb("gate_mark", 1)
        minus_half, eps = sb("minus_half", NP), sb("eps", 1)
        xn = [sb(f"xn{n}", NC, GB, S + 1) for n in (1, 2)]
        sx, xx = sb("sx", NC, GT), sb("xx", NC, GT)
        maa = sb("maa", 2, GT)
        x5 = sb("x5", 2, NC, GT)
        dec, dexp = sb("dec", GT), sb("dexp", NC, GT)
        decay = sb("decay", NC, GB, S)
        kF, vF, rF = sb("kF", NC, GT), sb("vF", NC, GT), sb("rF", NC, GT)
        th, gg = sb("th", NC, GT), sb("gg", NC, GT)
        kv = sb("kv", NS, GB, S)
        st, rs = sb("st", 3, GT), sb("rs", 2, GT)
        ruk, att, sqr, nrm = sb("ruk", NC, GT), sb("att", NC, GT), sb("sqr", NC, GT), sb("nrm", NC, GT)
        gn_var, gn_rstd = sb("gn_var", NC, GT), sb("gn_rstd", NC, GT)
        oT = sb("oT", NC, GT)
        relu, kk, rr, ff = sb("relu", NC, GT), sb("kk", NC, GT), sb("rr", NP, D), sb("ff", 2, D)

        ld_x, ld_s, stored, out_free = sem("ld_x"), sem("ld_s"), sem("stored"), sem("out_free")
        const_ok = sem("const_ok")
        bn_ok, mv_ok, var_ok, rstd_ok, xc_ok, ln_ps, xn_ok = (sem(n) for n in ("bn_ok", "mv_ok", "var_ok", "rstd_ok", "xc_ok", "ln_ps", "xn_ok"))
        state_ok, sx_ok, xx_ok, maa_ps, maa_ok = (sem(n) for n in ("state_ok", "sx_ok", "xx_ok", "maa_ps", "maa_ok"))
        mix_ps, mix_ok, x5_ok, proj_ps = (sem(n) for n in ("mix_ps", "mix_ok", "x5_ok", "proj_ps"))
        dec_ok, dexp_ok, decay_ok, k_ok, v_ok, r_ok, th_ok, gg_ok = (sem(n) for n in ("dec_ok", "dexp_ok", "decay_ok", "k_ok", "v_ok", "r_ok", "th_ok", "gg_ok"))
        ruk_ok, ruk_ps, vb_ps, kv_ok, st_ok, rs_ok, red_ps, bonus_ok, att_ok = (sem(n) for n in ("ruk_ok", "ruk_ps", "vb_ps", "kv_ok", "st_ok", "rs_ok", "red_ps", "bonus_ok", "att_ok"))
        mean_ps, dm_ok, sqr_ok, var_ps, gvar_ok, grstd_ok, nrm_ok, gn_ok, o_ok = (sem(n) for n in ("mean_ps", "dm_ok", "sqr_ok", "var_ps", "gvar_ok", "grstd_ok", "nrm_ok", "gn_ok", "o_ok"))
        o_ps, res_ok, ff_in_ok, kk_ps, relu_ok, kk_ok, rr_ps, rr_ok, ff_ps, ff_ok, out_ok = (sem(n) for n in ("o_ps", "res_ok", "ff_in_ok", "kk_ps", "relu_ok", "kk_ok", "rr_ps", "rr_ok", "ff_ps", "ff_ok", "out_ok"))

        rows = x_mid.rearrange("(g p q) d -> g q p d", p=NP, q=P)
        out_rows = io["out"].rearrange("(g p q) d -> g q p d", p=NP, q=P)

        def weight(n, c, a=0, b=None):
            lo, hi = WC[n]
            return w["wc"][:, c, lo + a:hi if b is None else lo + b]

        def vec(n, c):
            return w["vc"][:, VC[n] + c:VC[n] + c + 1]

        def seqs(ap):
            return ap.rearrange("f (b t) -> f b t", b=GB)

        LN, MAA, MIX, PROJ, VB, RED, MEAN, VAR, OUT, KK, RR, FF = 0, 2, 4, 0, 4, 6, 1, 4, 6, 2, 4, 6
        RUK = (3, 0)
        block = ctx.enter_context(nc.Block())

        @block.sync
        def _(sp):
            def store(it):
                sp.wait_ge(out_ok, NP * it + NP)
                sp.dma_start(out_rows[bass.ds(it, 1)].rearrange("g q p d -> (g q) p d"), x_out[:, :, :]).then_inc(stored, 16)
                sp.wait_ge(stored, 16 * it + 16)
                sp.sem_inc(out_free, 1)

            def flat(ap):
                return ap.rearrange("q a b -> q (a b)") if len(ap.shape) == 3 else ap.rearrange("q a b c -> q (a b c)")

            sp.dma_start(x_in[:, :, :], rows[0]).then_inc(ld_x, 16)
            sp.dma_start(flat(s0[:, :, :]), io["s0"][0]).then_inc(ld_s, 16)
            sp.dma_start(flat(prev[:, :, :, :]), io["prev"][0]).then_inc(ld_s, 16)
            sp.sem_inc(out_free, 1)
            with sp.Fori(0, NG - 1) as it:
                sp.wait_ge(state_ok, 3 * it + 3)
                sp.dma_start(flat(s0[:, :, :]), io["s0"][bass.ds(it + 1, 1)].rearrange("g q n -> (g q) n")).then_inc(ld_s, 16)
                sp.dma_start(flat(prev[:, :, :, :]), io["prev"][bass.ds(it + 1, 1)].rearrange("g q n -> (g q) n")).then_inc(ld_s, 16)
                sp.wait_ge(res_ok, NP * it + NP)
                sp.dma_start(x_in[:, :, :], rows[bass.ds(it + 1, 1)].rearrange("g q p d -> (g q) p d")).then_inc(ld_x, 16)
                store(it)
            store(NG - 1)

        @block.gpsimd
        def _(pool):
            pool.wait_ge(const_ok, 3)
            with pool.Fori(0, NG) as it:
                def inv_std(ln, tiles):
                    pool.wait_ge(var_ok, 2 * NP * it + ln * NP + tiles.stop)
                    pool.tensor_tensor(rstd[:, tiles], var[:, tiles], minus_half[:, tiles], ALU.pow).then_inc(rstd_ok, tiles.stop - tiles.start)

                inv_std(0, slice(0, NP))
                for n in range(NMAA):
                    for c in range(NC):
                        pool.wait_ge(mix_ok, NMAA * NC * it + n * NC + c + 1)
                        t = seqs(x5[:, n % 2, c, :])
                        pool.tensor_tensor(t, t, xn[0][:, c, :, 1:S + 1], ALU.add).then_inc(x5_ok, 1)
                for n in range(NS):
                    pool.wait_ge(st_ok, NS * it + n + 1)
                    if n >= 2:
                        pool.wait_ge(red_ps, NS * it + n - 1)
                    pool.tensor_tensor(rs[:, n % 2, :], st[:, n % 3, :], rF[:, n // RS, :], ALU.mult).then_inc(rs_ok, 1)
                for p in range(NP):
                    inv_std(1, slice(p, p + 1))

        @block.tensor
        def _(pe):
            pe.wait_ge(ld_c, 16 * N_C_CONST)
            with pe.Fori(0, NG) as it:
                def norm_T(ln):
                    for p in range(NP):
                        pe.wait_ge(xc_ok, 2 * NP * it + ln * NP + p + 1)
                        for c in range(NC):
                            mm = pe.transpose(ps[:, LN + c, p * P:(p + 1) * P], xc[:, p, c * P:(c + 1) * P], w["ident"][:, :])
                    mm.then_inc(ln_ps, 1)

                def mix(n):
                    i = ORDER[n]
                    src, first = (w["maa2a"], RMAA * i) if i < 4 else (w["maa2b"], 0)
                    f = slice(first, first + RMAA)
                    for c in range(NC):
                        m = n * NC + c
                        if m >= 4:
                            pe.wait_ge(mix_ok, NMAA * NC * it + m - 3)
                        pe.matmul(ps[:, MIX + m % 4, :], src[f, c * P:(c + 1) * P], maa[f, i // 4, :], start=True, stop=True).then_inc(mix_ps, 1)

                def bank_free(m):
                    old = m - 4
                    if old < 0:
                        return
                    if old == 0:
                        pe.wait_ge(dec_ok, it + 1)
                    elif old <= 2:
                        pe.wait_ge(dexp_ok, NC * it + old)
                    else:
                        pe.wait_ge((k_ok, v_ok, r_ok)[(old - 3) // 2], NC * it + (old - 3) % 2 + 1)

                def project(n, name, m0):
                    pe.wait_ge(x5_ok, NMAA * NC * it + n * NC + NC)
                    for c in range(NC):
                        bank_free(m0 + c)
                        for k in range(NC):
                            mm = pe.matmul(ps[:, PROJ + (m0 + c) % 4, :], weight(name, k, c * P, (c + 1) * P), x5[:, n % 2, k, :],
                                           start=(k == 0), stop=(k == NC - 1))
                        mm.then_inc(proj_ps, 1)

                norm_T(0)
                pe.wait_ge(xx_ok, NC * it + NC)
                for i, (rows_, bank) in enumerate(((P, MAA), (RMAA, MAA + 1))):
                    for k in range(NC):
                        mm = pe.matmul(ps[0:rows_, bank, :], weight("maa1", k, i * P, i * P + rows_), xx[:, k, :],
                                       start=(k == 0), stop=(k == NC - 1))
                    mm.then_inc(maa_ps, 1)
                pe.wait_ge(maa_ok, 2 * it + 2)
                mix(0)
                mix(1)
                pe.wait_ge(x5_ok, NMAA * NC * it + NC)
                for k in range(NC):
                    mm = pe.matmul(ps[0:RDEC, PROJ, :], weight("dec1", k), x5[:, 0, k, :], start=(k == 0), stop=(k == NC - 1))
                mm.then_inc(proj_ps, 1)
                mix(2)
                pe.wait_ge(dec_ok, it + 1)
                for c in range(NC):
                    pe.matmul(ps[:, PROJ + 1 + c, :], w["dec2"][0:RDEC, c * P:(c + 1) * P], dec[0:RDEC, :], start=True, stop=True).then_inc(proj_ps, 1)
                project(1, "k", 3)
                mix(3)
                project(2, "v", 5)
                mix(4)
                project(3, "r", 7)
                project(4, "g", 9)

                def spread_v(n):
                    c, d = divmod(n, RS)
                    if n >= 2:
                        pe.wait_ge(kv_ok, NS * it + n - 1)
                    pe.matmul(ps[:, VB + n % 2, :], w["sel"][:, d, :], vF[:, c, :], start=True, stop=True).then_inc(vb_ps, 1)

                def sum_k(n):
                    c, d = divmod(n, RS)
                    pe.wait_ge(rs_ok, NS * it + n + 1)
                    pe.matmul(ps[:, RED + c, :], w["red"][:, d, :], rs[:, n % 2, :], start=(d == 0), stop=(d == RS - 1)).then_inc(red_ps, 1)

                pe.wait_ge(v_ok, NC * it + NC)
                pe.wait_ge(mix_ok, NMAA * NC * it + NMAA * NC)
                spread_v(0)
                spread_v(1)
                for c in range(NC):
                    pe.wait_ge(ruk_ok, NC * it + c + 1)
                    pe.matmul(ps[:, RUK[c], :], w["head_ones"][:, :], ruk[:, c, :], start=True, stop=True).then_inc(ruk_ps, 1)
                for n in range(NS):
                    if n + 2 < NS:
                        spread_v(n + 2)
                    sum_k(n)
                pe.wait_ge(gg_ok, NC * it + NC)
                for c in range(NC):
                    pe.wait_ge(att_ok, NC * it + c + 1)
                    pe.matmul(ps[:, MEAN + c, :], w["head_mean"][:, :], att[:, c, :], start=True, stop=True).then_inc(mean_ps, 1)
                for c in range(NC):
                    pe.wait_ge(sqr_ok, NC * it + c + 1)
                    pe.matmul(ps[:, VAR + c, :], w["head_mean"][:, :], sqr[:, c, :], start=True, stop=True).then_inc(var_ps, 1)
                pe.wait_ge(o_ok, NC * it + NC)
                for p in range(NP):
                    if p >= 2:
                        pe.wait_ge(res_ok, NP * it + p - 1)
                    for k in range(NC):
                        mm = pe.matmul(ps[:, OUT + p % 2, 0:D], oT[:, k, p * P:(p + 1) * P], weight("o", k), start=(k == 0), stop=(k == NC - 1))
                    mm.then_inc(o_ps, 1)
                norm_T(1)
                pe.wait_ge(ff_in_ok, 2 * NC * it + 2 * NC)
                for c in range(NC):
                    for k in range(NC):
                        mm = pe.matmul(ps[:, KK + c, :], weight("fk", k, c * P, (c + 1) * P), x5[:, 0, k, :], start=(k == 0), stop=(k == NC - 1))
                    mm.then_inc(kk_ps, 1)
                for p in range(NP):
                    if p >= 2:
                        pe.wait_ge(rr_ok, NP * it + p - 1)
                    for k in range(NC):
                        mm = pe.matmul(ps[:, RR + p % 2, 0:D], x5[:, 1, k, p * P:(p + 1) * P], weight("fr", k), start=(k == 0), stop=(k == NC - 1))
                    mm.then_inc(rr_ps, 1)
                pe.wait_ge(kk_ok, NC * it + NC)
                for p in range(NP):
                    if p >= 2:
                        pe.wait_ge(ff_ok, NP * it + p - 1)
                    for k in range(NC):
                        mm = pe.matmul(ps[:, FF + p % 2, 0:D], kk[:, k, p * P:(p + 1) * P], weight("fv", k), start=(k == 0), stop=(k == NC - 1))
                    mm.then_inc(ff_ps, 1)

        @block.scalar
        def _(act):
            act.wait_ge(ld_c, 16 * N_C_CONST)
            act.wait_ge(const_ok, 3)
            with act.Fori(0, NG) as it:
                def norm_out(ln, scale, bias):
                    act.wait_ge(ln_ps, 2 * it + ln + 1)
                    for c in range(NC):
                        act.activation(xn[ln][:, c, :, 1:S + 1], seqs(ps[:, LN + c, :]), ACT.Identity, bias=vec(bias, c), scale=vec(scale, c)).then_inc(xn_ok, 1)

                norm_out(0, "ln1_w", "ln1_b")
                act.wait_ge(ld_s, 32 * it + 32)
                act.activation(xn[0][:, :, :, 0], prev[:, 1, :, :], ACT.Copy).then_inc(state_ok, 1)
                act.activation(xn[1][:, :, :, 0], prev[:, 0, :, :], ACT.Copy).then_inc(state_ok, 1)
                act.activation(kv[:, :, :, 0], s0[:, :, :], ACT.Copy).then_inc(state_ok, 1)
                for i, rows_ in enumerate((P, RMAA)):
                    act.wait_ge(maa_ps, 2 * it + i + 1)
                    act.activation(maa[0:rows_, i, :], ps[0:rows_, MAA + i, :], ACT.Tanh).then_inc(maa_ok, 1)
                act.wait_ge(proj_ps, OUTS * it + 1)
                act.activation(dec[0:RDEC, :], ps[0:RDEC, PROJ, :], ACT.Tanh).then_inc(dec_ok, 1)
                for c in range(NC):
                    act.wait_ge(proj_ps, OUTS * it + 2 + c)
                    act.activation(dexp[:, c, :], ps[:, PROJ + 1 + c, :], ACT.Exp, bias=vec("decay", c)).then_inc(dexp_ok, 1)
                for c in range(NC):
                    act.wait_ge(dexp_ok, NC * it + c + 1)
                    act.activation(decay[:, c, :, 1:S], seqs(dexp[:, c, :])[:, :, 0:S - 1], ACT.Exp, scale=-1.0).then_inc(decay_ok, 1)
                for dst, ok, m in ((kF, k_ok, 3), (vF, v_ok, 5), (rF, r_ok, 7)):
                    for c in range(NC):
                        act.wait_ge(proj_ps, OUTS * it + m + c + 1)
                        act.activation(dst[:, c, :], ps[:, PROJ + (m + c) % 4, :], ACT.Copy).then_inc(ok, 1)
                for c in range(NC):
                    act.wait_ge(proj_ps, OUTS * it + 9 + c + 1)
                    act.activation(th[:, c, :], ps[:, PROJ + (9 + c) % 4, :], ACT.Tanh, scale=0.5).then_inc(th_ok, 1)
                for c in range(NC):
                    act.wait_ge(dm_ok, NC * it + c + 1)
                    act.activation(sqr[:, c, :], att[:, c, :], ACT.Square).then_inc(sqr_ok, 1)
                for c in range(NC):
                    act.wait_ge(var_ps, NC * it + c + 1)
                    act.activation(gn_var[:, c, :], ps[:, VAR + c, :], ACT.Ln, bias=eps[:, 0:1]).then_inc(gvar_ok, 1)
                for c in range(NC):
                    act.wait_ge(gvar_ok, NC * it + c + 1)
                    act.activation(gn_rstd[:, c, :], gn_var[:, c, :], ACT.Exp, scale=-0.5).then_inc(grstd_ok, 1)
                for c in range(NC):
                    act.wait_ge(nrm_ok, NC * it + c + 1)
                    act.activation(nrm[:, c, :], nrm[:, c, :], ACT.Identity, bias=vec("gn_b", c), scale=vec("gn_w", c)).then_inc(gn_ok, 1)
                norm_out(1, "ln2_w", "ln2_b")
                for c in range(NC):
                    act.wait_ge(kk_ps, NC * it + c + 1)
                    act.activation(relu[:, c, :], ps[:, KK + c, :], ACT.Relu).then_inc(relu_ok, 1)
                for c in range(NC):
                    act.wait_ge(relu_ok, NC * it + c + 1)
                    act.activation(kk[:, c, :], relu[:, c, :], ACT.Square).then_inc(kk_ok, 1)
                for p in range(NP):
                    act.wait_ge(rr_ps, NP * it + p + 1)
                    act.activation(rr[:, p, :], ps[:, RR + p % 2, 0:D], ACT.Tanh, scale=0.5).then_inc(rr_ok, 1)

        @block.vector
        def _(dve):
            dve.memset(minus_half[:, :], -0.5).then_inc(const_ok, 1)
            dve.memset(eps[:, :], EPS).then_inc(const_ok, 1)
            dve.memset(decay[:, :, :, 0], 0.0).then_inc(const_ok, 1)
            dve.wait_ge(const_ok, 3)
            dve.wait_ge(ld_c, 16 * N_C_CONST)
            with dve.Fori(0, NG) as it:
                def stats(ln, src, tiles):
                    n = 2 * NP * it + ln * NP
                    for p in tiles:
                        dve.bn_stats(bn[:, p, :], src[:, p, :]).then_inc(bn_ok, 1)
                    dve.wait_ge(bn_ok, n + tiles[-1] + 1)
                    dve.memset(gate_mark[:, :], 0.0)
                    for p in tiles:
                        dve.bn_aggr(mv[:, p, :], bn[:, p, :]).then_inc(mv_ok, 1)
                    for p in tiles:
                        dve.wait_ge(mv_ok, n + p + 1)
                        dve.tensor_scalar(var[:, p:p + 1], mv[:, p, 1:2], EPS, None, ALU.add).then_inc(var_ok, 1)

                def norm(ln, src, tiles):
                    for p in tiles:
                        dve.wait_ge(rstd_ok, 2 * NP * it + ln * NP + p + 1)
                        dve.tensor_scalar(xc[:, p, :], src[:, p, :], mv[:, p, 0:1], rstd[:, p:p + 1], ALU.subtract, ALU.mult).then_inc(xc_ok, 1)

                def shift(ln):
                    dve.wait_ge(xn_ok, 2 * NC * it + (ln + 1) * NC)
                    if ln == 0:
                        dve.wait_ge(state_ok, 3 * it + 2)
                    for c in range(NC):
                        dve.tensor_tensor(seqs(sx[:, c, :]), xn[ln][:, c, :, 0:S], xn[ln][:, c, :, 1:S + 1], ALU.subtract).then_inc(sx_ok, 1)

                dve.wait_ge(ld_x, 16 * it + 16)
                stats(0, x_in, range(NP))
                norm(0, x_in, range(NP))
                shift(0)
                for c in range(NC):
                    dve.wait_ge(sx_ok, 2 * NC * it + c + 1)
                    dve.scalar_tensor_tensor(seqs(xx[:, c, :]), seqs(sx[:, c, :]), vec("maa_x", c), xn[0][:, c, :, 1:S + 1], ALU.mult, ALU.add).then_inc(xx_ok, 1)
                for n in range(NMAA):
                    if n >= 2:
                        dve.wait_ge(proj_ps, OUTS * it + PROJ_DONE[n - 2])
                    for c in range(NC):
                        m = n * NC + c
                        dve.wait_ge(mix_ps, NMAA * NC * it + m + 1)
                        dve.scalar_tensor_tensor(x5[:, n % 2, c, :], ps[:, MIX + m % 4, :], vec(f"st{ORDER[n]}", c), sx[:, c, :], ALU.add, ALU.mult).then_inc(mix_ok, 1)
                for c in range(NC):
                    dve.wait_ge(r_ok, NC * it + c + 1)
                    dve.wait_ge(k_ok, NC * it + c + 1)
                    dve.scalar_tensor_tensor(ruk[:, c, :], rF[:, c, :], vec("u", c), kF[:, c, :], ALU.mult, ALU.mult).then_inc(ruk_ok, 1)

                def key_value(n):
                    dve.wait_ge(vb_ps, NS * it + n + 1)
                    dve.tensor_tensor(kv[:, n, :, 1:S], seqs(ps[:, VB + n % 2, :])[:, :, 0:S - 1], seqs(kF[:, n // RS, :])[:, :, 0:S - 1], ALU.mult).then_inc(kv_ok, 1)

                def scan(n):
                    dve.wait_ge(kv_ok, NS * it + n + 1)
                    if n >= 3:
                        dve.wait_ge(rs_ok, NS * it + n - 2)
                    dve.tensor_tensor_scan(st[:, n % 3, :], decay[:, n // RS, :, :].rearrange("f b t -> f (b t)"),
                                           kv[:, n, :, :].rearrange("f b t -> f (b t)"), 0.0, ALU.mult, ALU.add).then_inc(st_ok, 1)

                dve.wait_ge(state_ok, 3 * it + 3)
                dve.wait_ge(decay_ok, NC * it + NC)
                key_value(0)
                for n in range(NS):
                    if n + 1 < NS:
                        key_value(n + 1)
                    scan(n)
                for c in range(NC):
                    dve.wait_ge(th_ok, NC * it + c + 1)
                    dve.scalar_tensor_tensor(gg[:, c, :], th[:, c, :], 1.0, ps[:, PROJ + (9 + c) % 4, :], ALU.add, ALU.mult).then_inc(gg_ok, 1)
                for c in range(NC):
                    dve.wait_ge(ruk_ps, NC * it + c + 1)
                    dve.tensor_tensor(ruk[:, c, :], ps[:, RUK[c], :], vF[:, c, :], ALU.mult).then_inc(bonus_ok, 1)
                for c in range(NC):
                    dve.wait_ge(bonus_ok, NC * it + c + 1)
                    dve.wait_ge(red_ps, NS * it + (c + 1) * RS)
                    dve.tensor_tensor(att[:, c, :], ps[:, RED + c, :], ruk[:, c, :], ALU.add).then_inc(att_ok, 1)
                for c in range(NC):
                    dve.wait_ge(mean_ps, NC * it + c + 1)
                    dve.tensor_tensor(att[:, c, :], att[:, c, :], ps[:, MEAN + c, :], ALU.subtract).then_inc(dm_ok, 1)
                for c in range(NC):
                    dve.wait_ge(grstd_ok, NC * it + c + 1)
                    dve.tensor_tensor(nrm[:, c, :], att[:, c, :], gn_rstd[:, c, :], ALU.mult).then_inc(nrm_ok, 1)
                for c in range(NC):
                    dve.wait_ge(gn_ok, NC * it + c + 1)
                    dve.scalar_tensor_tensor(oT[:, c, :], gg[:, c, :], 0.5, nrm[:, c, :], ALU.mult, ALU.mult).then_inc(o_ok, 1)

                def residual(p):
                    dve.wait_ge(o_ps, NP * it + p + 1)
                    dve.tensor_tensor(x_cur[:, p, :], ps[:, OUT + p % 2, 0:D], x_in[:, p, :], ALU.add).then_inc(res_ok, 1)
                    dve.wait_ge(res_ok, NP * it + p + 1)
                    stats(1, x_cur, [p])

                for p in range(NP):
                    residual(p)
                    if p >= 1:
                        norm(1, x_cur, [p - 1])
                norm(1, x_cur, [NP - 1])
                shift(1)
                for i, mixer in enumerate(("fmk", "fmr")):
                    for c in range(NC):
                        dve.wait_ge(sx_ok, 2 * NC * it + NC + c + 1)
                        dve.scalar_tensor_tensor(seqs(x5[:, i, c, :]), seqs(sx[:, c, :]), vec(mixer, c), xn[1][:, c, :, 1:S + 1], ALU.mult, ALU.add).then_inc(ff_in_ok, 1)
                dve.wait_ge(out_free, it + 1)
                for p in range(NP):
                    dve.wait_ge(ff_ps, NP * it + p + 1)
                    dve.wait_ge(rr_ok, NP * it + p + 1)
                    dve.scalar_tensor_tensor(ff[:, p % 2, :], rr[:, p, :], 1.0, ps[:, FF + p % 2, 0:D], ALU.add, ALU.mult).then_inc(ff_ok, 1)
                    dve.wait_ge(ff_ok, NP * it + p + 1)
                    dve.scalar_tensor_tensor(x_out[:, p, :], ff[:, p % 2, :], 0.5, x_cur[:, p, :], ALU.mult, ALU.add).then_inc(out_ok, 1)


def kernel(**inputs):
    import numpy as np
    import concourse.bacc as bacc
    from concourse import mybir as mb
    from concourse.bass_utils import run_bass_kernel_spmd

    a = {k: np.asarray(v) for k, v in inputs.items()}
    f4 = np.float32
    eye2 = [(0, S), (S, P)]

    def block_diag(m):
        out = np.zeros((P, P), f4)
        for lo, hi in eye2:
            out[lo:hi, lo:hi] = m
        return out

    def chunks(v):
        return v.reshape(-1, P).T

    lay = {}
    lay["x"] = a["x"].reshape(T, D)
    lay["ctx"] = a["ctx_2048"].reshape(T, D)
    lay["ctxT"] = lay["ctx"].T
    lay["w0"] = np.stack([block_diag(a["L0_xattn_" + n].T) for n in ("w_qk", "w_v", "w_t")], 1)
    lay["bv0"] = np.concatenate([a["L0_xattn_b_v"]] * 2)[None, :]
    lay["bt0"] = np.concatenate([a["L0_xattn_b_t"]] * 2)[:, None]
    lay["self_mask"] = a["mask_1x1xSxS2_fc1"].reshape(S, S)
    lay["cross_mask"] = a["mask_Bx1xSxS2_ff1"].reshape(T, S)
    even_head = (np.arange(P) // HD) % 2 == 0

    def by(width, m):
        v = m.reshape(m.shape[:-1] + (-1, 2, width))
        return np.moveaxis(v, -2, -3).reshape(m.shape)

    def head_chunks(v):
        out = np.zeros((P, 2 * NC), f4)
        for c in range(NC):
            for par, rows in enumerate((even_head, ~even_head)):
                out[rows, 2 * c + par] = chunks(v)[rows, c]
        return out

    wl, w2, vl, rl = [], [], [], []
    for n in ("L1_xattn_", "L2_xattn_"):
        g = lambda k: a[n + k]
        wl.append(np.concatenate([g("w_qkv")[:, 0:2 * D], by(PF, g("w_qkv")[:, 2 * D:]), by(HD, g("w_ao").T).T, g("w_kv")[:, 0:D],
                                  by(PF, g("w_kv")[:, D:]), g("w_q"), by(HD, g("w_co").T).T, g("w1")], 1))
        w2.append(g("w2"))
        vl.append(np.concatenate([chunks(g("ln1_s")), chunks(g("ln1_b")), head_chunks(g("b_qkv")[0:D]), chunks(g("b_qkv")[D:2 * D]),
                                  chunks(g("ln2_s")), chunks(g("ln2_b")), head_chunks(g("b_q")), chunks(g("b_kv")[0:D]),
                                  chunks(g("ln3_s")), chunks(g("ln3_b")), chunks(g("b1"))], 1))
        rl.append(np.concatenate([by(PF, g("b_qkv")[2 * D:]), g("b_ao"), by(PF, g("b_kv")[D:]), g("b_co"), g("b2")]))
    lay["wl"], lay["w2"], lay["vl"], lay["rl"] = np.stack(wl), np.stack(w2), np.stack(vl), np.stack(rl)
    c = lambda k: a["L3_xattn_" + k]
    lay["wc"] = np.concatenate([c("maa_w1"), c("decay_w1")] + [c(k).T for k in ("Wr", "Wk", "Wv", "Wg", "Wo", "ffn_Wk", "ffn_Wr", "ffn_Wv")], 1)
    lay["maa2"] = c("maa_w2").reshape(NMAA * RMAA, D)
    lay["dec2"] = c("decay_w2")
    lay["vc"] = np.concatenate([chunks(v) for v in [c("ln1_w"), c("ln1_b"), c("ln2_w"), c("ln2_b"), c("maa_x")]
                                + [c("maa_stack")[i] for i in range(NMAA)]
                                + [c("time_decay"), c("faaaa").reshape(D), c("gn_w"), c("gn_b"), c("ffn_maa_k"), c("ffn_maa_r")]], 1)
    ctx3 = a["ctx_2048"]
    s0 = ctx3[:, 2:2 + RS, :].reshape(NG, GB, NC, P, RS)
    lay["s0"] = s0.transpose(0, 3, 2, 4, 1).reshape(NG, P, NC * RS * GB)
    lay["prev"] = ctx3[:, 0:2, :].reshape(NG, GB, 2, NC, P).transpose(0, 4, 2, 3, 1).reshape(NG, P, 2 * NC * GB)
    i, j = np.arange(P)[:, None], np.arange(P)[None, :]
    lay["ident"] = (i == j)
    lay["parity"] = np.stack([even_head, ~even_head], 1)
    same = (i // RS) == (j // RS)
    lay["sel"] = np.stack([same & (i % RS == d) for d in range(RS)], 1)
    lay["red"] = np.stack([same & (j % RS == d) for d in range(RS)], 1)
    lay["head_ones"] = same
    lay["head_mean"] = same * f4(1 / RS)

    nc = bacc.Bacc("TRN2", target_bir_lowering=False, num_devices=1)
    arrays, io = {}, {}
    for name, v in lay.items():
        arrays["in_" + name] = np.ascontiguousarray(v, dtype=f4)
        io[name] = nc.dram_tensor("in_" + name, v.shape, mb.dt.float32, kind="ExternalInput").ap()
    io["out"] = nc.dram_tensor("out_x", (T, D), mb.dt.float32, kind="ExternalOutput").ap()
    build(nc, io)
    r = run_bass_kernel_spmd(nc, [arrays], core_ids=[0])
    return np.asarray(r.results[0]["out_x"]).reshape(B, S, D)
```

```python
from contextlib import ExitStack

import numpy as np

import concourse.bass as bass
from concourse import mybir

F32 = mybir.dt.float32
ALU = mybir.AluOpType
ACT = mybir.ActivationFunctionType
AX = mybir.AxisListType.X

P = 128
B, S, D = 32, 64, 256
T = B * S
NP = 4
GT = NP * P
GB = GT // S
NG = T // GT
NC = D // P
NH, HD = 16, 16
NPAIR = NH // 2
PF = 2 * HD
NR = P // PF
NPP = NPAIR // 2
VW = PF + 1
DFF = 1024
NJ = DFF // P
LAYERS = 2
TURNS = LAYERS * NG
EPS = 1e-5
GELU_C = 0.7978845608028654
RS = 8
HC = P // RS
Q = 2 * HC
NMAA, RMAA, RDEC = 5, 32, 64

SETS = {"first": 3, "middle": 3, "last": 4}


def packed(**sets):
    cols, spans, at = {}, {}, 0
    for s, parts in sets.items():
        start = at
        for n, width in parts:
            cols[n] = (at, at + width)
            at += width
        spans[s] = (start, at)
    return cols, spans, at


WL, WL_SETS, WL_COLS = packed(first=(("qk", 2 * D), ("v", D)), middle=(("ao", D), ("k2", D), ("v2", D), ("q2", D)),
                              last=(("co", D), ("w1", DFF)))
VL, VL_SETS, VL_COLS = packed(first=(("ln1_s", 2), ("ln1_b", 2), ("bq", 4), ("bk", 2)),
                              middle=(("ln2_s", 2), ("ln2_b", 2), ("bq2", 4), ("bk2", 2)),
                              last=(("ln3_s", 2), ("ln3_b", 2), ("b1", NJ)))
RL, RL_SETS, RL_COLS = packed(first=(("bv", D),), middle=(("bao", D), ("bv2", D), ("bco", D)), last=(("b2", D),))
WC = {}
_at = 0
for _n, _w in (("maa1", NMAA * RMAA), ("dec1", RDEC), ("r", D), ("k", D), ("v", D), ("g", D), ("o", D),
               ("fk", D), ("fr", D), ("fv", D)):
    WC[_n] = (_at, _at + _w)
    _at += _w
WC_COLS = _at
VC = {n: 2 * i for i, n in enumerate(("ln1_w", "ln1_b", "ln2_w", "ln2_b", "maa_x", "st0", "st1", "st2", "st3", "st4",
                                      "decay", "u", "gn_w", "gn_b", "fmk", "fmr"))}
VC_COLS = 2 * len(VC)


def build(nc, io):
    ctx = ExitStack()
    with ctx:
        def sb(name, *shape):
            return ctx.enter_context(nc.sbuf_tensor(name, [P, *shape], F32))

        ps = ctx.enter_context(nc.psum_tensor("ps", [P, 8, 512], F32))
        x_mid = nc.dram_tensor("x_mid", [T, D], F32, kind="Internal").ap()
        sem = lambda n: ctx.enter_context(nc.semaphore(n))
        ld_b, ld_c, zero_ok = sem("ld_b"), sem("ld_c"), sem("zero_ok")
        ld_set = {s: sem("ld_" + s) for s in SETS}
        a_stored, b_stored = sem("a_stored"), sem("b_stored")
        b_loads = {n: sem("b_ld_" + n) for n in ("x", "enc", "mask")}
        c_loads = {n: sem("c_ld_" + n) for n in ("x", "s")}
        sizes_b = {"self_q": (NC, GB, 2, S), "self_k": (NC, GB, NR, S), "self_v": (GB, NPP, 2 * VW)}
        sizes_c = {"wc": (NC, WC_COLS), "maa2a": (D,), "maa2b": (D,), "dec2": (D,), "vc": (VC_COLS,), "sel": (RS, P),
                   "red": (2, Q), "head_ones": (P,), "head_mean": (P,),
                   "c_x_in": (NP, D), "s0": (NC * RS, GB), "prev": (2, NC, GB)}
        size = lambda shape: int(np.prod(shape))
        area = sb("area", max(sum(map(size, sizes_b.values())), sum(map(size, sizes_c.values()))))
        weights = {"ident": sb("ident", P), "b_x_out": sb("b_x_out", NP, D)}
        for sizes in (sizes_b, sizes_c):
            at = 0
            for n, shape in sizes.items():
                dims = " ".join("abcd"[:len(shape)])
                weights[n] = area[:, at:at + size(shape)].rearrange(f"p ({dims}) -> p {dims}", **dict(zip("abcd", shape)))
                at += size(shape)
        with ExitStack() as layer_ctx:
            def sb(name, *shape):
                return layer_ctx.enter_context(nc.sbuf_tensor(name, [P, *shape], F32))
            weights |= {
                "wl": sb("wl", NC, WL_COLS), "w2": sb("w2", NJ, D), "vl": sb("vl", VL_COLS), "rl": sb("rl", RL_COLS),
                "self_mask": sb("self_mask", S), "parity": sb("parity", 2),
                "b_x_in": sb("b_x_in", NP, D), "enc": sb("enc", NC, GT), "raw_mask": sb("raw_mask", GB, S),
            }
            weights |= {"cross" + n[4:]: sb("cross" + n[4:], *shape) for n, shape in sizes_b.items()}
            phase_a(nc, io, ps, weights, x_mid, ld_b, ld_set, zero_ok, a_stored, b_loads)
            phase_b(nc, io, ps, weights, x_mid, ld_b, ld_c, ld_set, zero_ok, a_stored, b_loads, b_stored, c_loads)
        phase_c(nc, io, ps, weights, x_mid, ld_c, b_stored, c_loads)


def load_set(w, io, layer, s):
    wl, vl, rl = (slice(*spans[s]) for spans in (WL_SETS, VL_SETS, RL_SETS))
    loads = [(w["vl"][:, vl], io["vl"][layer][:, vl]),
             (w["rl"][:, rl], io["rl"][layer:layer + 1, rl].broadcast_to([P, rl.stop - rl.start])),
             (w["wl"][:, :, wl], io["wl"][layer].rearrange("(c p) n -> p c n", p=P)[:, :, wl])]
    if s == "last":
        loads.append((w["w2"][:, :, :], io["w2"][layer].rearrange("(c p) n -> p c n", p=P)))
    return loads


def group_rows(x):
    return x.rearrange("(g p q) d -> g q p d", p=NP, q=P)


def load_first_b(w, io, x_mid, loads):
    masks = io["cross_mask"].rearrange("(g b q) k -> g q b k", b=GB, q=S)
    return [(w["b_x_in"][:, :, :], group_rows(x_mid)[0], loads["x"]),
            (w["enc"][:, :, :], io["ctxT"].rearrange("(c p) (g t) -> g p c t", p=P, g=NG)[0], loads["enc"]),
            (w["raw_mask"][0:S, :, :], masks[0], loads["mask"]), (w["raw_mask"][S:P, :, :], masks[0], loads["mask"])]


def flat(ap):
    return ap.rearrange("q a b -> q (a b)") if len(ap.shape) == 3 else ap.rearrange("q a b c -> q (a b c)")


def load_first_c(w, io, x_mid, loads):
    return [(w["c_x_in"], group_rows(x_mid)[0], loads["x"]),
            (flat(w["s0"]), io["s0"][0], loads["s"]), (flat(w["prev"]), io["prev"][0], loads["s"])]


def load_c_weights(w, io):
    return [(w["vc"], io["vc"]), (w["wc"], io["wc"].rearrange("(c p) n -> p c n", p=P)),
            (w["maa2a"], io["maa2"][0:P, :]), (w["maa2b"][0:RMAA, :], io["maa2"][P:NMAA * RMAA, :]),
            (w["dec2"][0:RDEC, :], io["dec2"]), (w["sel"], io["sel"]), (w["red"], io["red"]),
            (w["head_ones"], io["head_ones"]), (w["head_mean"], io["head_mean"])]


N_B_CONST = 4
N_ZERO = 8
N_C_CONST = 9


def phase_a(nc, io, ps, w, x_mid, ld_b, ld_set, zero_ok, stored, b_loads):
    ctx = ExitStack()
    with ctx:
        def sb(name, *shape):
            return ctx.enter_context(nc.sbuf_tensor("a_" + name, [P, *shape], F32))

        def sem(name):
            return ctx.enter_context(nc.semaphore("a_" + name))

        TILES = NG * NP
        LEAD = 3
        OUT_CREDIT = 2

        x_in, y_in, x_keep, x_out = (sb(n, NP, D) for n in ("x_in", "y_in", "x_keep", "x_out"))
        w0, bv, bt = sb("w0", 3, P), sb("bv", P), sb("bt", 1)
        qk = sb("qk", 2, 2, D)
        att = sb("att", 2, 4, D)
        neg_max, row_sum, row_inv = sb("neg_max", NP, 4), sb("row_sum", NP, 4), sb("row_inv", NP, 4)
        xv_b, xv_n = sb("xv_b", 2, D), sb("xv_n", 2, D)
        col_inv, diff, gate = sb("col_inv", 2, D), sb("diff", 2, D), sb("gate", 2, D)

        ld_w, out_free = sem("ld_w"), sem("out_free")
        ld_xy = [sem(f"ld_xy{p}") for p in range(NP)]
        proj_ps, qk_ok, xv_ps, xvb_ok, xvn_ok = sem("proj_ps"), sem("qk_ok"), sem("xv_ps"), sem("xvb_ok"), sem("xvn_ok")
        en_ps, max_ok, exp_ok, inv_ok = sem("en_ps"), sem("max_ok"), sem("exp_ok"), sem("inv_ok")
        xr_ps, col_ok, xrn_ok, diff_ok = sem("xr_ps"), sem("col_ok"), sem("xrn_ok"), sem("diff_ok")
        t_ps, gate_ok, keep_ok, out_ok = sem("t_ps"), sem("gate_ok"), sem("keep_ok"), sem("out_ok")

        x_rows = io["x"].rearrange("(t q) d -> t q d", q=P)
        y_rows = io["ctx"].rearrange("(t q) d -> t q d", q=P)
        o_rows = x_mid.rearrange("(t q) d -> t q d", q=P)
        EN, PROJ, TPS, XV, XR = 0, 4, 5, 6, 7

        def after(engine, semaphore, count):
            if not (isinstance(count, int) and count <= 0):
                engine.wait_ge(semaphore, count)

        def run(engine, stages):
            def step(t, p, fixed):
                for ahead, stage in stages:
                    if not fixed or 0 <= t + ahead < TILES:
                        stage(t + ahead, (p + ahead) % NP)
            for t in range(-LEAD, 0):
                step(t, t % NP, True)
            with engine.Fori(0, NG - 1) as it:
                for p in range(NP):
                    step(NP * it + p, p, False)
            for t in range(TILES - NP, TILES):
                step(t, t % NP, True)

        block = ctx.enter_context(nc.Block())

        @block.sync
        def _(sp):
            def load(t, p):
                x, y = ((x_rows[t], y_rows[t]) if isinstance(t, int) else
                        (rows[bass.ds(t, 1)].rearrange("t q d -> (t q) d") for rows in (x_rows, y_rows)))
                sp.dma_start(x_in[:, p, :], x).then_inc(ld_xy[p], 16)
                sp.dma_start(y_in[:, p, :], y).then_inc(ld_xy[p], 16)

            def reload(t, p):
                sp.wait_ge(xv_ps, t - NP + 1)
                sp.wait_ge(keep_ok, t - NP + 1)
                load(t, p)

            def store(t, p):
                after(sp, stored, 16 * t)
                sp.sem_inc(out_free, 1)
                sp.wait_ge(out_ok, OUT_CREDIT + t + 1)
                dst = o_rows[t] if isinstance(t, int) else o_rows[bass.ds(t, 1)].rearrange("t q d -> (t q) d")
                sp.dma_start(dst, x_out[:, p, :]).then_inc(stored, 16)

            sp.sem_inc(out_free, NP - 1)
            sp.dma_start(w0[:, :, :], io["w0"]).then_inc(ld_w, 16)
            for t in range(NP):
                load(t, t)
                if t == 0:
                    sp.dma_start(bv[:, :], io["bv0"].broadcast_to([P, P])).then_inc(ld_w, 16)
                    sp.dma_start(bt[:, :], io["bt0"]).then_inc(ld_w, 16)
            for s in SETS:
                for dst, src in load_set(w, io, 0, s):
                    sp.dma_start(dst, src).then_inc(ld_set[s], 16)
            with sp.Fori(0, NG - 1) as it:
                for p in range(NP):
                    reload(NP * it + NP + p, p)
                for p in range(NP):
                    store(NP * it + p, p)
            sp.wait_ge(stored, 16 * NP)
            for dst, src, done in load_first_b(w, io, x_mid, b_loads):
                sp.dma_start(dst, src).then_inc(done, 16)
            for t in range(TILES - NP, TILES):
                store(t, t % NP)

        @block.gpsimd
        def _(pool):
            pool.dma_start(w["ident"][:, :], io["ident"]).then_inc(ld_b, 16)
            pool.dma_start(w["self_mask"][0:S, :], io["self_mask"]).then_inc(ld_b, 16)
            pool.dma_start(w["self_mask"][S:P, :], io["self_mask"]).then_inc(ld_b, 16)
            pool.dma_start(w["parity"][:, :], io["parity"]).then_inc(ld_b, 16)
            pool.memset(x_out[:, :, 0:1], 0.0).then_inc(out_ok, OUT_CREDIT)
            for a in ("self", "cross"):
                pool.memset(w[a + "_k"][:, :, :, :, :], 0.0).then_inc(zero_ok, 1)
                pool.memset(w[a + "_v"][:, :, :, :], 0.0).then_inc(zero_ok, 1)
            pool.wait_ge(zero_ok, 4)
            for a in ("self", "cross"):
                for odd in range(2):
                    pool.memset(w[a + "_v"][odd * S:(odd + 1) * S, :, :, odd * VW + PF:odd * VW + VW], 1.0).then_inc(zero_ok, 1)
            pool.wait_ge(zero_ok, N_ZERO)

            def add(t, p):
                pool.wait_ge(gate_ok, t + 1)
                pool.wait_ge(out_free, t + 1)
                pool.tensor_tensor(x_out[:, p, :], x_keep[:, p, :], gate[:, p % 2, :], ALU.add).then_inc(out_ok, 1)

            run(pool, ((0, add),))

        @block.tensor
        def _(pe):
            pe.wait_ge(ld_w, 16 * 3)

            def project(t, p):
                pe.wait_ge(ld_xy[p], 32 // NP * (t - p) + 32)
                after(pe, qk_ok, t)
                pe.matmul(ps[:, PROJ, 0:D], w0[:, 0, :], y_in[:, p, :], start=True, stop=True)
                pe.matmul(ps[:, PROJ, D:2 * D], w0[:, 0, :], x_in[:, p, :], start=True, stop=True).then_inc(proj_ps, 1)
                after(pe, xvb_ok, t)
                for j in range(2):
                    mm = pe.matmul(ps[:, XV, j * P:(j + 1) * P], x_in[:, p, j * P:(j + 1) * P], w0[:, 1, :],
                                   start=True, stop=True)
                mm.then_inc(xv_ps, 1)

            def energy(t, p):
                pe.wait_ge(qk_ok, t + 1)
                after(pe, exp_ok, t - 1)
                for j in range(2):
                    for b in range(2):
                        h = slice(b * S, (b + 1) * S)
                        mm = pe.matmul(ps[:, EN + 2 * (p % 2) + b, j * D:(j + 1) * D],
                                       qk[h, p % 2, 0, j * P:(j + 1) * P], qk[h, p % 2, 1, :], start=True, stop=True)
                mm.then_inc(en_ps, 1)

            def read_out(t, p):
                pe.wait_ge(exp_ok, t + 1)
                pe.wait_ge(xvn_ok, t + 1)
                after(pe, xrn_ok, t)
                for b in range(2):
                    for j in range(2):
                        pe.matmul(ps[b * S:(b + 1) * S, XR, 0:D], xv_n[:, p % 2, (2 * b + j) * S:(2 * b + j + 1) * S],
                                  att[:, p % 2, 2 * b + j, :], start=(j == 0), stop=(j == 1))
                for b in range(2):
                    for j in range(2):
                        mm = pe.matmul(ps[b * S:(b + 1) * S, XR, D:2 * D],
                                       row_inv[:, p, 2 * b + j:2 * b + j + 1].broadcast_to([P, S]),
                                       att[:, p % 2, 2 * b + j, :], start=(j == 0), stop=(j == 1))
                mm.then_inc(xr_ps, 1)

            def mix_out(t, p):
                pe.wait_ge(diff_ok, t + 1)
                after(pe, gate_ok, t)
                pe.matmul(ps[:, TPS, 0:D], w0[:, 2, :], diff[:, p % 2, :], start=True, stop=True).then_inc(t_ps, 1)

            run(pe, ((3, project), (2, energy), (1, read_out), (0, mix_out)))

        @block.scalar
        def _(act):
            act.wait_ge(ld_w, 16 * 3)

            def copy_qk(t, p):
                act.wait_ge(proj_ps, t + 1)
                after(act, en_ps, t - 1)
                act.activation(qk[:, p % 2, :, :].rearrange("q a d -> q (a d)"), ps[:, PROJ, :], ACT.Copy).then_inc(qk_ok, 1)

            def keep(t, p):
                after(act, out_ok, OUT_CREDIT + t - NP + 1)
                act.activation(x_keep[:, p, :], x_in[:, p, :], ACT.Copy).then_inc(keep_ok, 1)

            def exps(t, p):
                act.wait_ge(max_ok, t + 1)
                after(act, xr_ps, t - 1)
                for i in range(4):
                    a = act.activation(att[:, p % 2, i, :], ps[:, EN + 2 * (p % 2) + i // 2, (i % 2) * D:(i % 2 + 1) * D],
                                       ACT.Exp, bias=neg_max[:, p, i:i + 1], accum_out=row_sum[:, p, i:i + 1])
                a.then_inc(exp_ok, 1)

            def relu(t, p):
                act.wait_ge(t_ps, t + 1)
                act.wait_ge(out_ok, OUT_CREDIT + t - 1)
                act.activation(gate[:, p % 2, :], ps[:, TPS, 0:D], ACT.Relu, bias=bt[:, 0:1]).then_inc(gate_ok, 1)

            run(act, ((3, copy_qk), (2, exps), (0, relu), (3, keep)))

        @block.vector
        def _(dve):
            dve.wait_ge(ld_w, 16 * 3)

            def row_max(t, p):
                dve.wait_ge(en_ps, t + 1)
                dve.tensor_reduce(neg_max[:, p, :],
                                  ps[:, EN + 2 * (p % 2):EN + 2 * (p % 2) + 2, :].rearrange("q e (j m) -> q (e j) m", j=2),
                                  AX, ALU.max, negate=True).then_inc(max_ok, 1)

            def values(t, p):
                dve.wait_ge(xv_ps, t + 1)
                after(dve, xvn_ok, t - 1)
                dve.tensor_tensor(xv_b[:, p % 2, :].rearrange("q (j c) -> q j c", j=2),
                                  ps[:, XV, 0:D].rearrange("q (j c) -> q j c", j=2),
                                  bv[:, :].unsqueeze(1).broadcast_to([P, 2, P]), ALU.add).then_inc(xvb_ok, 1)

            def scale_values(t, p):
                dve.wait_ge(exp_ok, t + 1)
                dve.reciprocal(row_inv[:, p, :], row_sum[:, p, :]).then_inc(inv_ok, 1)
                dve.wait_ge(inv_ok, t + 1)
                dve.wait_ge(xvb_ok, t + 1)
                after(dve, xr_ps, t - 1)
                dve.tensor_tensor(xv_n[:, p % 2, :].rearrange("q (b j c) -> q b j c", b=2, j=2),
                                  xv_b[:, p % 2, :].rearrange("q (j b c) -> q b j c", b=2, j=2),
                                  row_inv[:, p, :].rearrange("q (b j) -> q b j", b=2).unsqueeze(3).broadcast_to([P, 2, 2, S]),
                                  ALU.mult).then_inc(xvn_ok, 1)

            def normalize(t, p):
                dve.wait_ge(xr_ps, t + 1)
                dve.tensor_scalar(col_inv[:, p % 2, :], ps[:, XR, D:2 * D], 1e-7, None, ALU.add).then_inc(col_ok, 1)
                dve.wait_ge(col_ok, 2 * t + 1)
                dve.reciprocal(col_inv[:, p % 2, :], col_inv[:, p % 2, :]).then_inc(col_ok, 1)
                dve.wait_ge(col_ok, 2 * t + 2)
                after(dve, t_ps, t - 1)
                dve.tensor_tensor(diff[:, p % 2, :], ps[:, XR, 0:D], col_inv[:, p % 2, :], ALU.mult).then_inc(xrn_ok, 1)

            def difference(t, p):
                dve.wait_ge(xrn_ok, t + 1)
                dve.wait_ge(keep_ok, t + 1)
                dve.tensor_tensor(diff[:, p % 2, :], x_keep[:, p, :], diff[:, p % 2, :], ALU.subtract).then_inc(diff_ok, 1)

            run(dve, ((3, values), (2, row_max), (1, normalize), (2, scale_values), (1, difference)))


def phase_b(nc, io, ps, w, x_mid, ld_b, ld_c, ld_set, zero_ok, a_stored, b_loads, stored, c_loads):
    ctx = ExitStack()
    with ctx:
        def sb(name, *shape):
            return ctx.enter_context(nc.sbuf_tensor("b_" + name, [P, *shape], F32))

        def sem(name):
            return ctx.enter_context(nc.semaphore("b_" + name))

        def sems(n, name):
            return [sem(f"{name}{i + 1}") for i in range(n)]

        x_in, x_cur, x_mlp, x_out = w["b_x_in"], sb("x_cur", NP, D), sb("x_mlp", NP, D), w["b_x_out"]
        enc, raw_mask = w["enc"], w["raw_mask"]
        cross_mul, cross_add = sb("cross_mul", GB, S), sb("cross_add", GB, S)
        self_mul, self_add = sb("self_mul", S), sb("self_add", S)
        bn, mv, var, rstd, xc = sb("bn", NP, 6), sb("mv", NP, 2), sb("var", NP), sb("rstd", NP), sb("xc", NP, D)
        minus_half, gate_mark = sb("minus_half", NP), sb("gate_mark", 1)
        hT = sb("hT", NC, GT)
        qM, kB, vP = ([w[a + n] for a in ("self", "cross")] for n in ("_q", "_k", "_v"))
        sc = sb("sc", 2, 2, NPAIR, S)
        neg_max = sb("neg_max", 2, 2 * NPAIR)
        pT = sb("pT", 2, NPP, P)
        inv_sum, c_tok = sb("inv_sum", 2, NPAIR), sb("c_tok", 2, P)
        cT = sb("cT", 2, GT)
        pre, poly = sb("pre", 4, GT), sb("poly", 4, GT)
        act_g = sb("act_g", NJ, GT)

        ld_x, ld_enc, ld_mask = b_loads["x"], b_loads["enc"], b_loads["mask"]
        out_free = sem("out_free")
        ready = {n: sem("ready_" + n) for n in SETS}
        const_ok, smask_ok, cmask_ok = sem("const_ok"), sem("smask_ok"), sem("cmask_ok")
        q_ps, q_ok, k_ps, k_ok, v_ps, v_ok = (sems(2, n) for n in ("q_ps", "q_ok", "k_ps", "k_ok", "v_ps", "v_ok"))
        stat_ok, var_ok, rstd_ok, xc_ok = (sems(2, n) for n in ("stat_ok", "var_ok", "rstd_ok", "xc_ok"))
        ln_ps, h_ok, bias_ok = sems(3, "ln_ps"), sems(3, "h_ok"), sems(3, "bias_ok")
        sc_ps, mul_ok, add_ok, max_ok, sub_ok, exp_ok = (sem(n) for n in ("sc_ps", "mul_ok", "add_ok", "max_ok", "sub_ok", "exp_ok"))
        pT_ps, pT_ok, v_sum_ps, inv_ok, tok_ok, c_ps, c_ok = (sem(n) for n in ("pT_ps", "pT_ok", "v_sum_ps", "inv_ok", "tok_ok", "c_ps", "c_ok"))
        o_ps, res_ok = sem("o_ps"), sem("res_ok")
        hid_ps, sq_ok, poly_ok, arg_ok, th_ok, g_ok = (sem(n) for n in ("hid_ps", "sq_ok", "poly_ok", "arg_ok", "th_ok", "g_ok"))
        m_ps, out_ok = sem("m_ps"), sem("out_ok")

        rows = group_rows(x_mid)
        enc_cols = io["ctxT"].rearrange("(c p) (g t) -> g p c t", p=P, g=NG)
        mask_rows = io["cross_mask"].rearrange("(g b q) k -> g q b k", b=GB, q=S)

        def weight(n, c, a=0, b=None):
            lo, hi = WL[n]
            return w["wl"][:, c, lo + a:hi if b is None else lo + b]

        def vec(n, i, f=slice(0, P)):
            return w["vl"][f, VL[n][0] + i:VL[n][0] + i + 1]

        def row(n):
            return w["rl"][:, slice(*RL[n])]

        def tile(a, n, p):
            return (2 * n + a) * NP + p

        def after(engine, semaphore, count):
            if not (isinstance(count, int) and count == 0):
                engine.wait_ge(semaphore, count)

        SC, PT, CX, YB = 0, 2, 4, 6
        CT, OUT = CX, CX + 1
        V2_BANK = (YB, SC + 1)
        block = ctx.enter_context(nc.Block())

        @block.sync
        def _(sp):
            def one(view, group):
                return view[bass.ds(group, 1)].rearrange("g p c t -> (g p) c t")

            def load_enc(n, src):
                sp.wait_ge(v_ps[1], 2 * n)
                sp.dma_start(enc[:, :, :], src).then_inc(ld_enc, 16)

            def load_mask(n, src):
                sp.wait_ge(cmask_ok, 2 * n)
                for par in range(2):
                    sp.dma_start(raw_mask[par * S:(par + 1) * S, :, :], src).then_inc(ld_mask, 16)

            def load_x(n, src):
                sp.wait_ge(res_ok, tile(0, n, 0) - NP)
                sp.dma_start(x_in[:, :, :], src).then_inc(ld_x, 16)

            def store(n, dst):
                sp.wait_ge(out_ok, NP * n + 2 * NP)
                sp.dma_start(dst, x_out[:, :, :]).then_inc(stored, 16)
                sp.wait_ge(stored, 16 * n + 16)
                sp.sem_inc(out_free, 1)

            def reload(s):
                for dst, src in load_set(w, io, 1, s):
                    sp.dma_start(dst, src).then_inc(ld_set[s], 16)

            def mark_ready(s, layer):
                sp.wait_ge(ld_set[s], 16 * SETS[s] * (layer + 1))
                sp.sem_inc(ready[s], NG)

            sp.wait_ge(a_stored, 16 * NG * NP)
            sp.sem_inc(out_free, 1)
            for s in SETS:
                mark_ready(s, 0)
            load_x(1, rows[1])
            with sp.Fori(0, NG - 2) as it:
                load_enc(it + 1, one(enc_cols, it + 1))
                load_mask(it + 1, one(mask_rows, it + 1))
                load_x(it + 2, one(rows, it + 2))
                store(it, one(rows, it))
            n = NG - 2
            load_enc(n + 1, enc_cols[n + 1])
            load_mask(n + 1, mask_rows[n + 1])
            for done, count in ((q_ok, 4), (k_ok, 2), (v_ok, 2)):
                sp.wait_ge(done[0], count * NG)
            reload("first")
            load_x(n + 2, rows[0])
            mark_ready("first", 1)
            store(n, rows[n])
            n = NG - 1
            load_enc(n + 1, enc_cols[0])
            load_mask(n + 1, mask_rows[0])
            for done, count in ((q_ok, 4), (k_ok, 2), (v_ok, 2)):
                sp.wait_ge(done[1], count * NG)
            sp.wait_ge(bias_ok[1], NP * NG)
            reload("middle")
            mark_ready("middle", 1)
            load_x(n + 2, rows[1])
            store(n, rows[n])
            reload("last")
            mark_ready("last", 1)
            with sp.Fori(NG, TURNS - 2) as it:
                load_enc(it + 1, one(enc_cols, it - (NG - 1)))
                load_mask(it + 1, one(mask_rows, it - (NG - 1)))
                load_x(it + 2, one(rows, it - (NG - 2)))
                store(it, one(rows, it - NG))
            n = TURNS - 2
            load_enc(n + 1, enc_cols[NG - 1])
            load_mask(n + 1, mask_rows[NG - 1])
            store(n, rows[NG - 2])
            sp.wait_ge(v_sum_ps, tile(1, TURNS - 1, 0))
            for dst, src in load_c_weights(w, io):
                sp.dma_start(dst, src).then_inc(ld_c, 16)
            for dst, src, done in load_first_c(w, io, x_mid, c_loads):
                sp.dma_start(dst, src).then_inc(done, 16)
            sp.wait_ge(out_ok, NP * TURNS + NP)
            sp.dma_start(rows[NG - 1], x_out[:, :, :]).then_inc(stored, 16)

        @block.gpsimd
        def _(pool):
            pool.wait_ge(smask_ok, 2)
            pool.wait_ge(const_ok, 1)

            def add_bias(ln, n, p):
                if ln < 2:
                    pool.wait_ge(xc_ok[ln], NP * n + p + 1 if ln == 0 else tile(0, n, p) + 1)
                    x = (x_in, x_cur)[ln]
                    pool.tensor_tensor(x[:, p, :], x[:, p, :], row(("bao", "bco")[ln]), ALU.add).then_inc(bias_ok[ln], 1)
                else:
                    pool.wait_ge(res_ok, tile(1, n, p) + 1)
                    pool.wait_ge(out_ok, NP * n + NP)
                    pool.tensor_tensor(x_mlp[:, p, :], x_cur[:, p, :], row("b2"), ALU.add).then_inc(bias_ok[ln], 1)

            def add_mask(a, n, p):
                pool.wait_ge(mul_ok, tile(a, n, p) + 1)
                t = sc[:, p % 2, :, :, :]
                if a == 0:
                    m = self_add[:, :].unsqueeze(1).broadcast_to([P, 2 * NPAIR, S])
                    t = t.rearrange("q b i k -> q (b i) k")
                else:
                    m = cross_add[:, 2 * p:2 * p + 2, :].unsqueeze(2).broadcast_to([P, 2, NPAIR, S])
                pool.tensor_tensor(t, t, m, ALU.add).then_inc(add_ok, 1)

            def inv_std(a, n, p):
                pool.wait_ge(var_ok[1], tile(a, n, p) + 1)
                pool.tensor_tensor(rstd[:, p:p + 1], var[:, p:p + 1], minus_half[:, p:p + 1], ALU.pow).then_inc(rstd_ok[1], 1)

            def inv_std_first(n):
                pool.wait_ge(var_ok[0], NP * n + NP)
                pool.tensor_tensor(rstd[:, :], var[:, :], minus_half[:, :], ALU.pow).then_inc(rstd_ok[0], NP)

            def cube(n, j):
                pool.wait_ge(poly_ok, NJ * n + j + 1)
                pool.tensor_tensor(poly[:, j % 4, :], poly[:, j % 4, :], pre[:, j % 4, :], ALU.mult).then_inc(arg_ok, 1)

            def cross(n, nxt):
                add_mask(1, n, 0)
                add_mask(1, n, 1)
                pool.wait_ge(ready["last"], n + 1)
                if nxt is not None:
                    pool.wait_ge(ready["middle"], nxt + 1)
                for p in range(NP):
                    if p >= 1:
                        inv_std(1, n, p - 1)
                    if p + 2 < NP:
                        add_mask(1, n, p + 2)
                    if p >= 1:
                        add_bias(2, n, p - 1)
                    if nxt is not None:
                        if p >= 2:
                            add_mask(0, nxt, p - 2)
                        add_bias(0, nxt, p)
                if nxt is None:
                    inv_std(1, n, NP - 1)
                    add_bias(2, n, NP - 1)
                    for j in range(NJ):
                        cube(n, j)

            def self_attention(n, last):
                if last is None:
                    add_mask(0, n, 0)
                    add_mask(0, n, 1)
                    pool.wait_ge(ready["middle"], n + 1)
                    for p in range(NP):
                        add_bias(0, n, p)
                cubes = ((), (0, 1), (2, 3, 4), (5, 6)) if last is not None else ((),) * NP
                for p in range(NP):
                    if p >= 1:
                        inv_std(0, n, p - 1)
                    elif last is not None:
                        inv_std(1, last, NP - 1)
                    if p + 2 < NP:
                        add_mask(0, n, p + 2)
                    if p == 0 and last is not None:
                        add_bias(2, last, NP - 1)
                    for j in cubes[p][:1]:
                        cube(last, j)
                    if p >= 1:
                        add_bias(1, n, p - 1)
                    for j in cubes[p][1:]:
                        cube(last, j)
                if last is not None:
                    cube(last, NJ - 1)
                inv_std(0, n, NP - 1)
                add_bias(1, n, NP - 1)

            inv_std_first(0)
            self_attention(0, None)
            with pool.Fori(0, TURNS - 1) as it:
                inv_std_first(it + 1)
                cross(it, it + 1)
                self_attention(it + 1, it)
            cross(TURNS - 1, None)

        @block.tensor
        def _(pe):
            pe.wait_ge(ld_b, 16 * N_B_CONST)
            pe.wait_ge(zero_ok, N_ZERO)

            def project_T(name, rhs, c, done, first=0, bank=YB):
                for k in range(NC):
                    mm = pe.matmul(ps[:, bank + c, :], weight(name, k, first + c * P, first + (c + 1) * P), rhs[:, k, :],
                                   start=(k == 0), stop=(k == NC - 1))
                mm.then_inc(done, 1)

            def project_v(name, lhs, half, done, bank):
                for b in range(GB // 2):
                    t = (half * GB // 2 + b) * S
                    for k in range(NC):
                        for odd in range(2):
                            mm = pe.matmul(ps[odd * S:(odd + 1) * S, bank, b * P:(b + 1) * P], lhs[:, k, t:t + S],
                                           weight(name, k, odd * P, (odd + 1) * P), start=(k == 0), stop=(k == NC - 1))
                mm.then_inc(done, 1)

            NORM_BANK = (CX, CX, YB)

            def norm_T(ln, n):
                for p in range(NP):
                    pe.wait_ge(xc_ok[min(ln, 1)], (NP * n if ln == 0 else tile(ln - 1, n, 0)) + p + 1)
                    for c in range(NC):
                        mm = pe.transpose(ps[:, NORM_BANK[ln] + c, p * P:(p + 1) * P], xc[:, p, c * P:(c + 1) * P], w["ident"][:, :])
                mm.then_inc(ln_ps[ln], 1)

            def first_norm_T(n):
                after(pe, h_ok[1], 2 * n)
                norm_T(0, n)

            def queries_1(n, c):
                if c == 0:
                    if not isinstance(n, int):
                        pe.wait_ge(out_ok, NP * n)
                    after(pe, k_ok[1], 2 * n)
                    after(pe, v_ok[1], 2 * n)
                    pe.wait_ge(h_ok[0], 2 * n + 2)
                    pe.wait_ge(ready["first"], n + 1)
                project_T("qk", hT, c, q_ps[0])

            def keys_1(n, c):
                pe.wait_ge(q_ok[0], 4 * n + 2 * c + 2)
                project_T("qk", hT, c, k_ps[0], first=D)

            def values_1(n, half):
                pe.wait_ge(k_ok[0], 2 * n + half + 1)
                project_v("v", hT, half, v_ps[0], YB + half)

            def keys_2(n, c):
                if c == 0:
                    pe.wait_ge(ld_enc, 16 * n + 16)
                    pe.wait_ge(ready["middle"], n + 1)
                pe.wait_ge(v_ok[0], 2 * n + c + 1)
                project_T("k2", enc, c, k_ps[1])

            def values_2(n, half):
                if half == 0:
                    pe.wait_ge(k_ok[1], 2 * n + 1)
                else:
                    pe.wait_ge(mul_ok, tile(1, n, 0))
                project_v("v2", enc, half, v_ps[1], V2_BANK[half])

            def queries_2(n, c):
                pe.wait_ge(h_ok[1], 2 * n + 2)
                project_T("q2", hT, c, q_ps[1], bank=PT)

            def scores(a, n, p):
                if p == 0:
                    pe.wait_ge(q_ok[a], 4 * n + 4)
                    pe.wait_ge(k_ok[a], 2 * n + 2)
                    if a == 1:
                        pe.wait_ge(v_ok[1], 2 * n + 2)
                after(pe, mul_ok, tile(a, n, p))
                for b in range(2):
                    for c in range(NC):
                        mm = pe.matmul(ps[:, SC + b, c * D:(c + 1) * D], qM[a][:, c, 2 * p + b, :, :].rearrange("f h q -> f (h q)"),
                                       kB[a][:, c, 2 * p + b, :, :].rearrange("f r k -> f (r k)"), start=True, stop=True)
                mm.then_inc(sc_ps, 1)

            def probs_T(a, n, p):
                pe.wait_ge(exp_ok, tile(a, n, p) + 1)
                for b in range(2):
                    for i in range(NPP):
                        mm = pe.transpose(ps[:, PT + b, i * P:(i + 1) * P],
                                          sc[:, p % 2, b, 2 * i:2 * i + 2, :].rearrange("q i k -> q (i k)"), w["ident"][:, :])
                    mm.then_inc(pT_ps, 1)

            def times_v(a, n, p):
                if p == 0:
                    pe.wait_ge(v_ok[a], 2 * n + 2)
                pe.wait_ge(pT_ok, 2 * tile(a, n, p) + 2)
                after(pe, c_ok, tile(a, n, p))
                after(pe, res_ok, tile(a, n, p))
                for b in range(2):
                    for i in range(NPP):
                        for par in range(2):
                            h = slice(par * S, (par + 1) * S)
                            mm = pe.matmul(ps[h, CX + b, i * 2 * VW:(i + 1) * 2 * VW], pT[:, b, i, h], vP[a][:, 2 * p + b, i, :],
                                           start=True, stop=True)
                mm.then_inc(v_sum_ps, 1)

            def result_T(a, n, p):
                pe.wait_ge(tok_ok, tile(a, n, p) + 1)
                for b in range(2):
                    mm = pe.transpose(ps[:, CT, b * P:(b + 1) * P], c_tok[:, b, :], w["ident"][:, :])
                mm.then_inc(c_ps, 1)

            def out_project(a, n, p):
                if p == 0:
                    pe.wait_ge(ready[("middle", "last")[a]], n + 1)
                pe.wait_ge(c_ok, tile(a, n, p) + 1)
                for par in range(2):
                    mm = pe.matmul(ps[:, OUT, 0:D], cT[:, par, p * P:(p + 1) * P], weight(("ao", "co")[a], par),
                                   start=(par == 0), stop=(par == 1))
                mm.then_inc(o_ps, 1)

            def third_norm_T(n, nxt):
                if nxt is not None:
                    pe.wait_ge(v_ok[1], 2 * nxt + 1)
                    pe.wait_ge(k_ok[1], 2 * nxt + 2)
                else:
                    pe.wait_ge(out_ok, NP * n + NP)
                norm_T(2, n)

            def hidden(n, j):
                if j < 2:
                    pe.wait_ge(h_ok[2], 2 * n + 2)
                else:
                    pe.wait_ge(sq_ok, NJ * n + j - 1)
                for k in range(NC):
                    mm = pe.matmul(ps[:, YB + j % 2, :], weight("w1", k, j * P, (j + 1) * P), hT[:, k, :],
                                   start=(k == 0), stop=(k == NC - 1))
                mm.then_inc(hid_ps, 1)

            def mlp_out(n, p, first=0, last=NJ):
                if p == 0 and first == 0:
                    pe.wait_ge(sq_ok, NJ * n + NJ - 1)
                elif p >= 2:
                    pe.wait_ge(out_ok, NP * n + NP + p - 1)
                for j in range(first, last):
                    if p == 0:
                        pe.wait_ge(g_ok, NJ * n + j + 1)
                    mm = pe.matmul(ps[:, YB + p % 2, 0:D], act_g[:, j, p * P:(p + 1) * P], w["w2"][:, j, :],
                                   start=(j == 0), stop=(j == NJ - 1))
                if last == NJ:
                    mm.then_inc(m_ps, 1)

            def cross(n, nxt):
                beside = nxt is not None
                if beside:
                    first_norm_T(nxt)
                scores(1, n, 0)
                if beside:
                    queries_1(nxt, 0)
                scores(1, n, 1)
                if beside:
                    queries_1(nxt, 1)
                    keys_1(nxt, 0)
                    keys_1(nxt, 1)
                for p in range(NP):
                    probs_T(1, n, p)
                    if p >= 1:
                        out_project(1, n, p - 1)
                    if p + 2 < NP:
                        scores(1, n, p + 2)
                    elif beside:
                        scores(0, nxt, p + 2 - NP)
                    times_v(1, n, p)
                    if beside:
                        (values_1, values_1, keys_2, keys_2)[p](nxt, p % 2)
                    result_T(1, n, p)
                if not beside:
                    out_project(1, n, NP - 1)
                    third_norm_T(n, None)
                    hidden(n, 0)
                    hidden(n, 1)
                    for j in range(2, NJ):
                        hidden(n, j)
                    for p in range(NP):
                        mlp_out(n, p)

            def self_attention(n, last):
                beside = last is not None
                if not beside:
                    scores(0, n, 0)
                    scores(0, n, 1)
                for p in range(NP):
                    probs_T(0, n, p)
                    if p >= 1:
                        out_project(0, n, p - 1)
                    elif beside:
                        out_project(1, last, NP - 1)
                    if beside and p == 1:
                        third_norm_T(last, n)
                    if p + 2 < NP:
                        scores(0, n, p + 2)
                    elif beside:
                        hidden(last, (3, 7)[p - 2])
                    times_v(0, n, p)
                    if beside:
                        for j in ((), (0, 1, 2), (4, 5, 6), ())[p]:
                            hidden(last, j)
                    if p % 3 == 0:
                        values_2(n, p // 3)
                    result_T(0, n, p)
                if beside:
                    mlp_out(last, 0, last=3)
                out_project(0, n, NP - 1)
                if beside:
                    mlp_out(last, 0, first=3)
                    mlp_out(last, 1)
                pe.wait_ge(res_ok, tile(0, n, NP))
                norm_T(1, n)
                if beside:
                    mlp_out(last, 2)
                queries_2(n, 0)
                queries_2(n, 1)
                if beside:
                    mlp_out(last, 3)

            first_norm_T(0)
            for c in range(2):
                queries_1(0, c)
            for c in range(2):
                keys_1(0, c)
            for half in range(2):
                values_1(0, half)
            for c in range(2):
                keys_2(0, c)
            self_attention(0, None)
            with pe.Fori(0, TURNS - 1) as it:
                cross(it, it + 1)
                self_attention(it + 1, it)
            cross(TURNS - 1, None)

        @block.scalar
        def _(act):
            act.wait_ge(ld_b, 16 * N_B_CONST)
            act.wait_ge(zero_ok, N_ZERO)

            def norm_out(ln, n):
                act.wait_ge(ready[("first", "middle", "last")[ln]], n + 1)
                act.wait_ge(ln_ps[ln], n + 1)
                for c in range(NC):
                    act.activation(hT[:, c, :], ps[:, (CX, CX, YB)[ln] + c, :], ACT.Identity, bias=vec(f"ln{ln + 1}_b", c),
                                   scale=vec(f"ln{ln + 1}_s", c)).then_inc(h_ok[ln], 1)

            def queries(a, n, c):
                act.wait_ge(q_ps[a], 2 * n + c + 1)
                for par in range(2):
                    act.activation(qM[a][:, c, :, par, :], ps[:, (YB, PT)[a] + c, :].rearrange("f (b q) -> f b q", q=S), ACT.Identity,
                                   bias=vec(("bq", "bq2")[a], 2 * c + par), scale=w["parity"][:, par:par + 1]).then_inc(q_ok[a], 1)

            def keys(a, n, c):
                act.wait_ge(k_ps[a], 2 * n + c + 1)
                for r in range(NR):
                    f = slice(r * PF, (r + 1) * PF)
                    op = act.activation(kB[a][f, c, :, r, :], ps[f, YB + c, :].rearrange("f (b k) -> f b k", k=S), ACT.Identity,
                                        bias=vec(("bk", "bk2")[a], c, f))
                op.then_inc(k_ok[a], 1)

            def exps(a, n, p):
                act.wait_ge(sub_ok, tile(a, n, p) + 1)
                t = sc[:, p % 2, :, :, :].rearrange("q b i k -> q (b i k)")
                act.activation(t, t, ACT.Exp).then_inc(exp_ok, 1)

            def copy_pT(a, n, p):
                for b in range(2):
                    act.wait_ge(pT_ps, 2 * tile(a, n, p) + b + 1)
                    act.activation(pT[:, b, :, :].rearrange("k i q -> k (i q)"), ps[:, PT + b, :], ACT.Copy).then_inc(pT_ok, 1)

            def copy_cT(a, n, p):
                act.wait_ge(c_ps, tile(a, n, p) + 1)
                act.activation(cT[:, :, p * P:(p + 1) * P].rearrange("f h (b q) -> f b h q", b=2),
                               ps[:, CT, 0:D].rearrange("f (b h q) -> f b h q", b=2, h=2), ACT.Copy).then_inc(c_ok, 1)

            def pre_square(n, j):
                act.wait_ge(hid_ps, NJ * n + j + 1)
                if j >= 4:
                    act.wait_ge(g_ok, NJ * n + j - 3)
                act.activation(pre[:, j % 4, :], ps[:, YB + j % 2, :], ACT.Identity, bias=vec("b1", j))
                act.activation(poly[:, j % 4, :], ps[:, YB + j % 2, :], ACT.Square, bias=vec("b1", j)).then_inc(sq_ok, 1)

            def tanh(n, j):
                act.wait_ge(arg_ok, NJ * n + j + 1)
                t = poly[:, j % 4, :]
                act.activation(t, t, ACT.Tanh, scale=GELU_C).then_inc(th_ok, 1)

            def cross(n, nxt):
                beside = nxt is not None
                if beside:
                    norm_out(0, nxt)
                    queries(0, nxt, 0)
                    queries(0, nxt, 1)
                exps(1, n, 0)
                if beside:
                    keys(0, nxt, 0)
                for p in range(NP):
                    if p >= 1:
                        copy_cT(1, n, p - 1)
                    copy_pT(1, n, p)
                    if beside and p == 0:
                        keys(0, nxt, 1)
                    if p + 1 < NP:
                        exps(1, n, p + 1)
                    elif beside:
                        exps(0, nxt, 0)
                        keys(1, nxt, 0)
                if not beside:
                    copy_cT(1, n, NP - 1)
                    norm_out(2, n)
                    pre_square(n, 0)
                    for j in range(NJ):
                        if j + 1 < NJ:
                            pre_square(n, j + 1)
                        tanh(n, j)

            def self_attention(n, last):
                beside = last is not None
                if not beside:
                    exps(0, n, 0)
                for p in range(NP):
                    if p >= 1:
                        copy_cT(0, n, p - 1)
                    elif beside:
                        copy_cT(1, last, NP - 1)
                    copy_pT(0, n, p)
                    if beside and p == 1:
                        norm_out(2, last)
                    if p + 1 < NP:
                        exps(0, n, p + 1)
                    if beside:
                        if p == 0:
                            keys(1, n, 1)
                        elif p == 1:
                            pre_square(last, 0)
                            pre_square(last, 1)
                        elif p == 2:
                            tanh(last, 0)
                            pre_square(last, 2)
                            tanh(last, 1)
                            pre_square(last, 3)
                            tanh(last, 2)
                            pre_square(last, 4)
                            pre_square(last, 5)
                        elif p == 3:
                            tanh(last, 3)
                            tanh(last, 4)
                            pre_square(last, 6)
                            tanh(last, 5)
                            pre_square(last, 7)
                copy_cT(0, n, NP - 1)
                if beside:
                    tanh(last, 6)
                    tanh(last, 7)
                norm_out(1, n)
                queries(1, n, 0)
                queries(1, n, 1)

            norm_out(0, 0)
            act.wait_ge(ready["middle"], 1)
            queries(0, 0, 0)
            queries(0, 0, 1)
            for a in range(2):
                for c in range(2):
                    keys(a, 0, c)
            self_attention(0, None)
            with act.Fori(0, TURNS - 1) as it:
                cross(it, it + 1)
                self_attention(it + 1, it)
            cross(TURNS - 1, None)

        @block.vector
        def _(dve):
            dve.memset(minus_half[:, :], -0.5).then_inc(const_ok, 1)
            dve.memset(inv_sum[:, :, :], 0.0).then_inc(out_ok, NP)
            dve.wait_ge(zero_ok, N_ZERO)
            dve.wait_ge(ld_b, 16 * N_B_CONST)
            dve.tensor_scalar(self_mul[:, :], w["self_mask"][:, :], HD ** -0.5, None, ALU.mult).then_inc(smask_ok, 1)
            dve.tensor_scalar(self_add[:, :], w["self_mask"][:, :], 10000.0, -10000.0, ALU.mult, ALU.add).then_inc(smask_ok, 1)
            dve.wait_ge(smask_ok, 2)

            def stats(s, count, src, tiles):
                before = 2 * (count + tiles[0])
                for p in tiles:
                    dve.bn_stats(bn[:, p, :], src[:, p, :]).then_inc(stat_ok[s], 1)
                dve.wait_ge(stat_ok[s], before + len(tiles))
                dve.memset(gate_mark[:, :], 0.0)
                for p in tiles:
                    dve.bn_aggr(mv[:, p, :], bn[:, p, :]).then_inc(stat_ok[s], 1)
                for i, p in enumerate(tiles):
                    dve.wait_ge(stat_ok[s], before + len(tiles) + i + 1)
                    dve.tensor_scalar(var[:, p:p + 1], mv[:, p, 1:2], EPS, None, ALU.add).then_inc(var_ok[s], 1)

            def norm(s, count, src, p):
                dve.wait_ge(rstd_ok[s], count + p + 1)
                dve.tensor_scalar(xc[:, p, :], src[:, p, :], mv[:, p, 0:1], rstd[:, p:p + 1], ALU.subtract, ALU.mult).then_inc(xc_ok[s], 1)

            def first_stats(n):
                dve.wait_ge(ld_x, 16 * n + 16)
                stats(0, NP * n, x_in, range(NP))

            def first_norm(n):
                after(dve, ln_ps[1], n)
                for p in range(NP):
                    norm(0, NP * n, x_in, p)

            def values(a, n, half):
                dve.wait_ge(v_ps[a], 2 * n + half + 1)
                for odd in range(2):
                    h = slice(odd * S, (odd + 1) * S)
                    r = row(("bv", "bv2")[a])[h, odd * P:(odd + 1) * P]
                    op = dve.tensor_tensor(vP[a][h, 4 * half:4 * half + 4, :, odd * VW:odd * VW + PF],
                                           ps[h, (YB + half, V2_BANK[half])[a], :].rearrange("k (b i e) -> k b i e", b=4, e=PF),
                                           r.rearrange("k (i e) -> k i e", e=PF).unsqueeze(1).broadcast_to([S, 4, NPP, PF]), ALU.add)
                op.then_inc(v_ok[a], 1)

            def cross_masks(n):
                dve.wait_ge(ld_mask, 32 * n + 32)
                dve.tensor_scalar(cross_mul[:, :, :], raw_mask[:, :, :], HD ** -0.5, None, ALU.mult).then_inc(cmask_ok, 1)
                dve.tensor_scalar(cross_add[:, :, :], raw_mask[:, :, :], 10000.0, -10000.0, ALU.mult, ALU.add).then_inc(cmask_ok, 1)
                dve.wait_ge(cmask_ok, 2 * n + 2)

            def mask(a, n, p):
                dve.wait_ge(sc_ps, tile(a, n, p) + 1)
                if a == 0:
                    dve.tensor_tensor(sc[:, p % 2, :, :, :].rearrange("q b i k -> q (b i) k"),
                                      ps[:, SC:SC + 2, :].rearrange("q b (i k) -> q (b i) k", k=S),
                                      self_mul[:, :].unsqueeze(1).broadcast_to([P, 2 * NPAIR, S]), ALU.mult).then_inc(mul_ok, 1)
                else:
                    dve.tensor_tensor(sc[:, p % 2, :, :, :], ps[:, SC:SC + 2, :].rearrange("q b (i k) -> q b i k", k=S),
                                      cross_mul[:, 2 * p:2 * p + 2, :].unsqueeze(2).broadcast_to([P, 2, NPAIR, S]),
                                      ALU.mult).then_inc(mul_ok, 1)

            def subtract_max(a, n, p):
                dve.wait_ge(add_ok, tile(a, n, p) + 1)
                t = sc[:, p % 2, :, :, :].rearrange("q b i k -> q (b i) k")
                dve.tensor_reduce(neg_max[:, p % 2, :], t, AX, ALU.max, negate=True).then_inc(max_ok, 1)
                dve.wait_ge(max_ok, tile(a, n, p) + 1)
                dve.tensor_tensor(t, t, neg_max[:, p % 2, :].unsqueeze(2).broadcast_to([P, 2 * NPAIR, S]), ALU.add).then_inc(sub_ok, 1)

            def normalize(a, n, p):
                dve.wait_ge(v_sum_ps, tile(a, n, p) + 1)
                pairs = ps[:, CX:CX + 2, 0:NPAIR * VW].rearrange("q b (i v) -> q b i v", v=VW)
                dve.reciprocal(inv_sum[:, :, :], pairs[:, :, :, PF:VW].rearrange("q b i v -> q b (i v)")).then_inc(inv_ok, 1)
                dve.wait_ge(inv_ok, tile(a, n, p) + 1)
                for par in range(2):
                    h = slice(par * S, (par + 1) * S)
                    op = dve.tensor_tensor(c_tok[h, :, :].rearrange("q b (i d) -> q b i d", d=HD),
                                           pairs[h, :, :, par * HD:(par + 1) * HD],
                                           inv_sum[h, :, :].unsqueeze(3).broadcast_to([S, 2, NPAIR, HD]), ALU.mult)
                op.then_inc(tok_ok, 1)

            def residual(a, n, p):
                dve.wait_ge(o_ps, tile(a, n, p) + 1)
                dve.wait_ge(bias_ok[a], NP * n + p + 1)
                if a == 0 and not isinstance(n, int):
                    dve.wait_ge(bias_ok[2], NP * (n - 1) + p + 1)
                dve.tensor_tensor(x_cur[:, p, :], ps[:, OUT, 0:D], (x_in, x_cur)[a][:, p, :], ALU.add).then_inc(res_ok, 1)
                dve.wait_ge(res_ok, tile(a, n, p) + 1)
                stats(1, tile(a, n, 0), x_cur, [p])

            def behind(a, n, p):
                norm(1, tile(a, n, 0), x_cur, p)

            def cubic(n, j):
                dve.wait_ge(sq_ok, NJ * n + j + 1)
                t = poly[:, j % 4, :]
                dve.tensor_scalar(t, t, 0.044715, 1.0, ALU.mult, ALU.add).then_inc(poly_ok, 1)

            def gelu(n, j):
                dve.wait_ge(th_ok, NJ * n + j + 1)
                dve.scalar_tensor_tensor(act_g[:, j, :], poly[:, j % 4, :], 1.0, pre[:, j % 4, :], ALU.add, ALU.mult).then_inc(g_ok, 1)

            def result(n, p):
                if p == 0:
                    dve.wait_ge(out_free, n + 1)
                dve.wait_ge(m_ps, NP * n + p + 1)
                dve.wait_ge(bias_ok[2], NP * n + p + 1)
                dve.scalar_tensor_tensor(x_out[:, p, :], ps[:, YB + p % 2, 0:D], 0.5, x_mlp[:, p, :], ALU.mult, ALU.add).then_inc(out_ok, 1)

            def cross(n, nxt):
                beside = nxt is not None
                mask(1, n, 0)
                mask(1, n, 1)
                subtract_max(1, n, 0)
                subtract_max(1, n, 1)
                if beside:
                    dve.wait_ge(ready["first"], nxt + 1)
                for p in range(NP):
                    if p >= 1:
                        residual(1, n, p - 1)
                    if p + 2 < NP:
                        mask(1, n, p + 2)
                    elif beside:
                        mask(0, nxt, p + 2 - NP)
                    normalize(1, n, p)
                    if beside and 1 <= p <= 2:
                        values(0, nxt, p - 1)
                    if p >= 1:
                        behind(1, n, p - 1)
                    if p + 2 < NP:
                        subtract_max(1, n, p + 2)
                    elif beside:
                        subtract_max(0, nxt, p + 2 - NP)
                if not beside:
                    residual(1, n, NP - 1)
                    behind(1, n, NP - 1)
                    cubic(n, 0)
                    for j in range(NJ):
                        if j + 1 < NJ:
                            cubic(n, j + 1)
                        gelu(n, j)
                    for p in range(NP):
                        result(n, p)

            def self_attention(n, last, nxt):
                beside = last is not None
                if not beside:
                    mask(0, n, 0)
                    mask(0, n, 1)
                    subtract_max(0, n, 0)
                    subtract_max(0, n, 1)
                for p in range(NP):
                    if p >= 1:
                        residual(0, n, p - 1)
                    elif beside:
                        residual(1, last, NP - 1)
                    if p + 2 < NP:
                        mask(0, n, p + 2)
                    if beside and p == 2:
                        gelu(last, 0)
                        cubic(last, 2)
                    if beside and p == 3:
                        gelu(last, 3)
                        cubic(last, 5)
                    if p >= 1:
                        behind(0, n, p - 1)
                    elif beside:
                        behind(1, last, NP - 1)
                    normalize(0, n, p)
                    if p == 0:
                        cross_masks(n)
                        dve.wait_ge(ready["middle"], n + 1)
                        values(1, n, 0)
                    if p + 2 < NP:
                        subtract_max(0, n, p + 2)
                    if beside:
                        if p == 1:
                            cubic(last, 0)
                            cubic(last, 1)
                        elif p == 2:
                            cubic(last, 3)
                            gelu(last, 1)
                            gelu(last, 2)
                            cubic(last, 4)
                        elif p == 3:
                            gelu(last, 4)
                            cubic(last, 6)
                            gelu(last, 5)
                if beside:
                    cubic(last, 7)
                    gelu(last, 6)
                residual(0, n, NP - 1)
                if beside:
                    gelu(last, 7)
                behind(0, n, NP - 1)
                values(1, n, 1)
                if beside:
                    result(last, 0)
                    result(last, 1)
                if nxt is not None:
                    first_stats(nxt)
                if beside:
                    result(last, 2)
                if nxt is not None:
                    first_norm(nxt)
                if beside:
                    result(last, 3)

            dve.wait_ge(ready["first"], 1)
            first_stats(0)
            first_norm(0)
            values(0, 0, 0)
            values(0, 0, 1)
            self_attention(0, None, 1)
            with dve.Fori(0, TURNS - 2) as it:
                cross(it, it + 1)
                self_attention(it + 1, it, it + 2)
            cross(TURNS - 2, TURNS - 1)
            self_attention(TURNS - 1, TURNS - 2, None)
            cross(TURNS - 1, None)


def phase_c(nc, io, ps, w, x_mid, ld_c, b_stored, c_loads):
    ctx = ExitStack()
    with ctx:
        def sb(name, *shape):
            return ctx.enter_context(nc.sbuf_tensor("c_" + name, [P, *shape], F32))

        def sem(name):
            return ctx.enter_context(nc.semaphore("c_" + name))

        def sems(n, name):
            return [sem(f"{name}{i + 1}") for i in range(n)]

        NS = NC * RS
        ORDER = (1, 0, 2, 3, 4)
        OUTS = 11
        PROJ_DONE = (1, 5, 7, 9, 11)
        LEAD = 4
        BONUS, ENTRY, SHIFT, LOW_RANK = 4, 6, 13, 12

        x_in, x_cur, x_out = w["c_x_in"], sb("x_cur", NP, D), sb("x_out", NP, D)
        s0, prev = w["s0"], w["prev"]
        bn, mv, var, rstd, xc = ([sb(f"{n}{i}", *shape) for i in range(2)] for n, shape in
                                 (("bn", (NP, 6)), ("mv", (NP, 2)), ("var", (NP,)), ("rstd", (NP,)), ("xc", (NP, D))))
        xn = [sb(f"xn{n}", NC, GB, S + 1) for n in (1, 2)]
        gate_mark = sb("gate_mark", 1)
        minus_half, eps = sb("minus_half", NP), sb("eps", 1)
        xx = sb("xx", NC, GT)
        maa = sb("maa", 2, GT)
        x5, ff_in = sb("x5", 2, NC, GT), sb("ff_in", 2, NC, GT)
        dec, dexp = sb("dec", GT), sb("dexp", NC, GT)
        decay = sb("decay", NC, GB, S)
        kF, vF, rF = sb("kF", NC, GT), sb("vF", NC, GT), sb("rF", NC, GT)
        gg = sb("gg", NC, GT)
        kv = sb("kv", NS, GB, S)
        st, rs = sb("st", 3, GT), sb("rs", 4, GT)
        ruk, att, sqr = sb("ruk", NC, GT), sb("att", NC, GT), sb("sqr", NC, GT)
        kk, rr, ff = sb("kk", NC, GT), sb("rr", NP, D), sb("ff", 2, D)
        sx = [sb("sx1", NC, GT), sqr]
        th = dexp
        gn_rstd = ff_in[:, 0, :, :]

        ld_x, ld_s = c_loads["x"], c_loads["s"]
        ld_cur, stored, out_free = sem("ld_cur"), sem("stored"), sem("out_free")
        const_ok, keep_ok, state_ok = sem("const_ok"), sem("keep_ok"), sem("state_ok")
        stat_ok, var_ok, rstd_ok, xc_ok, ln_ps, xn_ok, sx_ok = (sems(2, n) for n in (
            "stat_ok", "var_ok", "rstd_ok", "xc_ok", "ln_ps", "xn_ok", "sx_ok"))
        xx_ok, maa_ps, maa_ok = (sem(n) for n in ("xx_ok", "maa_ps", "maa_ok"))
        mix_ps, mix_ok, x5_ok, proj_ps = (sem(n) for n in ("mix_ps", "mix_ok", "x5_ok", "proj_ps"))
        dec_ok, decay_ok, k_ok, v_ok, r_ok, th_ok, gg_ok = (sem(n) for n in ("dec_ok", "decay_ok", "k_ok", "v_ok", "r_ok", "th_ok", "gg_ok"))
        ruk_ok, ruk_ps, vb_ps, kv_ok, st_ok, rs_ok, red_ps, bonus_ok, att_ok = (sem(n) for n in ("ruk_ok", "ruk_ps", "vb_ps", "kv_ok", "st_ok", "rs_ok", "red_ps", "bonus_ok", "att_ok"))
        mean_ps, dm_ok, sqr_ok, var_ps, grstd_ok, nrm_ok, gn_ok, o_ok = (sem(n) for n in ("mean_ps", "dm_ok", "sqr_ok", "var_ps", "grstd_ok", "nrm_ok", "gn_ok", "o_ok"))
        o_ps, res_ok, ff_in_ok, kk_ps, kk_ok, rr_ps, rr_ok, ff_ps, ff_ok, out_ok = (sem(n) for n in ("o_ps", "res_ok", "ff_in_ok", "kk_ps", "kk_ok", "rr_ps", "rr_ok", "ff_ps", "ff_ok", "out_ok"))

        rows, out_rows = group_rows(x_mid), group_rows(io["out"])

        def weight(n, c, a=0, b=None):
            lo, hi = WC[n]
            return w["wc"][:, c, lo + a:hi if b is None else lo + b]

        def vec(n, c):
            return w["vc"][:, VC[n] + c:VC[n] + c + 1]

        def seqs(ap):
            return ap.rearrange("f (b t) -> f b t", b=GB)

        def after(engine, semaphore, count):
            if not (isinstance(count, int) and count == 0):
                engine.wait_ge(semaphore, count)

        MEAN, VAR, OUT, LN2, KK, RR, FF = 0, 2, 0, 2, 0, 2, 0
        LN1, MAA, MIX, PROJ = 0, 4, 4, 6
        RUK, RED, VB = 0, 6, (4, 5, 2, 3)
        LN = (LN1, LN2)
        block = ctx.enter_context(nc.Block())

        @block.sync
        def _(sp):
            def store(n):
                sp.wait_ge(out_ok, NP * n + NP)
                sp.dma_start(out_rows[bass.ds(n, 1)].rearrange("g q p d -> (g q) p d"), x_out[:, :, :]).then_inc(stored, 16)
                sp.wait_ge(stored, 16 * n + 16)
                sp.sem_inc(out_free, 1)

            def group(rows_, n):
                return rows_[n] if isinstance(n, int) else rows_[bass.ds(n, 1)].rearrange("g q p d -> (g q) p d")

            def load_entry(n):
                sp.wait_ge(xc_ok[0], NP * n)
                sp.dma_start(x_in[:, :, :], group(rows, n)).then_inc(ld_x, 16)

            def load_states(n):
                sp.wait_ge(keep_ok, n)
                sp.dma_start(flat(s0[:, :, :]), io["s0"][bass.ds(n, 1)].rearrange("g q n -> (g q) n")).then_inc(ld_s, 16)
                sp.dma_start(flat(prev[:, :, :, :]), io["prev"][bass.ds(n, 1)].rearrange("g q n -> (g q) n")).then_inc(ld_s, 16)

            sp.dma_start(x_cur[:, :, :], rows[0]).then_inc(ld_cur, 16)
            sp.wait_ge(b_stored, 16 * TURNS)
            sp.sem_inc(out_free, 1)
            load_entry(1)
            load_states(1)
            with sp.Fori(0, NG - 2) as it:
                load_entry(it + 2)
                store(it)
                sp.dma_start(x_cur[:, :, :], group(rows, it + 1)).then_inc(ld_cur, 16)
                load_states(it + 2)
            store(NG - 2)
            sp.dma_start(x_cur[:, :, :], rows[NG - 1]).then_inc(ld_cur, 16)
            for p in range(NP):
                sp.wait_ge(out_ok, NP * (NG - 1) + p + 1)
                sp.dma_start(out_rows[NG - 1][:, p, :], x_out[:, p, :]).then_inc(stored, 16)
            sp.wait_ge(stored, 16 * (NG - 1 + NP))

        @block.gpsimd
        def _(pool):
            pool.wait_ge(const_ok, 3)

            def inv_std(ln, n, tiles):
                pool.wait_ge(var_ok[ln], NP * n + tiles.stop)
                pool.tensor_tensor(rstd[ln][:, tiles], var[ln][:, tiles], minus_half[:, tiles], ALU.pow).then_inc(rstd_ok[ln], tiles.stop - tiles.start)

            def add_x(n, i):
                for c in range(NC):
                    pool.wait_ge(mix_ok, NMAA * NC * n + i * NC + c + 1)
                    t = seqs(x5[:, i % 2, c, :])
                    pool.tensor_tensor(t, t, xn[0][:, c, :, 1:S + 1], ALU.add).then_inc(x5_ok, 1)

            def turn(last, n, nxt):
                if n is not None:
                    for i in range(3):
                        add_x(n, i)
                if nxt is not None:
                    inv_std(0, nxt, slice(0, NP))
                if last is not None:
                    for p in range(NP):
                        inv_std(1, last, slice(p, p + 1))
                if n is not None:
                    for i in range(3, NMAA):
                        add_x(n, i)

            def recurrence(n):
                for i in range(NS):
                    pool.wait_ge(st_ok, NS * n + i + 1)
                    if i >= 4:
                        pool.wait_ge(red_ps, NS * n + i - 3)
                    pool.tensor_tensor(rs[:, i % 4, :], st[:, i % 3, :], rF[:, i // RS, :], ALU.mult).then_inc(rs_ok, 1)

            inv_std(0, 0, slice(0, NP))
            turn(None, 0, 1)
            recurrence(0)
            with pool.Fori(0, NG - 2) as it:
                turn(it, it + 1, it + 2)
                recurrence(it + 1)
            turn(NG - 2, NG - 1, None)
            recurrence(NG - 1)
            turn(NG - 1, None, None)

        @block.tensor
        def _(pe):
            pe.wait_ge(ld_c, 16 * N_C_CONST)

            def norm_T(ln, n):
                for p in range(NP):
                    pe.wait_ge(xc_ok[ln], NP * n + p + 1)
                    for c in range(NC):
                        mm = pe.transpose(ps[:, LN[ln] + c, p * P:(p + 1) * P], xc[ln][:, p, c * P:(c + 1) * P], w["ident"][:, :])
                mm.then_inc(ln_ps[ln], 1)

            def low_rank(n):
                pe.wait_ge(xx_ok, NC * n + NC)
                for i, rows_ in enumerate((P, RMAA)):
                    for k in range(NC):
                        mm = pe.matmul(ps[0:rows_, MAA + i, :], weight("maa1", k, i * P, i * P + rows_), xx[:, k, :],
                                       start=(k == 0), stop=(k == NC - 1))
                    mm.then_inc(maa_ps, 1)

            def mix(n, j):
                i = ORDER[j]
                src, first = (w["maa2a"], RMAA * i) if i < 4 else (w["maa2b"], 0)
                f = slice(first, first + RMAA)
                if j == 0:
                    pe.wait_ge(maa_ok, 2 * n + 2)
                for c in range(NC):
                    m = j * NC + c
                    if m >= 2:
                        pe.wait_ge(mix_ok, NMAA * NC * n + m - 1)
                    pe.matmul(ps[:, MIX + c, :], src[f, c * P:(c + 1) * P], maa[f, i // 4, :], start=True, stop=True).then_inc(mix_ps, 1)

            def bank_free(n, m):
                old = m - 2
                if old == 0:
                    pe.wait_ge(dec_ok, n + 1)
                elif 1 <= old <= 2:
                    pe.wait_ge(decay_ok, 2 * NC * n + old)
                elif old >= 3:
                    pe.wait_ge((k_ok, v_ok, r_ok)[(old - 3) // 2], NC * n + (old - 3) % 2 + 1)

            def decay_rank(n):
                pe.wait_ge(x5_ok, NMAA * NC * n + NC)
                after(pe, att_ok, NC * n)
                for k in range(NC):
                    mm = pe.matmul(ps[0:RDEC, PROJ, :], weight("dec1", k), x5[:, 0, k, :], start=(k == 0), stop=(k == NC - 1))
                mm.then_inc(proj_ps, 1)

            def decay_out(n):
                pe.wait_ge(dec_ok, n + 1)
                for c in range(NC):
                    m = 1 + c
                    bank_free(n, m)
                    pe.matmul(ps[:, PROJ + m % 2, :], w["dec2"][0:RDEC, c * P:(c + 1) * P], dec[0:RDEC, :], start=True, stop=True).then_inc(proj_ps, 1)

            def project(n, j, name):
                pe.wait_ge(x5_ok, NMAA * NC * n + j * NC + NC)
                for c in range(NC):
                    m = 1 + 2 * j + c
                    bank_free(n, m)
                    for k in range(NC):
                        mm = pe.matmul(ps[:, PROJ + m % 2, :], weight(name, k, c * P, (c + 1) * P), x5[:, j % 2, k, :],
                                       start=(k == 0), stop=(k == NC - 1))
                    mm.then_inc(proj_ps, 1)

            def place(i):
                return i // RS, slice(i % 4 * Q, (i % 4 + 1) * Q), i % RS // 4

            def spread_v(n, i):
                c = place(i)[0]
                if i >= 4:
                    pe.wait_ge(kv_ok, NS * n + i - 3)
                pe.matmul(ps[:, VB[i % 4], :], w["sel"][:, i % RS, :], vF[:, c, :], start=True, stop=True).then_inc(vb_ps, 1)

            def sum_k(n, i):
                c, q, odd = place(i)
                pe.matmul(ps[q, RED + c, :], w["red"][:, odd, :], rs[:, i % 4, :], start=(odd == 0), stop=(odd == 1)).then_inc(red_ps, 1)

            def recurrence(n, nxt):
                pe.wait_ge(v_ok, NC * n + NC)
                pe.wait_ge(mix_ok, NMAA * NC * (n + 1))
                spread_v(n, 0)
                spread_v(n, 1)
                after(pe, rr_ok, NP * n)
                spread_v(n, 2)
                spread_v(n, 3)
                pe.wait_ge(gg_ok, NC * n + NC)
                for i in range(0, NS, 2):
                    if i + LEAD < NS:
                        spread_v(n, i + LEAD)
                        spread_v(n, i + LEAD + 1)
                    pe.wait_ge(rs_ok, NS * n + i + 2)
                    sum_k(n, i)
                    sum_k(n, i + 1)
                    if i == 0:
                        after(pe, ff_ok, NP * n)
                        for c in range(NC):
                            pe.wait_ge(ruk_ok, NC * n + c + 1)
                            pe.matmul(ps[:, RUK + c, :], w["head_ones"][:, :], ruk[:, c, :], start=True, stop=True).then_inc(ruk_ps, 1)
                    if i == ENTRY and nxt is not None:
                        pe.wait_ge(bonus_ok, NC * n + NC)
                        norm_T(0, nxt)
                    if i == LOW_RANK and nxt is not None:
                        low_rank(nxt)

            def mean(n, nxt):
                if nxt is not None:
                    pe.wait_ge(xn_ok[0], NC * nxt + NC)
                for c in range(NC):
                    pe.wait_ge(att_ok, NC * n + c + 1)
                    pe.wait_ge(bonus_ok, NC * n + NC)
                    pe.matmul(ps[:, MEAN + c, :], w["head_mean"][:, :], att[:, c, :], start=True, stop=True).then_inc(mean_ps, 1)

            def variance(n):
                for c in range(NC):
                    pe.wait_ge(sqr_ok, NC * n + c + 1)
                    pe.matmul(ps[:, VAR + c, :], w["head_mean"][:, :], sqr[:, c, :], start=True, stop=True).then_inc(var_ps, 1)

            def out_project(n):
                pe.wait_ge(o_ok, NC * n + NC)
                for p in range(NP):
                    if p >= 2:
                        pe.wait_ge(res_ok, NP * n + p - 1)
                    for k in range(NC):
                        mm = pe.matmul(ps[:, OUT + p % 2, 0:D], att[:, k, p * P:(p + 1) * P], weight("o", k), start=(k == 0), stop=(k == NC - 1))
                    mm.then_inc(o_ps, 1)

            def ffn_keys(n):
                pe.wait_ge(ff_in_ok, 2 * NC * n + NC)
                for c in range(NC):
                    for k in range(NC):
                        mm = pe.matmul(ps[:, KK + c, :], weight("fk", k, c * P, (c + 1) * P), ff_in[:, 0, k, :], start=(k == 0), stop=(k == NC - 1))
                    mm.then_inc(kk_ps, 1)

            def ffn_gate(n):
                pe.wait_ge(ff_in_ok, 2 * NC * n + 2 * NC)
                for p in range(NP):
                    if p >= 2:
                        pe.wait_ge(rr_ok, NP * n + p - 1)
                    for k in range(NC):
                        mm = pe.matmul(ps[:, RR + p % 2, 0:D], ff_in[:, 1, k, p * P:(p + 1) * P], weight("fr", k), start=(k == 0), stop=(k == NC - 1))
                    mm.then_inc(rr_ps, 1)

            def ffn_values(n):
                pe.wait_ge(kk_ok, 2 * NC * n + 2 * NC)
                for p in range(NP):
                    if p >= 2:
                        pe.wait_ge(ff_ok, NP * n + p - 1)
                    for k in range(NC):
                        mm = pe.matmul(ps[:, FF + p % 2, 0:D], kk[:, k, p * P:(p + 1) * P], weight("fv", k), start=(k == 0), stop=(k == NC - 1))
                    mm.then_inc(ff_ps, 1)

            def turn(last, n):
                tail, head = last is not None, n is not None
                if tail:
                    mean(last, n)
                if head:
                    mix(n, 0)
                if tail:
                    variance(last)
                if head:
                    mix(n, 1)
                    decay_rank(n)
                    mix(n, 2)
                    decay_out(n)
                    project(n, 1, "k")
                if tail:
                    out_project(last)
                if head:
                    mix(n, 3)
                    project(n, 2, "v")
                if tail:
                    norm_T(1, last)
                if head:
                    mix(n, 4)
                    project(n, 3, "r")
                if tail:
                    ffn_keys(last)
                if head:
                    project(n, 4, "g")
                if tail:
                    ffn_gate(last)
                    ffn_values(last)

            norm_T(0, 0)
            low_rank(0)
            turn(None, 0)
            recurrence(0, 1)
            with pe.Fori(0, NG - 2) as it:
                turn(it, it + 1)
                recurrence(it + 1, it + 2)
            turn(NG - 2, NG - 1)
            recurrence(NG - 1, None)
            turn(NG - 1, None)

        @block.scalar
        def _(act):
            act.wait_ge(ld_c, 16 * N_C_CONST)
            act.wait_ge(const_ok, 3)

            def norm_out(ln, n, scale, bias):
                act.wait_ge(ln_ps[ln], n + 1)
                for c in range(NC):
                    act.activation(xn[ln][:, c, :, 1:S + 1], seqs(ps[:, LN[ln] + c, :]), ACT.Identity, bias=vec(bias, c), scale=vec(scale, c)).then_inc(xn_ok[ln], 1)

            def entry(n):
                norm_out(0, n, "ln1_w", "ln1_b")
                act.wait_ge(ld_s, 32 * n + 32)
                act.activation(xn[0][:, :, :, 0], prev[:, 1, :, :], ACT.Copy).then_inc(state_ok, 1)
                low_rank_tanh(n)

            def start_states(n):
                after(act, att_ok, NC * n)
                act.activation(kv[:, :, :, 0], s0[:, :, :], ACT.Copy).then_inc(state_ok, 1)

            def low_rank_tanh(n):
                for i, rows_ in enumerate((P, RMAA)):
                    act.wait_ge(maa_ps, 2 * n + i + 1)
                    act.activation(maa[0:rows_, i, :], ps[0:rows_, MAA + i, :], ACT.Tanh).then_inc(maa_ok, 1)

            def decays(n):
                act.wait_ge(proj_ps, OUTS * n + 1)
                act.activation(dec[0:RDEC, :], ps[0:RDEC, PROJ, :], ACT.Tanh).then_inc(dec_ok, 1)
                after(act, gg_ok, NC * n)
                for c in range(NC):
                    act.wait_ge(proj_ps, OUTS * n + 2 + c)
                    act.activation(dexp[:, c, :], ps[:, PROJ + (1 + c) % 2, :], ACT.Exp, bias=vec("decay", c)).then_inc(decay_ok, 1)
                for c in range(NC):
                    act.wait_ge(decay_ok, 2 * NC * n + c + 1)
                    act.activation(decay[:, c, :, 1:S], seqs(dexp[:, c, :])[:, :, 0:S - 1], ACT.Exp, scale=-1.0).then_inc(decay_ok, 1)

            def copy_projection(n, dst, ok, j):
                for c in range(NC):
                    m = 1 + 2 * j + c
                    act.wait_ge(proj_ps, OUTS * n + m + 1)
                    act.activation(dst[:, c, :], ps[:, PROJ + m % 2, :], ACT.Copy).then_inc(ok, 1)

            def gate_tanh(n):
                act.wait_ge(decay_ok, 2 * NC * (n + 1))
                for c in range(NC):
                    m = 9 + c
                    act.wait_ge(proj_ps, OUTS * n + m + 1)
                    act.activation(th[:, c, :], ps[:, PROJ + m % 2, :], ACT.Tanh, scale=0.5).then_inc(th_ok, 1)

            def squares(n):
                for c in range(NC):
                    act.wait_ge(dm_ok, NC * n + c + 1)
                    act.activation(sqr[:, c, :], att[:, c, :], ACT.Square).then_inc(sqr_ok, 1)

            def group_rstd(n):
                for c in range(NC):
                    act.wait_ge(var_ps, NC * n + c + 1)
                    act.activation(gn_rstd[:, c, :], ps[:, VAR + c, :], ACT.Ln, bias=eps[:, 0:1]).then_inc(grstd_ok, 1)
                for c in range(NC):
                    act.wait_ge(grstd_ok, 2 * NC * n + c + 1)
                    act.activation(gn_rstd[:, c, :], gn_rstd[:, c, :], ACT.Exp, scale=-0.5).then_inc(grstd_ok, 1)

            def group_affine(n):
                for c in range(NC):
                    act.wait_ge(nrm_ok, NC * n + c + 1)
                    act.activation(att[:, c, :], att[:, c, :], ACT.Identity, bias=vec("gn_b", c), scale=vec("gn_w", c)).then_inc(gn_ok, 1)

            def ffn_squares(n):
                for c in range(NC):
                    act.wait_ge(kk_ps, NC * n + c + 1)
                    act.activation(kk[:, c, :], ps[:, KK + c, :], ACT.Relu).then_inc(kk_ok, 1)
                for c in range(NC):
                    act.wait_ge(kk_ok, 2 * NC * n + c + 1)
                    act.activation(kk[:, c, :], kk[:, c, :], ACT.Square).then_inc(kk_ok, 1)

            def ffn_tanh(n):
                for p in range(NP):
                    act.wait_ge(rr_ps, NP * n + p + 1)
                    act.activation(rr[:, p, :], ps[:, RR + p % 2, 0:D], ACT.Tanh, scale=0.5).then_inc(rr_ok, 1)

            def turn(last, n):
                tail, head = last is not None, n is not None
                if tail:
                    squares(last)
                if head:
                    start_states(n)
                if tail:
                    group_rstd(last)
                    group_affine(last)
                if head:
                    decays(n)
                    copy_projection(n, kF, k_ok, 1)
                    copy_projection(n, vF, v_ok, 2)
                if tail:
                    norm_out(1, last, "ln2_w", "ln2_b")
                if head:
                    copy_projection(n, rF, r_ok, 3)
                if tail:
                    ffn_squares(last)
                if head:
                    gate_tanh(n)
                if tail:
                    ffn_tanh(last)

            def keep(n):
                after(act, out_ok, NP * n)
                act.wait_ge(ld_s, 32 * n + 32)
                act.activation(xn[1][:, :, :, 0], prev[:, 0, :, :], ACT.Copy).then_inc(keep_ok, 1)

            entry(0)
            turn(None, 0)
            keep(0)
            entry(1)
            with act.Fori(0, NG - 2) as it:
                turn(it, it + 1)
                keep(it + 1)
                entry(it + 2)
            turn(NG - 2, NG - 1)
            keep(NG - 1)
            turn(NG - 1, None)

        @block.vector
        def _(dve):
            dve.memset(minus_half[:, :], -0.5).then_inc(const_ok, 1)
            dve.memset(eps[:, :], EPS).then_inc(const_ok, 1)
            dve.memset(decay[:, :, :, 0], 0.0).then_inc(const_ok, 1)
            dve.wait_ge(const_ok, 3)
            dve.wait_ge(ld_c, 16 * N_C_CONST)

            def stats(ln, n, src, tiles):
                before = 2 * (NP * n + tiles[0])
                for p in tiles:
                    dve.bn_stats(bn[ln][:, p, :], src[:, p, :]).then_inc(stat_ok[ln], 1)
                dve.wait_ge(stat_ok[ln], before + len(tiles))
                dve.memset(gate_mark[:, :], 0.0)
                for p in tiles:
                    dve.bn_aggr(mv[ln][:, p, :], bn[ln][:, p, :]).then_inc(stat_ok[ln], 1)
                for i, p in enumerate(tiles):
                    dve.wait_ge(stat_ok[ln], before + len(tiles) + i + 1)
                    dve.tensor_scalar(var[ln][:, p:p + 1], mv[ln][:, p, 1:2], EPS, None, ALU.add).then_inc(var_ok[ln], 1)

            def norm(ln, n, src, tiles):
                for p in tiles:
                    dve.wait_ge(rstd_ok[ln], NP * n + p + 1)
                    dve.tensor_scalar(xc[ln][:, p, :], src[:, p, :], mv[ln][:, p, 0:1], rstd[ln][:, p:p + 1], ALU.subtract, ALU.mult).then_inc(xc_ok[ln], 1)

            def shift(ln, n):
                dve.wait_ge(xn_ok[ln], NC * n + NC)
                if ln == 0:
                    dve.wait_ge(state_ok, 2 * n + 1)
                else:
                    dve.wait_ge(keep_ok, n + 1)
                for c in range(NC):
                    dve.tensor_tensor(seqs(sx[ln][:, c, :]), xn[ln][:, c, :, 0:S], xn[ln][:, c, :, 1:S + 1], ALU.subtract).then_inc(sx_ok[ln], 1)

            def low_rank_in(n):
                for c in range(NC):
                    dve.wait_ge(sx_ok[0], NC * n + c + 1)
                    dve.scalar_tensor_tensor(seqs(xx[:, c, :]), seqs(sx[0][:, c, :]), vec("maa_x", c), xn[0][:, c, :, 1:S + 1], ALU.mult, ALU.add).then_inc(xx_ok, 1)

            def mixed(n, j):
                if j >= 2:
                    dve.wait_ge(proj_ps, OUTS * n + PROJ_DONE[j - 2])
                for c in range(NC):
                    dve.wait_ge(mix_ps, NMAA * NC * n + j * NC + c + 1)
                    dve.scalar_tensor_tensor(x5[:, j % 2, c, :], ps[:, MIX + c, :], vec(f"st{ORDER[j]}", c), sx[0][:, c, :], ALU.add, ALU.mult).then_inc(mix_ok, 1)

            def own_weight(n):
                for c in range(NC):
                    dve.wait_ge(r_ok, NC * n + c + 1)
                    dve.wait_ge(k_ok, NC * n + c + 1)
                    dve.scalar_tensor_tensor(ruk[:, c, :], rF[:, c, :], vec("u", c), kF[:, c, :], ALU.mult, ALU.mult).then_inc(ruk_ok, 1)

            def gate(n):
                for c in range(NC):
                    dve.wait_ge(th_ok, NC * n + c + 1)
                    dve.scalar_tensor_tensor(gg[:, c, :], th[:, c, :], 1.0, ps[:, PROJ + (9 + c) % 2, :], ALU.add, ALU.mult).then_inc(gg_ok, 1)

            def key_value(n, i):
                dve.wait_ge(vb_ps, NS * n + i + 1)
                dve.tensor_tensor(kv[:, i, :, 1:S], seqs(ps[:, VB[i % 4], :])[:, :, 0:S - 1], seqs(kF[:, i // RS, :])[:, :, 0:S - 1], ALU.mult).then_inc(kv_ok, 1)

            def scan(n, i):
                dve.wait_ge(kv_ok, NS * n + i + 1)
                if i >= 3:
                    dve.wait_ge(rs_ok, NS * n + i - 2)
                dve.tensor_tensor_scan(st[:, i % 3, :], decay[:, i // RS, :, :].rearrange("f b t -> f (b t)"),
                                       kv[:, i, :, :].rearrange("f b t -> f (b t)"), 0.0, ALU.mult, ALU.add).then_inc(st_ok, 1)

            def recurrence(n, nxt):
                dve.wait_ge(state_ok, 2 * n + 2)
                dve.wait_ge(decay_ok, 2 * NC * (n + 1))
                key_value(n, 0)
                for i in range(NS):
                    if i + 1 < NS:
                        key_value(n, i + 1)
                    scan(n, i)
                    if i == BONUS:
                        for c in range(NC):
                            dve.wait_ge(ruk_ps, NC * n + c + 1)
                            dve.tensor_tensor(ruk[:, c, :], ps[:, RUK + c, :], vF[:, c, :], ALU.mult).then_inc(bonus_ok, 1)
                    if i == SHIFT and nxt is not None:
                        shift(0, nxt)
                        low_rank_in(nxt)

            def attention(n):
                for c in range(NC):
                    dve.wait_ge(bonus_ok, NC * n + c + 1)
                    dve.wait_ge(red_ps, NS * n + (c + 1) * RS)
                    dve.tensor_tensor(att[:, c, :], ps[:, RED + c, :], ruk[:, c, :], ALU.add).then_inc(att_ok, 1)

            def centre(n):
                for c in range(NC):
                    dve.wait_ge(mean_ps, NC * n + c + 1)
                    dve.tensor_tensor(att[:, c, :], att[:, c, :], ps[:, MEAN + c, :], ALU.subtract).then_inc(dm_ok, 1)

            def group_norm(n):
                for c in range(NC):
                    dve.wait_ge(grstd_ok, 2 * NC * n + NC + c + 1)
                    dve.wait_ge(sqr_ok, NC * n + c + 1)
                    dve.tensor_tensor(att[:, c, :], att[:, c, :], gn_rstd[:, c, :], ALU.mult).then_inc(nrm_ok, 1)

            def gated(n):
                for c in range(NC):
                    dve.wait_ge(gn_ok, NC * n + c + 1)
                    dve.scalar_tensor_tensor(att[:, c, :], gg[:, c, :], 0.5, att[:, c, :], ALU.mult, ALU.mult).then_inc(o_ok, 1)

            def residual(n):
                for p in range(NP):
                    dve.wait_ge(o_ps, NP * n + p + 1)
                    dve.wait_ge(ld_cur, 16 * n + 16)
                    dve.tensor_tensor(x_cur[:, p, :], ps[:, OUT + p % 2, 0:D], x_cur[:, p, :], ALU.add).then_inc(res_ok, 1)
                    dve.wait_ge(res_ok, NP * n + p + 1)
                    stats(1, n, x_cur, [p])
                    if p >= 1:
                        norm(1, n, x_cur, [p - 1])
                norm(1, n, x_cur, [NP - 1])

            def ffn_mix(n):
                for i, mixer in enumerate(("fmk", "fmr")):
                    for c in range(NC):
                        dve.wait_ge(sx_ok[1], NC * n + c + 1)
                        dve.scalar_tensor_tensor(seqs(ff_in[:, i, c, :]), seqs(sx[1][:, c, :]), vec(mixer, c), xn[1][:, c, :, 1:S + 1], ALU.mult, ALU.add).then_inc(ff_in_ok, 1)

            def result(n):
                dve.wait_ge(out_free, n + 1)
                for p in range(NP):
                    dve.wait_ge(ff_ps, NP * n + p + 1)
                    dve.wait_ge(rr_ok, NP * n + p + 1)
                    dve.scalar_tensor_tensor(ff[:, p % 2, :], rr[:, p, :], 1.0, ps[:, FF + p % 2, 0:D], ALU.add, ALU.mult).then_inc(ff_ok, 1)
                    dve.wait_ge(ff_ok, NP * n + p + 1)
                    dve.scalar_tensor_tensor(x_out[:, p, :], ff[:, p % 2, :], 0.5, x_cur[:, p, :], ALU.mult, ALU.add).then_inc(out_ok, 1)

            def entry_stats(n):
                dve.wait_ge(ld_x, 16 * n + 16)
                stats(0, n, x_in, range(NP))

            def turn(last, n, nxt):
                tail, head = last is not None, n is not None
                if tail:
                    attention(last)
                    centre(last)
                if head:
                    mixed(n, 0)
                    mixed(n, 1)
                if tail:
                    group_norm(last)
                    gated(last)
                if head:
                    mixed(n, 2)
                if nxt is not None:
                    entry_stats(nxt)
                    norm(0, nxt, x_in, range(NP))
                if tail:
                    residual(last)
                if head:
                    mixed(n, 3)
                    mixed(n, 4)
                if tail:
                    shift(1, last)
                    ffn_mix(last)
                if head:
                    own_weight(n)
                    gate(n)
                if tail:
                    result(last)

            entry_stats(0)
            norm(0, 0, x_in, range(NP))
            shift(0, 0)
            low_rank_in(0)
            turn(None, 0, 1)
            recurrence(0, 1)
            with dve.Fori(0, NG - 2) as it:
                turn(it, it + 1, it + 2)
                recurrence(it + 1, it + 2)
            turn(NG - 2, NG - 1, None)
            recurrence(NG - 1, None)
            turn(NG - 1, None, None)


def kernel(**inputs):
    import numpy as np
    import concourse.bacc as bacc
    from concourse import mybir as mb
    from concourse.bass_utils import run_bass_kernel_spmd

    a = {k: np.asarray(v) for k, v in inputs.items()}
    f4 = np.float32
    eye2 = [(0, S), (S, P)]

    def block_diag(m):
        out = np.zeros((P, P), f4)
        for lo, hi in eye2:
            out[lo:hi, lo:hi] = m
        return out

    def chunks(v):
        return v.reshape(-1, P).T

    lay = {}
    lay["x"] = a["x"].reshape(T, D)
    lay["ctx"] = a["ctx_2048"].reshape(T, D)
    lay["ctxT"] = lay["ctx"].T
    lay["w0"] = np.stack([block_diag(a["L0_xattn_" + n].T) for n in ("w_qk", "w_v", "w_t")], 1)
    lay["bv0"] = np.concatenate([a["L0_xattn_b_v"]] * 2)[None, :]
    lay["bt0"] = np.concatenate([a["L0_xattn_b_t"]] * 2)[:, None]
    lay["self_mask"] = a["mask_1x1xSxS2_fc1"].reshape(S, S)
    lay["cross_mask"] = a["mask_Bx1xSxS2_ff1"].reshape(T, S)
    even_head = (np.arange(P) // HD) % 2 == 0

    def by(width, m):
        v = m.reshape(m.shape[:-1] + (-1, 2, width))
        return np.moveaxis(v, -2, -3).reshape(m.shape)

    def by_d(m):
        return np.swapaxes(m.reshape(m.shape[:-1] + (NC, HC, RS)), -1, -2).reshape(m.shape)

    def head_chunks(v):
        out = np.zeros((P, 2 * NC), f4)
        for c in range(NC):
            for par, rows in enumerate((even_head, ~even_head)):
                out[rows, 2 * c + par] = chunks(v)[rows, c]
        return out

    wl, w2, vl, rl = [], [], [], []
    for n in ("L1_xattn_", "L2_xattn_"):
        g = lambda k: a[n + k]
        wl.append(np.concatenate([g("w_qkv")[:, 0:2 * D], by(PF, g("w_qkv")[:, 2 * D:]), by(HD, g("w_ao").T).T, g("w_kv")[:, 0:D],
                                  by(PF, g("w_kv")[:, D:]), g("w_q"), by(HD, g("w_co").T).T, g("w1")], 1))
        w2.append(g("w2"))
        vl.append(np.concatenate([chunks(g("ln1_s")), chunks(g("ln1_b")), head_chunks(g("b_qkv")[0:D]), chunks(g("b_qkv")[D:2 * D]),
                                  chunks(g("ln2_s")), chunks(g("ln2_b")), head_chunks(g("b_q")), chunks(g("b_kv")[0:D]),
                                  chunks(g("ln3_s")), chunks(g("ln3_b")), chunks(g("b1"))], 1))
        rl.append(np.concatenate([by(PF, g("b_qkv")[2 * D:]), g("b_ao"), by(PF, g("b_kv")[D:]), g("b_co"), g("b2")]))
    lay["wl"], lay["w2"], lay["vl"], lay["rl"] = np.stack(wl), np.stack(w2), np.stack(vl), np.stack(rl)
    c = lambda k: a["L3_xattn_" + k]
    lay["wc"] = np.concatenate([c("maa_w1"), c("decay_w1"), c("Wr").T, c("Wk").T, by_d(c("Wv").T), by_d(c("Wg").T), by_d(c("Wo")).T]
                               + [c(k).T for k in ("ffn_Wk", "ffn_Wr", "ffn_Wv")], 1)
    lay["maa2"] = c("maa_w2").reshape(NMAA * RMAA, D)
    lay["dec2"] = c("decay_w2")
    lay["vc"] = np.concatenate([chunks(v) for v in [c("ln1_w"), c("ln1_b"), c("ln2_w"), c("ln2_b"), c("maa_x")]
                                + [c("maa_stack")[i] for i in range(NMAA)]
                                + [c("time_decay"), c("faaaa").reshape(D), by_d(c("gn_w")), by_d(c("gn_b")), c("ffn_maa_k"), c("ffn_maa_r")]], 1)
    ctx3 = a["ctx_2048"]
    s0 = ctx3[:, 2:2 + RS, :].reshape(NG, GB, NC, P, RS)
    lay["s0"] = by(1, s0).transpose(0, 3, 2, 4, 1).reshape(NG, P, NC * RS * GB)
    lay["prev"] = ctx3[:, 0:2, :].reshape(NG, GB, 2, NC, P).transpose(0, 4, 2, 3, 1).reshape(NG, P, 2 * NC * GB)
    i, j = np.arange(P)[:, None], np.arange(P)[None, :]
    lay["ident"] = (i == j)
    lay["parity"] = np.stack([even_head, ~even_head], 1)
    lay["sel"] = np.stack([(i % HC == j // RS) & (i // HC == d) for d in [*range(0, RS, 2), *range(1, RS, 2)]], 1)
    lay["red"] = np.stack([(i // RS == j % HC) & (j // HC == d) for d in range(2)], 1)[:, :, 0:Q]
    lay["head_ones"] = i // RS == j % HC
    lay["head_mean"] = (i % HC == j % HC) * f4(1 / RS)

    nc = bacc.Bacc("TRN2", target_bir_lowering=False, num_devices=1)
    arrays, io = {}, {}
    for name, v in lay.items():
        arrays["in_" + name] = np.ascontiguousarray(v, dtype=f4)
        io[name] = nc.dram_tensor("in_" + name, v.shape, mb.dt.float32, kind="ExternalInput").ap()
    io["out"] = nc.dram_tensor("out_x", (T, D), mb.dt.float32, kind="ExternalOutput").ap()
    build(nc, io)
    r = run_bass_kernel_spmd(nc, [arrays], core_ids=[0])
    return np.asarray(r.results[0]["out_x"]).reshape(B, S, D)
```
